# Optimizing a Trainium2 kernel written in Bass

```python
import numpy as np
import jax
import jax.numpy as jnp

def _softmax(x, axis=-1):
    return jax.nn.softmax(x, axis=axis)

def _gelu(x):
    return jax.nn.gelu(x, approximate=True)

def _silu(x):
    return jax.nn.silu(x)

def _sigmoid(x):
    return jax.nn.sigmoid(x)

def _layernorm(x, axis=-1, eps=1e-05):
    m = jnp.mean(x, axis=axis, keepdims=True)
    v = jnp.var(x, axis=axis, keepdims=True)
    return (x - m) / jnp.sqrt(v + eps)

def _scatter_add(tgt, idx, src, axis=0):
    return tgt.at[idx].add(src)

def _segment_sum(src, seg, n):
    return jax.ops.segment_sum(src, seg, n)
kernel_name = 'mk_decoder_preln_d2_seqx_r8_34b4f3'

def setup_inputs(seed: int=0):
    np.random.seed(seed)
    _w = jnp.asarray

    def _rec_inputs():
        import jax
        import jax.numpy as jnp
        _rk = jax.random.key(seed)
        x = 6.313e-05 + 0.9998 * jax.random.normal(jax.random.fold_in(_rk, 1), (2, 512, 128), jnp.float32)
        _lenS = 512 - jax.random.randint(jax.random.fold_in(_rk, 7), (2,), 0, max(1, 512 // 4) + 1, jnp.int32)
        _lenS2 = 77 - jax.random.randint(jax.random.fold_in(_rk, 8), (2,), 0, max(1, 77 // 4) + 1, jnp.int32)
        _ctx_1024P = jax.random.normal(jax.random.fold_in(_rk, 11), (2, 16, 128), jnp.float32)
        _ctx_1024c = jax.random.dirichlet(jax.random.fold_in(_rk, 511), 0.3 * jnp.ones((16,), jnp.float32), (2, 77))
        _ctx_1024t = jnp.einsum('bsk,bkd->bsd', _ctx_1024c, _ctx_1024P)
        _ctx_1024t = _ctx_1024t * jax.lax.rsqrt(jnp.mean(jnp.square(_ctx_1024t)) + 1e-12) * 0.953939
        ctx_1024 = -0.000214406 + 1.00034 * (_ctx_1024t + 0.3 * jax.random.normal(jax.random.fold_in(_rk, 611), (2, 77, 128), jnp.float32))
        return (x, ctx_1024)
    x, ctx_1024 = _rec_inputs()

    def _L0_attn_setup():
        import jax, jax.numpy as jnp
        import numpy as np
        N, L, D, A, F, B = (4, 512, 128, 128, 512, 8)
        EPS_LN = 1e-06
        EPS_Z = 1e-06

        def _layernorm(x, scale, bias):
            m = jnp.mean(x, axis=-1, keepdims=True)
            v = jnp.mean(jnp.square(x - m), axis=-1, keepdims=True)
            return (x - m) * jax.lax.rsqrt(v + EPS_LN) * scale + bias

        def _block(x, p):
            Wq, bq, Wk, bk, Wv, bv, Wo, bo, ln1_s, ln1_b, Wf1, bf1, Wf2, bf2, ln2_s, ln2_b = p
            residual = x
            q = jnp.einsum('nld,da->nla', x, Wq) + bq
            k = jnp.einsum('nld,da->nla', x, Wk) + bk
            v = jnp.einsum('nld,da->nla', x, Wv) + bv
            Q = jax.nn.elu(q) + 1.0
            K = jax.nn.elu(k) + 1.0
            KV = jnp.einsum('nsh,nsh->nh', K, v)
            Ksum = jnp.sum(K, axis=1)
            Z = 1.0 / (Q * Ksum[:, None, :] + EPS_Z)
            V = Q * KV[:, None, :] * Z
            attn = jax.nn.gelu(jnp.einsum('nla,ad->nld', V, Wo) + bo)
            x = _layernorm(attn + residual, ln1_s, ln1_b)
            residual = x
            h = jax.nn.gelu(jnp.einsum('nld,df->nlf', x, Wf1) + bf1)
            ff = jax.nn.gelu(jnp.einsum('nlf,fd->nld', h, Wf2) + bf2)
            x = _layernorm(ff + residual, ln2_s, ln2_b)
            return (x, None)
        key = jax.random.key(seed)
        ks = jax.random.split(key, 10)
        s = 0.02
        x = jax.random.normal(ks[0], (N, L, D), dtype=jnp.float32)
        Wq = jax.random.normal(ks[1], (B, D, A), dtype=jnp.float32) * s
        Wk = jax.random.normal(ks[2], (B, D, A), dtype=jnp.float32) * s
        Wv = jax.random.normal(ks[3], (B, D, A), dtype=jnp.float32) * s
        Wo = jax.random.normal(ks[4], (B, A, D), dtype=jnp.float32) * s
        Wf1 = jax.random.normal(ks[5], (B, D, F), dtype=jnp.float32) * s
        Wf2 = jax.random.normal(ks[6], (B, F, D), dtype=jnp.float32) * s
        return {'x': x, 'Wq': Wq, 'bq': jnp.zeros((B, A), jnp.float32), 'Wk': Wk, 'bk': jnp.zeros((B, A), jnp.float32), 'Wv': Wv, 'bv': jnp.zeros((B, A), jnp.float32), 'Wo': Wo, 'bo': jnp.zeros((B, D), jnp.float32), 'ln1_s': jnp.ones((B, D), jnp.float32), 'ln1_b': jnp.zeros((B, D), jnp.float32), 'Wf1': Wf1, 'bf1': jnp.zeros((B, F), jnp.float32), 'Wf2': Wf2, 'bf2': jnp.zeros((B, D), jnp.float32), 'ln2_s': jnp.ones((B, D), jnp.float32), 'ln2_b': jnp.zeros((B, D), jnp.float32)}
    _L0_attn_all = _L0_attn_setup()
    _L0_attn_in = {k: v for k, v in _L0_attn_all.items() if k in ('Wq', 'bq', 'Wk', 'bk', 'Wv', 'bv', 'Wo', 'bo', 'ln1_s', 'ln1_b', 'Wf1', 'bf1', 'Wf2', 'bf2', 'ln2_s', 'ln2_b')}
    del _L0_attn_all

    def _L0_xattn_setup():
        import jax, jax.numpy as jnp
        import numpy as np
        from jax import lax
        BIG = jnp.float32(1e+30)

        def _pairwise_euclidean(a, b):
            aa = jnp.sum(a * a, axis=-1)[:, None]
            bb = jnp.sum(b * b, axis=-1)[None, :]
            ab = a @ b.T
            return jnp.sqrt(jnp.maximum(aa + bb - 2.0 * ab, 0.0))

        def _dtw_cost(D):
            row0 = jnp.cumsum(D[0])

            def row_step(prev_row, d_row):
                first = d_row[0] + prev_row[0]

                def col_step(left, inp):
                    d_ij, up, diag = inp
                    r = d_ij + jnp.minimum(jnp.minimum(up, left), diag)
                    return (r, r)
                _, rest = lax.scan(col_step, first, (d_row[1:], prev_row[1:], prev_row[:-1]))
                row = jnp.concatenate([first[None], rest])
                return (row, row)
            _, rows = lax.scan(row_step, row0, D[1:])
            return jnp.concatenate([row0[None], rows], axis=0)

        def _backtrack(R, T1, T2):
            L = T1 + T2 - 1

            def step(carry, _):
                i, j, done = carry
                valid = jnp.logical_not(done)
                cd = jnp.where((i > 0) & (j > 0), R[jnp.maximum(i - 1, 0), jnp.maximum(j - 1, 0)], BIG)
                cu = jnp.where(i > 0, R[jnp.maximum(i - 1, 0), j], BIG)
                cl = jnp.where(j > 0, R[i, jnp.maximum(j - 1, 0)], BIG)
                choice = jnp.argmin(jnp.stack([cd, cu, cl]))
                ni = jnp.where(choice <= 1, i - 1, i)
                nj = jnp.where((choice == 0) | (choice == 2), j - 1, j)
                at_origin = (i == 0) & (j == 0)
                ni = jnp.where(at_origin, 0, ni)
                nj = jnp.where(at_origin, 0, nj)
                return ((ni, nj, done | at_origin), (i, j, valid))
            init = (jnp.int32(T1 - 1), jnp.int32(T2 - 1), jnp.bool_(False))
            _, (i_idx, j_idx, valid) = lax.scan(step, init, None, length=L)
            return (i_idx, j_idx, valid)

        def _align_one(small, large):
            T_small, d = small.shape
            T_large = large.shape[0]
            D = _pairwise_euclidean(small, large)
            R = _dtw_cost(D)
            i_idx, j_idx, valid = _backtrack(R, T_small, T_large)
            contrib = small[i_idx] * valid[:, None].astype(small.dtype)
            expanded = jnp.zeros((T_large, d), dtype=small.dtype).at[j_idx].add(contrib)
            return expanded
        key = jax.random.key(seed)
        k1, k2 = jax.random.split(key)
        teacher = jax.random.normal(k1, (16, 50, 128), dtype=jnp.float32)
        student = jax.random.normal(k2, (16, 75, 128), dtype=jnp.float32)
        return {'teacher_features': teacher, 'student_features': student}
    _L0_xattn_all = _L0_xattn_setup()
    _L0_xattn_in = {k: v for k, v in _L0_xattn_all.items() if k in ()}
    del _L0_xattn_all

    def _L0_ffn_setup():
        import jax, jax.numpy as jnp
        import numpy as np
        TOPK = 2
        CAPACITY_FACTOR = 1.0
        EPS = 1e-06
        B, S, D = (4, 512, 128)
        E = 8
        SUB_H = 256 // E
        key = jax.random.key(seed)
        ks = jax.random.split(key, 7)
        x = jax.random.normal(ks[0], (B, S, D), dtype=jnp.float32)
        w_gate_w = jax.random.normal(ks[1], (D, E), dtype=jnp.float32) * 0.02
        w_gate_b = jnp.zeros((E,), jnp.float32)
        W1 = jax.random.normal(ks[2], (E, D, SUB_H), dtype=jnp.float32) * 0.02
        b1 = jnp.zeros((E, SUB_H), jnp.float32)
        W2 = jax.random.normal(ks[3], (E, SUB_H, D), dtype=jnp.float32) * 0.02
        b2 = jnp.zeros((E, D), jnp.float32)
        return {'x': x, 'w_gate_w': w_gate_w, 'w_gate_b': w_gate_b, 'W1': W1, 'b1': b1, 'W2': W2, 'b2': b2}
    _L0_ffn_all = _L0_ffn_setup()
    _L0_ffn_in = {k: v for k, v in _L0_ffn_all.items() if k in ('w_gate_w', 'w_gate_b', 'W1', 'b1', 'W2', 'b2')}
    del _L0_ffn_all

    def _L1_attn_setup():
        import jax, jax.numpy as jnp
        import numpy as np
        from jax import lax
        B, S, E, H, KS = (2, 256, 128, 16, 3)
        DH = E // H
        key = jax.random.key(seed)
        ks = jax.random.split(key, 11)
        s = 1.0 / np.sqrt(E)
        sc = 1.0 / np.sqrt(H * KS)
        return {'query': jax.random.normal(ks[0], (B, S, E), jnp.float32), 'Wq': jax.random.uniform(ks[1], (E, E), jnp.float32, -s, s), 'bq': jax.random.uniform(ks[2], (E,), jnp.float32, -s, s), 'Wk': jax.random.uniform(ks[3], (E, E), jnp.float32, -s, s), 'bk': jax.random.uniform(ks[4], (E,), jnp.float32, -s, s), 'Wv': jax.random.uniform(ks[5], (E, E), jnp.float32, -s, s), 'bv': jax.random.uniform(ks[6], (E,), jnp.float32, -s, s), 'Wo': jax.random.uniform(ks[7], (E, E), jnp.float32, -s, s), 'bo': jax.random.uniform(ks[8], (E,), jnp.float32, -s, s), 'conv_w': jax.random.uniform(ks[9], (H, H, KS), jnp.float32, -sc, sc), 'conv_b': jax.random.uniform(ks[10], (H,), jnp.float32, -sc, sc)}
    _L1_attn_all = _L1_attn_setup()
    _L1_attn_in = {k: v for k, v in _L1_attn_all.items() if k in ('Wq', 'bq', 'Wk', 'bk', 'Wv', 'bv', 'Wo', 'bo', 'conv_w', 'conv_b')}
    del _L1_attn_all

    def _L1_xattn_setup():
        import jax, jax.numpy as jnp
        import numpy as np
        B, S, E = (8, 256, 128)
        key = jax.random.key(seed)
        ks = jax.random.split(key, 9)

        def xavier(k, shape):
            fan_in, fan_out = (shape[1], shape[0])
            lim = (6.0 / (fan_in + fan_out)) ** 0.5
            return jax.random.uniform(k, shape, jnp.float32, -lim, lim)
        return {'queries': jax.random.normal(ks[0], (B, S, E), jnp.float32), 'keys': jax.random.normal(ks[1], (B, S, E), jnp.float32), 'values': jax.random.normal(ks[2], (B, S, E), jnp.float32), 'Wq': xavier(ks[3], (E, E)), 'bq': jnp.zeros((E,), jnp.float32), 'Wk': xavier(ks[4], (E, E)), 'bk': jnp.zeros((E,), jnp.float32), 'Wv': xavier(ks[5], (E, E)), 'bv': jnp.zeros((E,), jnp.float32)}
    _L1_xattn_all = _L1_xattn_setup()
    _L1_xattn_in = {k: v for k, v in _L1_xattn_all.items() if k in ('Wq', 'bq', 'Wk', 'bk', 'Wv', 'bv')}
    del _L1_xattn_all

    def _L1_ffn_setup():
        import jax, jax.numpy as jnp
        import numpy as np
        B, S, D_MODEL, D_FF = (4, 256, 128, 512)

        def _quantum_transform(hidden, theta, w_real, w_imag):
            imag = w_imag * jnp.sin(theta + hidden * 0.1)
            quantum_phase = jnp.cos(theta) * w_real + jnp.sin(theta) * w_imag
            return hidden + quantum_phase * imag * 0.1
        key = jax.random.key(seed)
        ks = jax.random.split(key, 8)
        return {'x': jax.random.normal(ks[0], (B, S, D_MODEL), dtype=jnp.float32), 'W1': jax.random.normal(ks[1], (D_MODEL, D_FF), dtype=jnp.float32) * (1.0 / np.sqrt(D_MODEL)), 'b1': jnp.zeros((D_FF,), dtype=jnp.float32), 'quantum_phases': jax.random.normal(ks[2], (D_FF,), dtype=jnp.float32) * (2.0 * np.pi), 'quantum_weights_real': jax.random.normal(ks[3], (D_FF,), dtype=jnp.float32) * 0.1, 'quantum_weights_imag': jax.random.normal(ks[4], (D_FF,), dtype=jnp.float32) * 0.1, 'W2': jax.random.normal(ks[5], (D_FF, D_MODEL), dtype=jnp.float32) * (1.0 / np.sqrt(D_FF)), 'b2': jnp.zeros((D_MODEL,), dtype=jnp.float32)}
    _L1_ffn_all = _L1_ffn_setup()
    _L1_ffn_in = {k: v for k, v in _L1_ffn_all.items() if k in ('W1', 'b1', 'quantum_phases', 'quantum_weights_real', 'quantum_weights_imag', 'W2', 'b2')}
    del _L1_ffn_all
    return {'x': x, 'ctx_1024': ctx_1024, 'L0_attn_Wq': _L0_attn_in['Wq'], 'L0_attn_bq': _L0_attn_in['bq'], 'L0_attn_Wk': _L0_attn_in['Wk'], 'L0_attn_bk': _L0_attn_in['bk'], 'L0_attn_Wv': _L0_attn_in['Wv'], 'L0_attn_bv': _L0_attn_in['bv'], 'L0_attn_Wo': _L0_attn_in['Wo'], 'L0_attn_bo': _L0_attn_in['bo'], 'L0_attn_ln1_s': _L0_attn_in['ln1_s'], 'L0_attn_ln1_b': _L0_attn_in['ln1_b'], 'L0_attn_Wf1': _L0_attn_in['Wf1'], 'L0_attn_bf1': _L0_attn_in['bf1'], 'L0_attn_Wf2': _L0_attn_in['Wf2'], 'L0_attn_bf2': _L0_attn_in['bf2'], 'L0_attn_ln2_s': _L0_attn_in['ln2_s'], 'L0_attn_ln2_b': _L0_attn_in['ln2_b'], 'L0_ffn_w_gate_w': _L0_ffn_in['w_gate_w'], 'L0_ffn_w_gate_b': _L0_ffn_in['w_gate_b'], 'L0_ffn_W1': _L0_ffn_in['W1'], 'L0_ffn_b1': _L0_ffn_in['b1'], 'L0_ffn_W2': _L0_ffn_in['W2'], 'L0_ffn_b2': _L0_ffn_in['b2'], 'L1_attn_Wq': _L1_attn_in['Wq'], 'L1_attn_bq': _L1_attn_in['bq'], 'L1_attn_Wk': _L1_attn_in['Wk'], 'L1_attn_bk': _L1_attn_in['bk'], 'L1_attn_Wv': _L1_attn_in['Wv'], 'L1_attn_bv': _L1_attn_in['bv'], 'L1_attn_Wo': _L1_attn_in['Wo'], 'L1_attn_bo': _L1_attn_in['bo'], 'L1_attn_conv_w': _L1_attn_in['conv_w'], 'L1_attn_conv_b': _L1_attn_in['conv_b'], 'L1_xattn_Wq': _L1_xattn_in['Wq'], 'L1_xattn_bq': _L1_xattn_in['bq'], 'L1_xattn_Wk': _L1_xattn_in['Wk'], 'L1_xattn_bk': _L1_xattn_in['bk'], 'L1_xattn_Wv': _L1_xattn_in['Wv'], 'L1_xattn_bv': _L1_xattn_in['bv'], 'L1_ffn_W1': _L1_ffn_in['W1'], 'L1_ffn_b1': _L1_ffn_in['b1'], 'L1_ffn_quantum_phases': _L1_ffn_in['quantum_phases'], 'L1_ffn_quantum_weights_real': _L1_ffn_in['quantum_weights_real'], 'L1_ffn_quantum_weights_imag': _L1_ffn_in['quantum_weights_imag'], 'L1_ffn_W2': _L1_ffn_in['W2'], 'L1_ffn_b2': _L1_ffn_in['b2']}

def reference(x, ctx_1024, L0_attn_Wq, L0_attn_bq, L0_attn_Wk, L0_attn_bk, L0_attn_Wv, L0_attn_bv, L0_attn_Wo, L0_attn_bo, L0_attn_ln1_s, L0_attn_ln1_b, L0_attn_Wf1, L0_attn_bf1, L0_attn_Wf2, L0_attn_bf2, L0_attn_ln2_s, L0_attn_ln2_b, L0_ffn_w_gate_w, L0_ffn_w_gate_b, L0_ffn_W1, L0_ffn_b1, L0_ffn_W2, L0_ffn_b2, L1_attn_Wq, L1_attn_bq, L1_attn_Wk, L1_attn_bk, L1_attn_Wv, L1_attn_bv, L1_attn_Wo, L1_attn_bo, L1_attn_conv_w, L1_attn_conv_b, L1_xattn_Wq, L1_xattn_bq, L1_xattn_Wk, L1_xattn_bk, L1_xattn_Wv, L1_xattn_bv, L1_ffn_W1, L1_ffn_b1, L1_ffn_quantum_phases, L1_ffn_quantum_weights_real, L1_ffn_quantum_weights_imag, L1_ffn_W2, L1_ffn_b2):
    import jax
    import jax.numpy as jnp

    def _L0_attn_ref(x, Wq, bq, Wk, bk, Wv, bv, Wo, bo, ln1_s, ln1_b, Wf1, bf1, Wf2, bf2, ln2_s, ln2_b):
        import jax, jax.numpy as jnp
        import numpy as np
        N, L, D, A, F, B = (4, 512, 128, 128, 512, 8)
        EPS_LN = 1e-06
        EPS_Z = 1e-06

        def _layernorm(x, scale, bias):
            m = jnp.mean(x, axis=-1, keepdims=True)
            v = jnp.mean(jnp.square(x - m), axis=-1, keepdims=True)
            return (x - m) * jax.lax.rsqrt(v + EPS_LN) * scale + bias

        def _block(x, p):
            Wq, bq, Wk, bk, Wv, bv, Wo, bo, ln1_s, ln1_b, Wf1, bf1, Wf2, bf2, ln2_s, ln2_b = p
            residual = x
            q = jnp.einsum('nld,da->nla', x, Wq) + bq
            k = jnp.einsum('nld,da->nla', x, Wk) + bk
            v = jnp.einsum('nld,da->nla', x, Wv) + bv
            Q = jax.nn.elu(q) + 1.0
            K = jax.nn.elu(k) + 1.0
            KV = jnp.einsum('nsh,nsh->nh', K, v)
            Ksum = jnp.sum(K, axis=1)
            Z = 1.0 / (Q * Ksum[:, None, :] + EPS_Z)
            V = Q * KV[:, None, :] * Z
            attn = jax.nn.gelu(jnp.einsum('nla,ad->nld', V, Wo) + bo)
            x = _layernorm(attn + residual, ln1_s, ln1_b)
            residual = x
            h = jax.nn.gelu(jnp.einsum('nld,df->nlf', x, Wf1) + bf1)
            ff = jax.nn.gelu(jnp.einsum('nlf,fd->nld', h, Wf2) + bf2)
            x = _layernorm(ff + residual, ln2_s, ln2_b)
            return (x, None)
        params = (Wq, bq, Wk, bk, Wv, bv, Wo, bo, ln1_s, ln1_b, Wf1, bf1, Wf2, bf2, ln2_s, ln2_b)
        out, _ = jax.lax.scan(_block, x, params)
        return out

    def _L0_xattn_ref(teacher_features, student_features):
        import jax, jax.numpy as jnp
        import numpy as np
        from jax import lax
        BIG = jnp.float32(1e+30)

        def _pairwise_euclidean(a, b):
            aa = jnp.sum(a * a, axis=-1)[:, None]
            bb = jnp.sum(b * b, axis=-1)[None, :]
            ab = a @ b.T
            return jnp.sqrt(jnp.maximum(aa + bb - 2.0 * ab, 0.0))

        def _dtw_cost(D):
            row0 = jnp.cumsum(D[0])

            def row_step(prev_row, d_row):
                first = d_row[0] + prev_row[0]

                def col_step(left, inp):
                    d_ij, up, diag = inp
                    r = d_ij + jnp.minimum(jnp.minimum(up, left), diag)
                    return (r, r)
                _, rest = lax.scan(col_step, first, (d_row[1:], prev_row[1:], prev_row[:-1]))
                row = jnp.concatenate([first[None], rest])
                return (row, row)
            _, rows = lax.scan(row_step, row0, D[1:])
            return jnp.concatenate([row0[None], rows], axis=0)

        def _backtrack(R, T1, T2):
            L = T1 + T2 - 1

            def step(carry, _):
                i, j, done = carry
                valid = jnp.logical_not(done)
                cd = jnp.where((i > 0) & (j > 0), R[jnp.maximum(i - 1, 0), jnp.maximum(j - 1, 0)], BIG)
                cu = jnp.where(i > 0, R[jnp.maximum(i - 1, 0), j], BIG)
                cl = jnp.where(j > 0, R[i, jnp.maximum(j - 1, 0)], BIG)
                choice = jnp.argmin(jnp.stack([cd, cu, cl]))
                ni = jnp.where(choice <= 1, i - 1, i)
                nj = jnp.where((choice == 0) | (choice == 2), j - 1, j)
                at_origin = (i == 0) & (j == 0)
                ni = jnp.where(at_origin, 0, ni)
                nj = jnp.where(at_origin, 0, nj)
                return ((ni, nj, done | at_origin), (i, j, valid))
            init = (jnp.int32(T1 - 1), jnp.int32(T2 - 1), jnp.bool_(False))
            _, (i_idx, j_idx, valid) = lax.scan(step, init, None, length=L)
            return (i_idx, j_idx, valid)

        def _align_one(small, large):
            T_small, d = small.shape
            T_large = large.shape[0]
            D = _pairwise_euclidean(small, large)
            R = _dtw_cost(D)
            i_idx, j_idx, valid = _backtrack(R, T_small, T_large)
            contrib = small[i_idx] * valid[:, None].astype(small.dtype)
            expanded = jnp.zeros((T_large, d), dtype=small.dtype).at[j_idx].add(contrib)
            return expanded
        return jax.vmap(_align_one)(teacher_features, student_features)

    def _L0_ffn_ref(x, w_gate_w, w_gate_b, W1, b1, W2, b2):
        import jax, jax.numpy as jnp
        import numpy as np
        TOPK = 2
        CAPACITY_FACTOR = 1.0
        EPS = 1e-06
        B, S, D = (4, 512, 128)
        E = 8
        SUB_H = 256 // E
        Bx, Sx, Dx = x.shape
        Ex = w_gate_b.shape[0]
        K = Sx // 2
        capacity = int(CAPACITY_FACTOR * Bx)
        gate_scores = jax.nn.softmax(x @ w_gate_w + w_gate_b, axis=-1)
        _, top_idx = jax.lax.top_k(gate_scores, TOPK)
        mask = jax.nn.one_hot(top_idx, Ex, dtype=gate_scores.dtype).sum(axis=-2)
        masked = gate_scores * mask
        denom = masked.sum(axis=0, keepdims=True) + EPS
        route = masked / denom * capacity
        route_eb = jnp.transpose(route, (2, 0, 1))
        _, seq_ids = jax.lax.top_k(route_eb, K)
        seq_ids = jnp.sort(seq_ids, axis=-1)
        xg = jax.vmap(lambda idx: jnp.take_along_axis(x, idx[..., None], axis=1))(seq_ids)
        h = jnp.einsum('ebkd,edh->ebkh', xg, W1) + b1[:, None, None, :]
        h = jax.nn.gelu(h, approximate=False)
        o = jnp.einsum('ebkh,ehd->ebkd', h, W2) + b2[:, None, None, :]
        flat_ids = (jnp.arange(Bx)[None, :, None] * Sx + seq_ids).reshape(-1)
        outs = jnp.zeros((Bx * Sx, Dx), x.dtype).at[flat_ids].add(o.reshape(-1, Dx))
        return outs.reshape(Bx, Sx, Dx)

    def _L1_attn_ref(query, Wq, bq, Wk, bk, Wv, bv, Wo, bo, conv_w, conv_b):
        import jax, jax.numpy as jnp
        import numpy as np
        from jax import lax
        B, S, E, H, KS = (2, 256, 128, 16, 3)
        DH = E // H
        b, s, e = query.shape
        h, dh = (H, DH)
        Q = (query @ Wq.T + bq).reshape(b, s, h, dh).transpose(0, 2, 1, 3)
        K = (query @ Wk.T + bk).reshape(b, s, h, dh).transpose(0, 2, 1, 3)
        V = (query @ Wv.T + bv).reshape(b, s, h, dh).transpose(0, 2, 1, 3)
        scores = jnp.einsum('bhqd,bhkd->bhqk', Q, K) / np.sqrt(dh).astype(np.float32)
        x = scores.transpose(0, 2, 1, 3).reshape(b * s, h, s)
        x = lax.conv_general_dilated(x, conv_w, window_strides=(1,), padding=[(KS // 2, KS // 2)], dimension_numbers=('NCW', 'OIW', 'NCW'))
        x = x + conv_b[None, :, None]
        scores = x.reshape(b, s, h, s).transpose(0, 2, 1, 3)
        weights = jax.nn.softmax(scores, axis=-1)
        out = jnp.einsum('bhqk,bhkd->bqhd', weights, V).reshape(b, s, e)
        return out @ Wo.T + bo

    def _L1_xattn_ref(queries, keys, values, Wq, bq, Wk, bk, Wv, bv):
        import jax, jax.numpy as jnp
        import numpy as np
        B, S, E = (8, 256, 128)
        q = jnp.einsum('bse,fe->bsf', queries, Wq) + bq
        k = jnp.einsum('bse,fe->bsf', keys, Wk) + bk
        v = jnp.einsum('bse,fe->bsf', values, Wv) + bv
        d = q.shape[-1]
        scores = jnp.einsum('bqe,bke->bqk', q, k) / jnp.sqrt(jnp.float32(d))
        attn = jax.nn.softmax(scores, axis=-1)
        out = jnp.einsum('bqk,bke->bqe', attn, v)
        return jnp.squeeze(out, axis=1) if out.shape[1] == 1 else out

    def _L1_ffn_ref(x, W1, b1, quantum_phases, quantum_weights_real, quantum_weights_imag, W2, b2):
        import jax, jax.numpy as jnp
        import numpy as np
        B, S, D_MODEL, D_FF = (4, 256, 128, 512)

        def _quantum_transform(hidden, theta, w_real, w_imag):
            imag = w_imag * jnp.sin(theta + hidden * 0.1)
            quantum_phase = jnp.cos(theta) * w_real + jnp.sin(theta) * w_imag
            return hidden + quantum_phase * imag * 0.1
        hidden = jnp.einsum('bsd,df->bsf', x, W1) + b1
        q = _quantum_transform(hidden, quantum_phases, quantum_weights_real, quantum_weights_imag)
        act = jax.nn.relu(q)
        return jnp.einsum('bsf,fd->bsd', act, W2) + b2
    x = x + _L0_attn_ref(_layernorm(x, axis=-1), L0_attn_Wq, L0_attn_bq, L0_attn_Wk, L0_attn_bk, L0_attn_Wv, L0_attn_bv, L0_attn_Wo, L0_attn_bo, L0_attn_ln1_s, L0_attn_ln1_b, L0_attn_Wf1, L0_attn_bf1, L0_attn_Wf2, L0_attn_bf2, L0_attn_ln2_s, L0_attn_ln2_b)
    x = x + _L0_xattn_ref(ctx_1024, _layernorm(x, axis=-1))
    x = x + _L0_ffn_ref(_layernorm(x, axis=-1), L0_ffn_w_gate_w, L0_ffn_w_gate_b, L0_ffn_W1, L0_ffn_b1, L0_ffn_W2, L0_ffn_b2)
    x = x + _L1_attn_ref(_layernorm(x, axis=-1), L1_attn_Wq, L1_attn_bq, L1_attn_Wk, L1_attn_bk, L1_attn_Wv, L1_attn_bv, L1_attn_Wo, L1_attn_bo, L1_attn_conv_w, L1_attn_conv_b)
    x = x + _L1_xattn_ref(_layernorm(x, axis=-1), ctx_1024, ctx_1024, L1_xattn_Wq, L1_xattn_bq, L1_xattn_Wk, L1_xattn_bk, L1_xattn_Wv, L1_xattn_bv)
    x = x + _L1_ffn_ref(_layernorm(x, axis=-1), L1_ffn_W1, L1_ffn_b1, L1_ffn_quantum_phases, L1_ffn_quantum_weights_real, L1_ffn_quantum_weights_imag, L1_ffn_W2, L1_ffn_b2)
    return x

_drawn_inputs = setup_inputs


def setup_inputs(seed=0):
    import zlib

    import numpy as np

    out = dict(_drawn_inputs(seed))
    spreads = {'L0_attn_bq': (0.0, 2.0),
     'L0_attn_bk': (0.0, 0.8),
     'L0_attn_bv': (0.0, 0.465),
     'L0_attn_bo': (0.0, 0.1),
     'L0_attn_ln1_s': (1.0, 0.2),
     'L0_attn_ln1_b': (0.0, 0.1),
     'L0_attn_bf1': (0.0, 0.486),
     'L0_attn_bf2': (0.0, 0.1),
     'L0_attn_ln2_s': (1.0, 0.2),
     'L0_attn_ln2_b': (0.0, 0.1),
     'L0_ffn_w_gate_b': (0.0, 0.1),
     'L0_ffn_b1': (0.0, 0.8),
     'L0_ffn_b2': (0.0, 0.1),
     'L1_xattn_bq': (0.0, 0.616),
     'L1_xattn_bk': (0.0, 2.0),
     'L1_xattn_bv': (0.0, 0.1),
     'L1_ffn_b1': (0.0, 0.277),
     'L1_ffn_b2': (0.0, 0.1)}
    factors = {'L0_attn_Wq': 64.0,
     'L0_attn_Wk': 8.0,
     'L0_attn_Wv': 4.463,
     'L0_attn_Wo': 3.125,
     'L0_ffn_W1': 4.526,
     'L0_ffn_W2': 4.109,
     'L1_attn_Wq': 8.0,
     'L1_attn_bq': 8.0,
     'L1_attn_Wk': 8.0,
     'L1_attn_bk': 200.0,
     'L1_attn_bv': 4.021,
     'L1_attn_conv_w': 8.0,
     'L1_attn_conv_b': 200.0,
     'L1_ffn_quantum_phases': 32.154,
     'L1_ffn_quantum_weights_real': 64.0,
     'L1_ffn_quantum_weights_imag': 26.398}
    for name, (base, spread) in spreads.items():
        noise = np.random.default_rng([zlib.crc32(name.encode()), seed]).standard_normal(out[name].shape)
        drawn = base * np.exp(spread * noise) if base else spread * noise
        out[name] = jnp.asarray(drawn.astype(out[name].dtype))
    for name, factor in factors.items():
        out[name] = (out[name] * factor).astype(out[name].dtype)
    return out
```

```python
from collections import namedtuple
from contextlib import ExitStack

import numpy as np

import concourse.bass as bass
from concourse import mybir

P = 128
B = 2
S = 512
NC = S // P
T = 77
LAYERS = 8
FF = 512
NF = FF // P
E = 8
HID = 32
TOPK = 2
CAP = B
KEEP = S // 2
H = 16
DH = P // H
BLK = 16
W = S // BLK
LAG = 2
SLOTS = T + LAG * (BLK - 1)
PAD = LAG * (BLK - 1)
BIG = 1e30
SHIFTS = [28, 25, 22, 19, 16, 13, 10, 7, 4, 1, 0]

F32 = mybir.dt.float32
I32 = mybir.dt.int32
BF16 = mybir.dt.bfloat16
ALU = mybir.AluOpType
ACT = mybir.ActivationFunctionType
AX = mybir.AxisListType

LOWEST = [7.0 if s == 0 else 1.0 for s in SHIFTS]

L0_COLS = ["Wq", "Wk", "Wv", "Wo", "Wf1", "Wf2", "bq", "bk", "bv", "bo", "s1", "b1", "bf2", "s2", "b2", "bf1"]
L0_WIDTH = dict(Wq=P, Wk=P, Wv=P, Wo=P, Wf1=FF, Wf2=FF, bf1=NF)


def columns(names, width):
    at, out = 0, {}
    for n in names:
        w = width.get(n, 1)
        out[n] = (at, at + w)
        at += w
    return out, at


L0_AT, L0_N = columns(L0_COLS, L0_WIDTH)
C_WIDTH = dict(row_ok=SLOTS - T, ident=P, cent=P, mean=P, one=P, shift_r=32, shift_l=32, block8=P, kk=len(SHIFTS), pick=2 * P,
               lower=E * E)
C_AT, C_N = columns(["ident", "cent", "mean", "one", "shift_r", "shift_l", "big_first", "init0", "bnd_last", "row_ok", "block8",
                     "kk", "pick", "lower"], C_WIDTH)
G_WIDTH = dict(ctxT=B * T, wg=E, bg=E, W1=E * HID, W2=2 * P, b1=2, b2=P, aWq=P, aWk=P, aWv=P, aWo=P, abv=P,
               conv_w=3 * H, conv_b=H, xWq=P, xWk=P, xWv=P, xbv=P, fW1=FF, fW2=FF, fb1=NF, ph=NF, wr=NF, wi=NF)
G_AT, G_N = columns(["ctxT", "wg", "bg", "W1", "W2", "b1", "b2", "aWq", "aWk", "aWv", "aWo", "abq", "abk", "abv",
                     "abo", "conv_w", "conv_b", "xWq", "xWk", "xWv", "xbq", "xbk", "xbv", "fW1", "fW2", "fb1", "ph",
                     "wr", "wi", "fb2"], G_WIDTH)


def constants():
    c = np.zeros((P, C_N), np.float32)

    def put(name, a):
        lo, hi = C_AT[name]
        c[:a.shape[0], lo:hi] = a

    put("ident", np.eye(P))
    put("cent", np.eye(P) - 1.0 / P)
    put("mean", np.full((P, P), 1.0 / P))
    put("one", np.ones((P, P)))
    r, l = np.zeros((32, 32)), np.zeros((32, 32))
    big, init0, last = np.zeros((32, 1)), np.full((32, 1), BIG), np.ones((32, 1))
    for b in range(B):
        for k in range(BLK):
            p = b * BLK + BLK - 1 - k
            if k + 1 < BLK:
                r[p, p - 1] = 1
                l[p - 1, p] = 1
        big[b * BLK + BLK - 1] = BIG
        init0[b * BLK + BLK - 1] = 0
        last[b * BLK] = 0
    put("shift_r", r)
    put("shift_l", l)
    put("big_first", big)
    put("init0", init0)
    put("bnd_last", last)
    ok = np.zeros((32, SLOTS - T))
    for p in range(32):
        k = BLK - 1 - p % BLK
        ok[p] = np.arange(T, SLOTS) - LAG * k < T
    put("row_ok", ok)
    put("block8", np.kron(np.eye(P // 8), np.ones((8, 8))))
    kk = np.array([[(p % 8) << s if s or p % 8 < 2 else 0 for s in SHIFTS] for p in range(P)], np.int32)
    put("kk", kk.view(np.float32))
    pick = np.zeros((P, 2, P))
    for b in range(B):
        for e in range(E):
            pick[b * 64 + e * 8, e // 4, (e % 4) * HID:(e % 4 + 1) * HID] = 1
    put("pick", pick.reshape(P, 2 * P))
    put("lower", np.broadcast_to(np.tril(np.ones((E, E)), -1).reshape(1, E * E), (P, E * E)))
    return c


class Shared:
    pass


def build(nc, a):
    with ExitStack() as ctx:
        sems = {}

        def sem(name):
            assert name not in sems
            sems[name] = ctx.enter_context(nc.semaphore(name))
            return sems[name]

        def sem_set(prefix, names):
            return namedtuple("Semaphores", names)(*(sem(f"{prefix}_{n}") for n in names.split()))

        def sb(name, shape, dt=F32, stack=ctx):
            return stack.enter_context(nc.sbuf_tensor(name, shape, dt))

        g = Shared()
        g.c = sb("consts", [P, C_N])
        g.w = sb("params", [P, G_N])
        g.xT = sb("xT", [P, B, S])
        g.nT = sb("nT", [P, B, S])
        g.ctx = sb("ctx", [T, B, P])
        g.eps6 = sb("eps6", [P, 1])
        g.eps5 = sb("eps5", [P, 1])
        g.sq = sb("sq", [P, B, S])
        g.rs = sb("rs", [P, B, S])
        g.psum = ctx.enter_context(nc.psum_tensor("banks", [P, 8, 512], F32))
        g.ps = [g.psum[:, i] for i in range(8)]
        g.sem, g.sem_set, g.sb = sem, sem_set, sb
        g.C = lambda n: g.c[:, C_AT[n][0]:C_AT[n][1]]
        g.G = lambda n: g.w[:, G_AT[n][0]:G_AT[n][1]]
        g.loaded = sem("params_loaded")
        g.ln, g.norms = sem_set("ln", LN_SEMS), 0
        load_stage(nc, a, g)
        l0_stage(nc, a, g)
        if STAGES >= 2:
            dtw_stage(nc, a, g)
        if STAGES >= 3:
            moe_stage(nc, a, g)
        if STAGES >= 4:
            attn_stage(nc, a, g)
        if STAGES >= 5:
            xattn_stage(nc, a, g)
        if STAGES >= 6:
            ffn_stage(nc, a, g)
        store_stage(nc, a, g)


STAGES = 6


def ln_pe(nc, pe, g, s, n, src, bank_c, bank_v, sq):
    nc.tensor.matmul(bank_c[:], g.C("cent"), src, start=True, stop=True).then_inc(s.cen, 1)
    pe.wait_ge(s.sq, n)
    nc.tensor.matmul(bank_v[:], g.C("mean"), sq, start=True, stop=True).then_inc(s.var, 1)


def ln_act_square(nc, act, g, s, n, bank_c, sq):
    act.wait_ge(s.cen, n)
    nc.scalar.activation(sq, bank_c[:], ACT.Square).then_inc(s.sq, 1)


def ln_act_rstd(nc, act, g, s, n, bank_v, sq, rs, eps):
    act.wait_ge(s.var, n)
    nc.scalar.activation(sq, bank_v[:], ACT.Ln, bias=eps[:]).then_inc(s.ln, 1)
    act.wait_ge(s.ln, n)
    nc.scalar.activation(rs, sq, ACT.Exp, scale=-0.5).then_inc(s.rs, 1)


LN_SET = "natural_log_exp_and_others"
LN_SEMS = "cen sq var ln rs"


def ln_block(nc, g):
    s, n0 = g.ln, g.norms * B
    g.norms += 1
    with nc.Block() as block:
        @block.tensor
        def _(pe):
            for b in range(B):
                nc.tensor.matmul(g.ps[b], g.C("cent"), g.xT[:, b], start=True, stop=True).then_inc(s.cen, 1)
            for b in range(B):
                pe.wait_ge(s.sq, n0 + b + 1)
                nc.tensor.matmul(g.ps[2 + b], g.C("mean"), g.sq[:, b], start=True, stop=True).then_inc(s.var, 1)

        @block.scalar
        def _(act):
            nc.scalar.preload_act_table_set(LN_SET)
            for b in range(B):
                ln_act_square(nc, act, g, s, n0 + b + 1, g.ps[b], g.sq[:, b])
            for b in range(B):
                ln_act_rstd(nc, act, g, s, n0 + b + 1, g.ps[2 + b], g.sq[:, b], g.rs[:, b], g.eps5)

        @block.vector
        def _(dve):
            for b in range(B):
                dve.wait_ge(s.rs, n0 + b + 1)
                nc.vector.tensor_tensor(g.nT[:, b], g.ps[b], g.rs[:, b], ALU.mult)


def load_stage(nc, a, g):
    with ExitStack() as st:
        xn = g.sb("x_rows", [P, B * NC, P], stack=st)
        s = g.sem_set("load", "x consts ctx turned")
        g.ctx_loaded = s.ctx
        with nc.Block() as block:
            @block.sync
            def _(sp):
                sp.dma_start(xn[:], a["x"].rearrange("b (c p) d -> p (b c) d", p=P)).then_inc(s.x, 16)
                sp.dma_start(g.w[:], a["params"]).then_inc(g.loaded, 16)
                sp.dma_start(g.ctx[:], a["ctx"].rearrange("b t d -> t b d")).then_inc(s.ctx, 16)

            @block.scalar
            def _(act):
                act.dma_start(g.c[:], a["consts"]).then_inc(s.consts, 16)

            @block.tensor
            def _(pe):
                pe.wait_ge(s.x, 16)
                pe.wait_ge(s.consts, 16)
                for b in range(B):
                    for c in range(NC):
                        last = nc.tensor.transpose(g.ps[b][:, c * P:(c + 1) * P], xn[:, b * NC + c, :], g.C("ident"))
                    last.then_inc(s.turned, 1)

            @block.vector
            def _(dve):
                nc.vector.memset(g.eps6[:], 1e-6)
                nc.vector.memset(g.eps5[:], 1e-5)
                for b in range(B):
                    dve.wait_ge(s.turned, b + 1)
                    nc.vector.tensor_copy(g.xT[:, b], g.ps[b][:])
    ln_block(nc, g)


def l0_stage(nc, a, g):
    with ExitStack() as st:
        def sb(name, shape, dt=F32):
            return g.sb("l0_" + name, shape, dt, stack=st)

        wt = sb("wt", [P, 2, L0_N])
        x = sb("x", [P, B, S])
        x1 = sb("x1", [P, B, S])
        eq, rq, ek, rk = (sb(n, [P, B, S]) for n in ("eq", "rq", "ek", "rk"))
        Q, K, V, den, rec, junk = (sb(n, [P, B, S]) for n in ("Q", "K", "V", "den", "rec", "junk"))
        go, r1, gf, r2, u = (sb(n, [P, B, S]) for n in ("go", "r1", "gf", "r2", "u"))
        h = sb("h", [P, B, NF, S])
        ksum, kv = sb("ksum", [P, B, 1]), sb("kv", [P, B, 1])
        s = g.sem_set("l0", "w0 w1 q k v eq ek mq mk Q K kv den rec V o go r1 h1 hg f2 gf r2 x u1 x1 u2 x0")
        n1, n2 = g.sem_set("l0n1", LN_SEMS), g.sem_set("l0n2", LN_SEMS)
        bank = [[g.ps[4 * b + i] for i in range(4)] for b in range(B)]

        def wcol(u_, n):
            return wt[:, u_, L0_AT[n][0]:L0_AT[n][1]]

        with nc.Block() as block:
            @block.sync
            def _(sp):
                for l in range(2):
                    sp.dma_start(wt[:, l], a["l0"][l]).then_inc((s.w0, s.w1)[l], 16)
                with sp.Fori(0, LAYERS // 2 - 1) as i:
                    for l in range(2):
                        sp.wait_ge(s.x, i * 4 + (2 * l + 2))
                        sp.dma_start(wt[:, l], a["l0"][bass.ds(i * 2 + (l + 2), 1)].rearrange("o p n -> p (o n)")
                                     ).then_inc((s.w0, s.w1)[l], 16)
                sp.wait_ge(g.ctx_loaded, 16)
                sp.wait_ge(g.loaded, 16)

            @block.tensor
            def _(pe):
                pe.wait_ge(s.x0, B)
                with pe.Fori(0, LAYERS // 2) as i:
                    for l in range(2):
                        pe.wait_ge((s.w0, s.w1)[l], i * 16 + 16)
                        for b in range(B):
                            n = i * 4 + (2 * l + b + 1)
                            if l > 0:
                                pe.wait_ge(s.x, n - 2)
                            for j, (w, sg) in enumerate((("Wq", s.q), ("Wk", s.k), ("Wv", s.v))):
                                nc.tensor.matmul(bank[b][j][:], wcol(l, w), x[:, b], start=True, stop=True
                                                 ).then_inc(sg, 1)
                        for b in range(B):
                            n = i * 4 + (2 * l + b + 1)
                            pe.wait_ge(s.V, n)
                            nc.tensor.matmul(bank[b][0][:], wcol(l, "Wo"), V[:, b], start=True, stop=True
                                             ).then_inc(s.o, 1)
                        for b in range(B):
                            pe.wait_ge(s.r1, i * 4 + (2 * l + b + 1))
                            nc.tensor.matmul(bank[b][1][:], g.C("cent"), r1[:, b], start=True, stop=True
                                             ).then_inc(n1.cen, 1)
                        for b in range(B):
                            pe.wait_ge(n1.sq, i * 4 + (2 * l + b + 1))
                            nc.tensor.matmul(bank[b][3][:], g.C("mean"), g.sq[:, b], start=True, stop=True
                                             ).then_inc(n1.var, 1)
                        for b in range(B):
                            pe.wait_ge(s.x1, i * 4 + (2 * l + b + 1))
                            for f, j in enumerate((0, 2, 3, 1)):
                                nc.tensor.matmul(bank[b][j][:], wcol(l, "Wf1")[:, f * P:(f + 1) * P], x1[:, b],
                                                 start=True, stop=True).then_inc(s.h1, 1)
                        for b in range(B):
                            for f in range(NF):
                                pe.wait_ge(s.hg, i * 16 + (8 * l + 4 * b + f + 1))
                                last = nc.tensor.matmul(bank[b][0][:], wcol(l, "Wf2")[:, f * P:(f + 1) * P],
                                                        h[:, b, f], start=(f == 0), stop=(f == NF - 1))
                            last.then_inc(s.f2, 1)
                        for b in range(B):
                            pe.wait_ge(s.r2, i * 4 + (2 * l + b + 1))
                            nc.tensor.matmul(bank[b][1][:], g.C("cent"), r2[:, b], start=True, stop=True
                                             ).then_inc(n2.cen, 1)
                        for b in range(B):
                            pe.wait_ge(n2.sq, i * 4 + (2 * l + b + 1))
                            nc.tensor.matmul(bank[b][2][:], g.C("mean"), g.sq[:, b], start=True, stop=True
                                             ).then_inc(n2.var, 1)
                    for b in range(B):
                        pe.wait_ge(s.x, i * 4 + (2 + b + 1))

            @block.scalar
            def _(act):
                with act.Fori(0, LAYERS // 2) as i:
                    for l in range(2):
                        nc.scalar.preload_act_table_set(LN_SET)
                        act.wait_ge((s.w0, s.w1)[l], i * 16 + 16)
                        for b in range(B):
                            n = i * 4 + (2 * l + b + 1)
                            for j, sg, e_, r_, bias, out in ((0, s.q, eq, rq, "bq", s.eq), (1, s.k, ek, rk, "bk", s.ek)):
                                act.wait_ge(sg, n)
                                nc.scalar.activation(e_[:, b], bank[b][j][:], ACT.Exp, bias=wcol(l, bias))
                                nc.scalar.activation(r_[:, b], bank[b][j][:], ACT.Relu, bias=wcol(l, bias)
                                                     ).then_inc(out, 1)
                        for b in range(B):
                            n = i * 4 + (2 * l + b + 1)
                            act.wait_ge(s.Q, n)
                            act.wait_ge(s.K, n)
                            nc.scalar.activation(den[:, b], Q[:, b], ACT.Ln, bias=g.eps6[:], scale=ksum[:, b]
                                                 ).then_inc(s.den, 1)
                            act.wait_ge(s.den, n)
                            nc.scalar.activation(rec[:, b], den[:, b], ACT.Exp, scale=-1.0).then_inc(s.rec, 1)
                        nc.scalar.preload_act_table(ACT.Gelu_apprx_tanh)
                        for b in range(B):
                            act.wait_ge(s.o, i * 4 + (2 * l + b + 1))
                            nc.scalar.activation(go[:, b], bank[b][0][:], ACT.Gelu_apprx_tanh, bias=wcol(l, "bo")
                                                 ).then_inc(s.go, 1)
                        nc.scalar.preload_act_table_set(LN_SET)
                        for b in range(B):
                            ln_act_square(nc, act, g, n1, i * 4 + (2 * l + b + 1), bank[b][1], g.sq[:, b])
                        for b in range(B):
                            ln_act_rstd(nc, act, g, n1, i * 4 + (2 * l + b + 1), bank[b][3], g.sq[:, b], g.rs[:, b],
                                        g.eps6)
                        nc.scalar.preload_act_table(ACT.Gelu_apprx_tanh)
                        for b in range(B):
                            for f, j in enumerate((0, 2, 3, 1)):
                                act.wait_ge(s.h1, i * 16 + (8 * l + 4 * b + f + 1))
                                nc.scalar.activation(h[:, b, f], bank[b][j][:], ACT.Gelu_apprx_tanh,
                                                     bias=wcol(l, "bf1")[:, f:f + 1]).then_inc(s.hg, 1)
                        for b in range(B):
                            act.wait_ge(s.f2, i * 4 + (2 * l + b + 1))
                            nc.scalar.activation(gf[:, b], bank[b][0][:], ACT.Gelu_apprx_tanh, bias=wcol(l, "bf2")
                                                 ).then_inc(s.gf, 1)
                        nc.scalar.preload_act_table_set(LN_SET)
                        for b in range(B):
                            ln_act_square(nc, act, g, n2, i * 4 + (2 * l + b + 1), bank[b][1], g.sq[:, b])
                        for b in range(B):
                            ln_act_rstd(nc, act, g, n2, i * 4 + (2 * l + b + 1), bank[b][2], g.sq[:, b], g.rs[:, b],
                                        g.eps6)

            @block.vector
            def _(dve):
                for b in range(B):
                    nc.vector.tensor_copy(x[:, b], g.nT[:, b]).then_inc(s.x0, 1)
                dve.wait_ge(s.x0, B)
                with dve.Fori(0, LAYERS // 2) as i:
                    for l in range(2):
                        dve.wait_ge((s.w0, s.w1)[l], i * 16 + 16)
                        for b in range(B):
                            n = i * 4 + (2 * l + b + 1)
                            dve.wait_ge(s.eq, n)
                            nc.vector.tensor_scalar(eq[:, b], eq[:, b], 1.0, -1.0, ALU.min, ALU.add).then_inc(s.mq, 1)
                            dve.wait_ge(s.ek, n)
                            nc.vector.tensor_scalar(ek[:, b], ek[:, b], 1.0, -1.0, ALU.min, ALU.add).then_inc(s.mk, 1)
                            dve.wait_ge(s.mq, n)
                            nc.vector.scalar_tensor_tensor(out=Q[:, b], in0=eq[:, b], scalar=1.0, in1=rq[:, b],
                                                           op0=ALU.add, op1=ALU.add).then_inc(s.Q, 1)
                            dve.wait_ge(s.mk, n)
                            nc.vector.scalar_tensor_tensor(out=K[:, b], in0=ek[:, b], scalar=1.0, in1=rk[:, b],
                                                           op0=ALU.add, op1=ALU.add, accum_out=ksum[:, b]
                                                           ).then_inc(s.K, 1)
                            dve.wait_ge(s.v, n)
                            dve.wait_ge(s.K, n)
                            nc.vector.scalar_tensor_tensor(out=junk[:, b], in0=bank[b][2][:], scalar=wcol(l, "bv"),
                                                           in1=K[:, b], op0=ALU.add, op1=ALU.mult,
                                                           accum_out=kv[:, b]).then_inc(s.kv, 1)
                            dve.wait_ge(s.rec, n)
                            dve.wait_ge(s.kv, n)
                            nc.vector.scalar_tensor_tensor(out=V[:, b], in0=Q[:, b], scalar=kv[:, b], in1=rec[:, b],
                                                           op0=ALU.mult, op1=ALU.mult).then_inc(s.V, 1)
                        for b in range(B):
                            dve.wait_ge(s.go, i * 4 + (2 * l + b + 1))
                            nc.vector.tensor_tensor(r1[:, b], go[:, b], x[:, b], ALU.add).then_inc(s.r1, 1)
                        for b in range(B):
                            n = i * 4 + (2 * l + b + 1)
                            dve.wait_ge(n1.rs, n)
                            nc.vector.tensor_tensor(u[:, b], bank[b][1][:], g.rs[:, b], ALU.mult).then_inc(s.u1, 1)
                            dve.wait_ge(s.u1, n)
                            nc.vector.tensor_scalar(x1[:, b], u[:, b], wcol(l, "s1"), wcol(l, "b1"), ALU.mult, ALU.add
                                                    ).then_inc(s.x1, 1)
                        for b in range(B):
                            n = i * 4 + (2 * l + b + 1)
                            dve.wait_ge(s.gf, n)
                            dve.wait_ge(s.x1, n)
                            nc.vector.tensor_tensor(r2[:, b], gf[:, b], x1[:, b], ALU.add).then_inc(s.r2, 1)
                        for b in range(B):
                            n = i * 4 + (2 * l + b + 1)
                            dve.wait_ge(n2.rs, n)
                            nc.vector.tensor_tensor(u[:, b], bank[b][1][:], g.rs[:, b], ALU.mult).then_inc(s.u2, 1)
                            dve.wait_ge(s.u2, n)
                            nc.vector.tensor_scalar(x[:, b], u[:, b], wcol(l, "s2"), wcol(l, "b2"), ALU.mult, ALU.add
                                                    ).then_inc(s.x, 1)
                        dve.wait_ge(s.x, i * 4 + (2 * l + 2))
                for b in range(B):
                    nc.vector.tensor_tensor(g.xT[:, b], g.xT[:, b], x[:, b], ALU.add).then_inc(s.x0, 1)


def dtw_stage(nc, a, g):
    ln_block(nc, g)
    with ExitStack() as st:
        def sb(name, shape, dt=F32):
            return g.sb("dtw_" + name, shape, dt, stack=st)

        rows = T + 2 * PAD
        scr_d = [nc.dram_tensor(f"scratch_dist{b}", (rows, S), F32, kind="Internal").ap() for b in range(B)]
        scr_p = [nc.dram_tensor(f"scratch_path{b}", (rows, S), F32, kind="Internal").ap() for b in range(B)]
        ctx2 = sb("ctx2", [P, B * T])
        nsq = sb("nsq", [P, B, S])
        junk, aa = sb("junk", [T, P]), sb("aa", [T, B])
        d2, dist = sb("d2", [T, B, S]), sb("dist", [T, B, S])
        zero = sb("zero", [PAD, S])
        D = sb("D", [32, SLOTS, W])
        R = sb("R", [32, SLOTS + 1, W + 1])
        q = sb("q", [32, SLOTS, W])
        isq, isn, left = sb("diag_le_up", [32, SLOTS, W]), sb("not_left", [32, SLOTS, W]), sb("nu", [32, SLOTS, W])
        dg = sb("diag", [32, SLOTS, W + 1])
        theta = sb("theta", [32, SLOTS, W])
        I = sb("I", [32, SLOTS + 1, W + 1])
        X = sb("X", [32, SLOTS, W])
        t1, t2, path = isq, isn, left
        pn = sb("path_rows", [T, B, S])
        s = g.sem_set("dtw", "nsq ctx2 aa dd d2 dist zero stored D q R edge Redge big m dgc dge theta X I Iedge t P "
                             "pst pn ex")

        def skewed(scr):
            return bass.AP(tensor=scr.tensor, offset=scr.offset + W * (BLK - 1),
                           ap=[[LAG * S - W, BLK], [S, SLOTS], [1, W]])

        psR, psI, psG, psD = g.ps[0:2], g.ps[5:7], g.ps[2], g.ps[3:5]
        with nc.Block() as block:
            @block.scalar
            def _(act):
                for b in range(B):
                    nc.scalar.activation(nsq[:, b], g.nT[:, b], ACT.Square).then_inc(s.nsq, 1)
                nc.scalar.preload_act_table(ACT.Sqrt)
                for b in range(B):
                    act.wait_ge(s.d2, b + 1)
                    nc.scalar.activation(dist[:, b], d2[:, b], ACT.Sqrt).then_inc(s.dist, 1)
                for t in range(SLOTS - LAG):
                    act.wait_ge(s.edge, t + 1)
                    nc.scalar.activation(R[:, t + LAG + 1, 0:1], psR[t % 2][0:32, t:t + 1], ACT.Identity,
                                         bias=g.C("big_first")[0:32]).then_inc(s.Redge, 1)

            @block.tensor
            def _(pe):
                pe.wait_ge(s.ctx2, 1)
                for b in range(B):
                    pe.wait_ge(s.nsq, b + 1)
                    nc.tensor.matmul(psD[b][0:T, :], g.C("one")[:, 0:T], nsq[:, b], start=True, stop=False)
                    nc.tensor.matmul(psD[b][0:T, :], ctx2[:, b * T:(b + 1) * T], g.nT[:, b], start=False, stop=True
                                     ).then_inc(s.dd, 1)
                for t in range(SLOTS - LAG):
                    pe.wait_ge(s.R, t + 1)
                    nc.tensor.matmul(psR[t % 2][0:32, t:t + 1], g.C("shift_r")[0:32], R[:, t + 1, W:W + 1],
                                     start=True, stop=True).then_inc(s.edge, 1)

            @block.vector
            def _(dve):
                nc.vector.tensor_scalar(ctx2[:], g.G("ctxT"), -2.0, None, ALU.mult).then_inc(s.ctx2, 1)
                nc.vector.memset(zero[:], 0.0).then_inc(s.zero, 1)
                for b in range(B):
                    if b:
                        dve.wait_ge(s.aa, b)
                    nc.vector.scalar_tensor_tensor(out=junk[:], in0=g.ctx[:, b], scalar=1.0, in1=g.ctx[:, b],
                                                   op0=ALU.mult, op1=ALU.mult, accum_out=aa[:, b:b + 1]
                                                   ).then_inc(s.aa, 1)
                dve.wait_ge(s.aa, B)
                for b in range(B):
                    dve.wait_ge(s.dd, b + 1)
                    nc.vector.tensor_scalar(d2[:, b], psD[b][0:T, :], aa[:, b:b + 1], 0.0, ALU.add, ALU.max
                                            ).then_inc(s.d2, 1)
                nc.vector.memset(R[:, 0, :], BIG)
                nc.vector.memset(R[:, 1:LAG + 1, 0:1], BIG).then_inc(s.big, 1)
                dve.wait_ge(s.big, 1)
                dve.wait_ge(s.D, 16 * B)
                for t in range(SLOTS):
                    if t >= 1:
                        dve.wait_ge(s.R, t)
                    nc.vector.tensor_tensor(q[:, t], R[:, t, 0:W], R[:, t, 1:W + 1], ALU.min).then_inc(s.q, 1)
                    dve.wait_ge(s.q, t + 1)
                    if t >= LAG:
                        dve.wait_ge(s.Redge, t - LAG + 1)
                    first = g.C("init0")[0:32] if t == 0 else R[:, t + 1, 0:1]
                    nc.vector.tensor_tensor_scan(R[:, t + 1, 1:W + 1], q[:, t], D[:, t], first, ALU.min, ALU.add
                                                 ).then_inc(s.R, 1)

            @block.sync
            def _(sp):
                sp.wait_ge(s.zero, 1)
                for b in range(B):
                    sp.dma_start(scr_d[b][0:PAD, :], zero[:]).then_inc(s.stored, 16)
                    sp.dma_start(scr_d[b][PAD + T:rows, :], zero[:]).then_inc(s.stored, 16)
                for b in range(B):
                    sp.wait_ge(s.dist, b + 1)
                    sp.dma_start(scr_d[b][PAD:PAD + T, :], dist[:, b]).then_inc(s.stored, 16)
                sp.wait_ge(s.stored, 16 * 3 * B)
                for b in range(B):
                    sp.dma_start(D[b * BLK:(b + 1) * BLK], skewed(scr_d[b])).then_inc(s.D, 16)

        with nc.Block() as block:
            @block.vector
            def _(dve):
                up, cd, cl = R[:, 0:SLOTS, 1:W + 1], R[:, 0:SLOTS, 0:W], R[:, 1:SLOTS + 1, 0:W]
                nc.vector.tensor_tensor(isq[:], cd, up, ALU.is_le)
                nc.vector.tensor_tensor(isn[:], q[:], cl, ALU.is_le).then_inc(s.m, 1)
                dve.wait_ge(s.m, 1)
                nc.vector.tensor_tensor(dg[:, :, 0:W], isq[:], isn[:], ALU.mult).then_inc(s.m, 1)
                dve.wait_ge(s.m, 2)
                nc.vector.scalar_tensor_tensor(out=left[:], in0=isn[:], scalar=1.0, in1=dg[:, :, 0:W],
                                               op0=ALU.subtract, op1=ALU.subtract).then_inc(s.m, 1)
                nc.vector.memset(dg[:, :, W:W + 1], 0.0).then_inc(s.dge, 1)
                dve.wait_ge(s.dge, 1)
                dve.wait_ge(s.dgc, 1)
                nc.vector.tensor_copy(dg[:, 0:SLOTS - LAG, W], psG[0:32, LAG:SLOTS]).then_inc(s.dge, 1)
                dve.wait_ge(s.dge, 2)
                dve.wait_ge(s.m, 3)
                nc.vector.scalar_tensor_tensor(out=theta[:], in0=dg[:, :, 1:W + 1], scalar=2.0, in1=left[:],
                                               op0=ALU.subtract, op1=ALU.mult).then_inc(s.theta, 1)
                dve.wait_ge(s.theta, 1)
                nc.vector.tensor_tensor(theta[:, T:SLOTS], theta[:, T:SLOTS],
                                        g.C("row_ok")[0:32].unsqueeze(2).broadcast_to([32, SLOTS - T, W]), ALU.mult
                                        ).then_inc(s.theta, 1)
                nc.vector.memset(I[:, SLOTS, 0:W], 1.0)
                for t in range(SLOTS, SLOTS - LAG - 1, -1):
                    last = nc.vector.tensor_copy(I[:, t, W:W + 1], g.C("bnd_last")[0:32])
                last.then_inc(s.theta, 1)
                dve.wait_ge(s.theta, 3)
                for k, t in enumerate(range(SLOTS - 1, -1, -1)):
                    if k >= 1:
                        dve.wait_ge(s.I, k)
                    nc.vector.tensor_tensor(X[:, t], I[:, t + 1, 0:W], I[:, t + 1, 1:W + 1], ALU.add).then_inc(s.X, 1)
                    dve.wait_ge(s.X, k + 1)
                    if k >= LAG:
                        dve.wait_ge(s.Iedge, k - LAG + 1)
                    nc.vector.tensor_tensor_scan(I[:, t, W - 1::-1], X[:, t, ::-1], theta[:, t, ::-1],
                                                 I[:, t, W:W + 1], ALU.add, ALU.is_gt).then_inc(s.I, 1)
                dve.wait_ge(s.I, SLOTS)
                now, nxt = I[:, 1:SLOTS + 1], I[:, 0:SLOTS]
                nc.vector.tensor_tensor(t1[:], nxt[:, :, 0:W], nxt[:, :, 1:W + 1], ALU.subtract)
                nc.vector.tensor_tensor(t2[:], dg[:, :, 1:W + 1], now[:, :, 1:W + 1], ALU.mult).then_inc(s.t, 1)
                dve.wait_ge(s.t, 1)
                nc.vector.tensor_tensor(t2[:], t1[:], t2[:], ALU.mult)
                nc.vector.tensor_tensor(path[:], now[:, :, 0:W], nxt[:, :, 1:W + 1], ALU.subtract).then_inc(s.t, 1)
                dve.wait_ge(s.t, 2)
                nc.vector.tensor_tensor(path[:], path[:], t2[:], ALU.subtract).then_inc(s.P, 1)
                for b in range(B):
                    dve.wait_ge(s.ex, b + 1)
                    nc.vector.tensor_tensor(g.xT[:, b], g.xT[:, b], psD[b][:], ALU.add)

            @block.tensor
            def _(pe):
                pe.wait_ge(s.m, 2)
                nc.tensor.matmul(psG[0:32, 0:SLOTS], g.C("shift_l")[0:32], dg[:, :, 0], start=True, stop=True
                                 ).then_inc(s.dgc, 1)
                for k, t in enumerate(range(SLOTS - 1, LAG - 1, -1)):
                    pe.wait_ge(s.I, k + 1)
                    nc.tensor.matmul(psI[t % 2][0:32, t:t + 1], g.C("shift_l")[0:32], I[:, t, 0:1],
                                     start=True, stop=True).then_inc(s.edge, 1)
                for b in range(B):
                    pe.wait_ge(s.pn, 16 * B)
                    nc.tensor.matmul(psD[b][:], g.ctx[:, b], pn[:, b], start=True, stop=True).then_inc(s.ex, 1)

            @block.scalar
            def _(act):
                for k, t in enumerate(range(SLOTS - 1, LAG - 1, -1)):
                    act.wait_ge(s.edge, SLOTS - LAG + k + 1)
                    nc.scalar.activation(I[:, t - LAG, W:W + 1], psI[t % 2][0:32, t:t + 1], ACT.Identity).then_inc(s.Iedge, 1)

            @block.sync
            def _(sp):
                sp.wait_ge(s.P, 1)
                for b in range(B):
                    sp.dma_start(skewed(scr_p[b]), path[b * BLK:(b + 1) * BLK]).then_inc(s.pst, 16)
                sp.wait_ge(s.pst, 16 * B)
                for b in range(B):
                    sp.dma_start(pn[:, b], scr_p[b][PAD:PAD + T, :]).then_inc(s.pn, 16)


def moe_stage(nc, a, g):
    ln_block(nc, g)
    with ExitStack() as st:
        def sb(name, shape, dt=F32):
            return g.sb("moe_" + name, shape, dt, stack=st)

        N = B * NC
        lg, ex, mx = sb("lg", [P, N, E]), sb("ex", [P, N, E]), sb("mx", [P, N])
        sm, rsm, sc = sb("sm", [P, N]), sb("rsm", [P, N]), sb("sc", [P, N, E])
        gt, ge, rank, top = sb("gt", [P, N * E, E]), sb("ge", [P, N * E, E]), sb("rank", [P, N * E]), sb("top", [P, N, E])
        den, rden, route = sb("den", [P, NC, E]), sb("rden", [P, NC, E]), sb("route", [P, NC, B, E])
        route8 = sb("route8", [P, NC, B * E * 8])
        v = sb("v", [P, S])
        hit = sb("hit", [P, S])
        cnt, enough, pick_i = sb("cnt", [P, 1]), sb("enough", [P, 1], BF16), sb("pick_i", [P, 1], I32)
        low, thr = sb("low", [P, 1], I32), sb("thr", [P, 1], I32)
        above, eqm, run, chosen = sb("above", [P, S]), sb("eqm", [P, S]), sb("run", [P, S]), sb("chosen", [P, S])
        room = sb("room", [P, 2])
        block8 = sb("block8", [P, P], BF16)
        hT = sb("hT", [P, B, 2, S])
        s = g.sem_set("moe", "gate gates ex0 ex vps v low thr cnt enough sum pick route8 "
                             "b8 above eqm run room chosen h1 h mask hm out")
        psA, psV, psS = g.ps[0], g.ps[1], g.ps[2]
        kk = g.C("kk").bitcast(I32)
        NF_ = len(SHIFTS)
        with nc.Block() as block:
            @block.tensor
            def _(pe):
                for b in range(B):
                    for c in range(NC):
                        n = b * NC + c
                        last = nc.tensor.matmul(psA[:, n * E:(n + 1) * E], g.nT[:, b, c * P:(c + 1) * P], g.G("wg"),
                                                start=True, stop=True)
                last.then_inc(s.gate, 1)
                for b in range(B):
                    for k in range(2):
                        nc.tensor.matmul(g.ps[4 + 2 * b + k][:], g.G("W1")[:, k * P:(k + 1) * P], g.nT[:, b],
                                         start=True, stop=True).then_inc(s.h1, 1)
                pe.wait_ge(s.route8, 1)
                for c in range(NC):
                    last = nc.tensor.matmul(psV[:, c * P:(c + 1) * P], route8[:, c], g.C("ident"), start=True,
                                            stop=True)
                last.then_inc(s.vps, 1)
                pe.wait_ge(s.b8, 1)
                for n in range(NF_):
                    pe.wait_ge(s.enough, n + 1)
                    nc.tensor.matmul(psS[:, n:n + 1], block8[:], enough[:], start=True, stop=True).then_inc(s.sum, 1)
                pe.wait_ge(s.chosen, 1)
                pe.wait_ge(s.h, 4)
                for b in range(B):
                    rows = slice(b * 64, b * 64 + 64)
                    for k in range(2):
                        nc.tensor.matmul(g.ps[4 + 2 * b + k][:], g.C("pick")[rows, k * P:(k + 1) * P], chosen[rows],
                                         start=True, stop=True).then_inc(s.mask, 1)
                for b in range(B):
                    rows = slice(b * 64, b * 64 + 64)
                    nc.tensor.matmul(g.ps[b][:], g.G("b2")[rows], chosen[rows], start=True, stop=False)
                    for k in range(2):
                        pe.wait_ge(s.hm, 2 * b + k + 1)
                        last = nc.tensor.matmul(g.ps[b][:], g.G("W2")[:, k * P:(k + 1) * P], hT[:, b, k],
                                                start=False, stop=(k == 1))
                    last.then_inc(s.out, 1)

            @block.scalar
            def _(act):
                act.wait_ge(s.ex0, 1)
                nc.scalar.activation(ex[:], lg[:], ACT.Exp).then_inc(s.ex, 1)
                for b in range(B):
                    for k in range(2):
                        act.wait_ge(s.h1, 2 * b + k + 1)
                        nc.scalar.activation(hT[:, b, k], g.ps[4 + 2 * b + k][:], ACT.Gelu,
                                             bias=g.G("b1")[:, k:k + 1]).then_inc(s.h, 1)

            @block.vector
            def _(dve):
                def bc(t, axis, shape):
                    return t.unsqueeze(axis).broadcast_to(shape)

                nc.vector.tensor_copy(block8[:], g.C("block8")).then_inc(s.b8, 1)
                nc.vector.memset(low[:], 0).then_inc(s.low, 1)
                dve.wait_ge(s.gate, 1)
                nc.vector.tensor_tensor(lg[:], psA[:, 0:N * E].rearrange("p (n e) -> p n e", e=E),
                                        bc(g.G("bg"), 1, [P, N, E]), ALU.add).then_inc(s.gates, 1)
                dve.wait_ge(s.gates, 1)
                nc.vector.tensor_reduce(mx[:], lg[:], AX.X, ALU.max).then_inc(s.gates, 1)
                dve.wait_ge(s.gates, 2)
                nc.vector.tensor_tensor(lg[:], lg[:], bc(mx[:], 2, [P, N, E]), ALU.subtract).then_inc(s.ex0, 1)
                dve.wait_ge(s.ex, 1)
                nc.vector.tensor_reduce(sm[:], ex[:], AX.X, ALU.add).then_inc(s.gates, 1)
                dve.wait_ge(s.gates, 3)
                nc.vector.reciprocal(rsm[:], sm[:]).then_inc(s.gates, 1)
                dve.wait_ge(s.gates, 4)
                nc.vector.tensor_tensor(sc[:], ex[:], bc(rsm[:], 2, [P, N, E]), ALU.mult).then_inc(s.gates, 1)
                dve.wait_ge(s.gates, 5)
                mine = bc(sc[:].rearrange("p n e -> p (n e)"), 2, [P, N * E, E]).rearrange("p (n e) f -> p n e f", e=E)
                other = bc(sc[:], 2, [P, N, E, E])
                gt4, ge4 = (t[:].rearrange("p (n e) f -> p n e f", e=E) for t in (gt, ge))
                nc.vector.tensor_tensor(gt4, other, mine, ALU.is_gt)
                nc.vector.tensor_tensor(ge4, other, mine, ALU.is_ge).then_inc(s.gates, 1)
                dve.wait_ge(s.gates, 6)
                lower = bc(g.C("lower"), 1, [P, N, E * E])
                flat = lambda t: t[:].rearrange("p (n e) f -> p n (e f)", e=E)
                nc.vector.tensor_tensor(flat(ge), flat(ge), lower, ALU.mult).then_inc(s.gates, 1)
                dve.wait_ge(s.gates, 7)
                nc.vector.tensor_tensor(gt[:], gt[:], ge[:], ALU.max).then_inc(s.gates, 1)
                dve.wait_ge(s.gates, 8)
                nc.vector.tensor_reduce(rank[:], gt[:], AX.X, ALU.add).then_inc(s.gates, 1)
                dve.wait_ge(s.gates, 9)
                nc.vector.scalar_tensor_tensor(out=top[:].rearrange("p n e -> p (n e)"), in0=rank[:],
                                               scalar=float(TOPK), in1=sc[:].rearrange("p n e -> p (n e)"),
                                               op0=ALU.is_lt, op1=ALU.mult).then_inc(s.gates, 1)
                dve.wait_ge(s.gates, 10)
                nc.vector.scalar_tensor_tensor(out=den[:], in0=top[:, 0:NC], scalar=1.0, in1=top[:, NC:N],
                                               op0=ALU.mult, op1=ALU.add).then_inc(s.gates, 1)
                dve.wait_ge(s.gates, 11)
                nc.vector.tensor_scalar(den[:], den[:], 1e-6, None, ALU.add).then_inc(s.gates, 1)
                dve.wait_ge(s.gates, 12)
                nc.vector.reciprocal(rden[:], den[:]).then_inc(s.gates, 1)
                dve.wait_ge(s.gates, 13)
                for b in range(B):
                    last = nc.vector.scalar_tensor_tensor(out=route[:, :, b, :], in0=top[:, b * NC:(b + 1) * NC],
                                                          scalar=float(CAP), in1=rden[:], op0=ALU.mult, op1=ALU.mult)
                last.then_inc(s.gates, 1)
                dve.wait_ge(s.gates, 14)
                nc.vector.tensor_copy(route8[:].rearrange("p c (r k) -> p (c r) k", k=8),
                                      bc(route[:].rearrange("p c b e -> p (c b e)"), 2, [P, NC * B * E, 8])
                                      ).then_inc(s.route8, 1)
                dve.wait_ge(s.vps, 1)
                nc.vector.tensor_copy(v[:], psV[:]).then_inc(s.v, 1)
                dve.wait_ge(s.low, 1)
                nc.vector.tensor_tensor(thr[:], low[:], kk[:, 0:1], ALU.bitwise_or).then_inc(s.thr, 1)
                dve.wait_ge(s.v, 1)
                for n, shift in enumerate(SHIFTS):
                    dve.wait_ge(s.thr, n + 1)
                    nc.vector.tensor_scalar(hit[:], v[:], thr[:].bitcast(F32), None, ALU.is_ge, ALU.add,
                                            accum_out=cnt[:]).then_inc(s.cnt, 1)
                    dve.wait_ge(s.cnt, n + 1)
                    nc.vector.tensor_scalar(enough[:], cnt[:], float(KEEP), None, ALU.is_ge).then_inc(s.enough, 1)
                    dve.wait_ge(s.sum, n + 1)
                    nc.vector.tensor_scalar(pick_i[:], psS[:, n:n + 1], -LOWEST[n], float(1 << shift), ALU.add, ALU.mult
                                            ).then_inc(s.pick, 1)
                    dve.wait_ge(s.pick, n + 1)
                    nc.vector.tensor_tensor(low[:], low[:], pick_i[:], ALU.bitwise_or).then_inc(s.low, 1)
                    dve.wait_ge(s.low, n + 2)
                    if n + 1 < NF_:
                        nc.vector.tensor_tensor(thr[:], low[:], kk[:, n + 1:n + 2], ALU.bitwise_or).then_inc(s.thr, 1)
                least = low[:].bitcast(F32)
                nc.vector.tensor_scalar(above[:], v[:], least, None, ALU.is_gt, ALU.add, accum_out=room[:, 0:1]
                                        ).then_inc(s.above, 1)
                nc.vector.tensor_scalar(eqm[:], v[:], least, None, ALU.is_equal).then_inc(s.eqm, 1)
                dve.wait_ge(s.above, 1)
                nc.vector.tensor_scalar(room[:, 1:2], room[:, 0:1], -1.0, float(KEEP), ALU.mult, ALU.add
                                        ).then_inc(s.room, 1)
                dve.wait_ge(s.eqm, 1)
                nc.vector.tensor_tensor_scan(run[:], g.C("one")[:, 0:1].broadcast_to([P, S]), eqm[:], 0.0,
                                             ALU.mult, ALU.add).then_inc(s.run, 1)
                dve.wait_ge(s.run, 1)
                dve.wait_ge(s.room, 1)
                nc.vector.scalar_tensor_tensor(out=run[:], in0=run[:], scalar=room[:, 1:2], in1=eqm[:], op0=ALU.is_le,
                                               op1=ALU.mult).then_inc(s.run, 1)
                dve.wait_ge(s.run, 2)
                nc.vector.tensor_tensor(chosen[:], run[:], above[:], ALU.add).then_inc(s.chosen, 1)
                for b in range(B):
                    for k in range(2):
                        dve.wait_ge(s.mask, 2 * b + k + 1)
                        nc.vector.tensor_tensor(hT[:, b, k], hT[:, b, k], g.ps[4 + 2 * b + k][:], ALU.mult
                                                ).then_inc(s.hm, 1)
                for b in range(B):
                    dve.wait_ge(s.out, b + 1)
                    nc.vector.tensor_tensor(g.xT[:, b], g.xT[:, b], g.ps[b][:], ALU.add)


def attn_stage(nc, a, g):
    ln_block(nc, g)
    with ExitStack() as st:
        def sb(name, shape, dt=F32):
            return g.sb("at_" + name, shape, dt, stack=st)

        SCALE = 1.0 / np.sqrt(np.float32(DH))
        PAIRS = NC // 2
        STEPS = B * PAIRS
        UNROLL = 2
        BODY = UNROLL * STEPS
        QT = sb("QT", [P, B, S])
        KT = sb("KT", [P, B, S + 2])
        V = sb("V", [P, B, NC, P])
        kc = sb("kc", [P, 2, B, S])
        prob = sb("prob", [P, 2, S])
        pT = sb("pT", [P, 2, NC, P])
        mx, mb, bias = sb("mx", [P, 2, 2]), sb("mb", [P, 2, 2]), sb("bias", [P, 2, 2])
        sums, rsum = sb("sums", [P, B, NC, H]), sb("rsum", [P, B * NC * H])
        on, oT = sb("on", [P, B, S]), sb("oT", [P, B, S])
        s = g.sem_set("at", "q k v k1 kc0 kc S mx mb bias exp T copy rsum on turned oT o")
        psS = [g.psum[:, 0:2], g.psum[:, 2:4]]
        psT, psO = g.ps[4:6], g.ps[6:8]

        with nc.Block() as block:
            @block.tensor
            def _(pe):
                for b in range(B):
                    nc.tensor.matmul(g.ps[b], g.G("aWq"), g.nT[:, b], start=True, stop=True).then_inc(s.q, 1)
                    nc.tensor.matmul(g.ps[2 + b], g.G("aWk"), g.nT[:, b], start=True, stop=True).then_inc(s.k, 1)
                for b in range(B):
                    for c in range(NC):
                        last = nc.tensor.matmul(g.ps[4 + b][:, c * P:(c + 1) * P], g.nT[:, b, c * P:(c + 1) * P],
                                                g.G("aWv"), start=True, stop=True)
                    last.then_inc(s.v, 1)

            @block.scalar
            def _(act):
                for b in range(B):
                    act.wait_ge(s.q, b + 1)
                    nc.scalar.activation(QT[:, b], g.ps[b], ACT.Identity, bias=g.G("abq"))

            @block.vector
            def _(dve):
                nc.vector.memset(KT[:, :, 0:1], 0.0)
                nc.vector.memset(KT[:, :, S + 1:S + 2], 0.0)
                for b in range(B):
                    dve.wait_ge(s.k, b + 1)
                    nc.vector.tensor_scalar(KT[:, b, 1:S + 1], g.ps[2 + b], g.G("abk"), None, ALU.add
                                            )
                for b in range(B):
                    dve.wait_ge(s.v, b + 1)
                    nc.vector.tensor_tensor(V[:, b], g.ps[4 + b].rearrange("p (c d) -> p c d", d=P),
                                            g.G("abv").unsqueeze(1).broadcast_to([P, NC, P]), ALU.add
                                            )

        def tap(o, t):
            return g.G("conv_w")[:, bass.ds(o * 3 + t, 1)]

        def at_step(k):
            return k % STEPS // PAIRS, k % PAIRS * 2, k % 2

        with nc.Block() as block:
            @block.tensor
            def _(pe):
                def scores(k, c):
                    b, c0, u = at_step(k)
                    nc.tensor.matmul(psS[u][:, c], QT[:, b, (c0 + c) * P:(c0 + c + 1) * P],
                                     kc[:, k % BODY // STEPS, b], start=True, stop=True).then_inc(s.S, 1)

                def body(i, last):
                    for k in range(BODY):
                        b, c0, u = at_step(k)
                        more = not (last and k == BODY - 1)
                        if more and (k + 1) % STEPS == 0:
                            pe.wait_ge(s.kc, i * UNROLL + (k + 1) // STEPS + 1)
                        for c in range(2):
                            if more:
                                scores(k + 1, c)
                            pe.wait_ge(s.exp, i * (2 * BODY) + (2 * k + c + 1))
                            for kt in range(NC):
                                t = nc.tensor.transpose(psT[c][:, kt * P:(kt + 1) * P],
                                                        prob[:, c, kt * P:(kt + 1) * P], g.C("ident"))
                            t.then_inc(s.T, 1)
                        for c in range(2):
                            pe.wait_ge(s.copy, i * (2 * BODY) + (2 * k + c + 1))
                            head = i * (UNROLL * DH) + (k // STEPS * DH)
                            for kt in range(NC):
                                o = nc.tensor.matmul(psO[b][:, bass.ds(head + ((c0 + c) * P), DH)], pT[:, c, kt],
                                                     V[:, b, kt, bass.ds(head, DH)], start=(kt == 0),
                                                     stop=(kt == NC - 1))

                pe.wait_ge(s.kc, 1)
                for c in range(2):
                    scores(0, c)
                with pe.Fori(0, H // UNROLL - 1) as i:
                    body(i, False)
                body(H // UNROLL - 1, True)

            @block.scalar
            def _(act):
                def middle(o, u):
                    nc.scalar.activation(kc[:, u], KT[:, :, 1:S + 1], ACT.Identity, scale=tap(o, 1)
                                         ).then_inc(s.k1, 1)

                def exps(i, k):
                    b, c0, u = at_step(k)
                    act.wait_ge(s.bias, i * BODY + (k + 1))
                    for c in range(2):
                        col = i * UNROLL + ((b * NC + c0 + c) * H + k // STEPS)
                        nc.scalar.activation(prob[:, c], psS[u][:, c], ACT.Exp, bias=bias[:, u, c:c + 1],
                                             scale=float(SCALE),
                                             accum_out=sums[:].rearrange("p b c h -> p (b c h)")[:, bass.ds(col, 1)]
                                             ).then_inc(s.exp, 1)

                def body(i, last):
                    for k in range(BODY):
                        for c in range(2):
                            act.wait_ge(s.T, i * (2 * BODY) + (2 * k + c + 1))
                            nc.scalar.activation(pT[:, c].rearrange("p c q -> p (c q)"), psT[c], ACT.Identity
                                                 ).then_inc(s.copy, 1)
                        if k < BODY - 1:
                            exps(i, k + 1)
                        elif not last:
                            exps_next(i)
                        if k % STEPS == 0 and not (last and k // STEPS == UNROLL - 1):
                            middle(i * UNROLL + (k // STEPS + 1), (k // STEPS + 1) % 2)

                def exps_next(i):
                    act.wait_ge(s.bias, i * BODY + (BODY + 1))
                    for c in range(2):
                        col = i * UNROLL + (c * H + UNROLL)
                        nc.scalar.activation(prob[:, c], psS[0][:, c], ACT.Exp, bias=bias[:, 0, c:c + 1],
                                             scale=float(SCALE),
                                             accum_out=sums[:].rearrange("p b c h -> p (b c h)")[:, bass.ds(col, 1)]
                                             ).then_inc(s.exp, 1)

                middle(0, 0)
                exps(0, 0)
                with act.Fori(0, H // UNROLL - 1) as i:
                    body(i, False)
                body(H // UNROLL - 1, True)

            @block.vector
            def _(dve):
                def outer(o, u, t):
                    if t == 0:
                        dve.wait_ge(s.k1, o + 1)
                    else:
                        dve.wait_ge(s.kc0, o + 1)
                    nc.vector.scalar_tensor_tensor(out=kc[:, u], in0=KT[:, :, t:t + S], scalar=tap(o, t),
                                                   in1=kc[:, u], op0=ALU.mult, op1=ALU.add
                                                   ).then_inc(s.kc if t else s.kc0, 1)

                def maxima(n, u, head):
                    cb = g.G("conv_b")[:, bass.ds(head, 1)]
                    dve.wait_ge(s.S, n * 2 + 2)
                    nc.vector.tensor_reduce(mx[:, u], psS[u], AX.X, ALU.max).then_inc(s.mx, 1)
                    dve.wait_ge(s.mx, n + 1)
                    nc.vector.tensor_scalar(mb[:, u], mx[:, u], float(SCALE), cb, ALU.mult, ALU.add).then_inc(s.mb, 1)
                    dve.wait_ge(s.mb, n + 1)
                    nc.vector.tensor_scalar(bias[:, u], mb[:, u], -1.0, cb, ALU.mult, ALU.add).then_inc(s.bias, 1)

                def body(i, last):
                    for k in range(BODY):
                        if not (last and k == BODY - 1):
                            maxima(i * BODY + (k + 1), (k + 1) % 2, i * UNROLL + ((k + 1) // STEPS))
                        if k % STEPS in (1, 2) and not (last and k // STEPS == UNROLL - 1):
                            outer(i * UNROLL + (k // STEPS + 1), (k // STEPS + 1) % 2, 0 if k % STEPS == 1 else 2)

                outer(0, 0, 0)
                outer(0, 0, 2)
                maxima(0, 0, 0)
                with dve.Fori(0, H // UNROLL - 1) as i:
                    body(i, False)
                body(H // UNROLL - 1, True)

        with nc.Block() as block:
            @block.vector
            def _(dve):
                nc.vector.reciprocal(rsum[:], sums[:].rearrange("p b c h -> p (b c h)")).then_inc(s.rsum, 1)
                dve.wait_ge(s.rsum, 1)
                for b in range(B):
                    nc.vector.tensor_tensor(on[:, b].rearrange("p (n d) -> p n d", d=DH),
                                            psO[b].rearrange("p (n d) -> p n d", d=DH),
                                            rsum[:, b * NC * H:(b + 1) * NC * H].unsqueeze(2
                                                ).broadcast_to([P, NC * H, DH]), ALU.mult).then_inc(s.on, 1)
                for b in range(B):
                    dve.wait_ge(s.o, b + 1)
                    nc.vector.scalar_tensor_tensor(out=g.xT[:, b], in0=g.ps[2 + b], scalar=g.G("abo"), in1=g.xT[:, b],
                                                   op0=ALU.add, op1=ALU.add)

            @block.tensor
            def _(pe):
                for b in range(B):
                    pe.wait_ge(s.on, b + 1)
                    for c in range(NC):
                        last = nc.tensor.transpose(g.ps[b][:, c * P:(c + 1) * P], on[:, b, c * P:(c + 1) * P],
                                                   g.C("ident"))
                    last.then_inc(s.turned, 1)
                for b in range(B):
                    pe.wait_ge(s.oT, b + 1)
                    nc.tensor.matmul(g.ps[2 + b], g.G("aWo"), oT[:, b], start=True, stop=True).then_inc(s.o, 1)

            @block.scalar
            def _(act):
                for b in range(B):
                    act.wait_ge(s.turned, b + 1)
                    nc.scalar.activation(oT[:, b], g.ps[b], ACT.Identity).then_inc(s.oT, 1)


def xattn_stage(nc, a, g):
    ln_block(nc, g)
    with ExitStack() as st:
        def sb(name, shape, dt=F32):
            return g.sb("xa_" + name, shape, dt, stack=st)

        SCALE = 1.0 / np.sqrt(np.float32(P))
        qT, kT, v = sb("qT", [P, B, S]), sb("kT", [P, B * T]), sb("v", [T, B, P])
        mx, bias = sb("mx", [P, B, NC]), sb("bias", [P, B, NC])
        sums, rsum = sb("sums", [P, B, NC]), sb("rsum", [P, B, NC])
        prob, pn, pT = sb("prob", [P, B, NC, T]), sb("pn", [P, B, NC, T]), sb("pT", [T, B, S])
        s = g.sem_set("xa", "k kT v V q qT S mx bias exp rsum pn T pT o")
        with nc.Block() as block:
            @block.tensor
            def _(pe):
                nc.tensor.matmul(g.ps[2][:, 0:B * T], g.G("xWk"), g.G("ctxT"), start=True, stop=True).then_inc(s.k, 1)
                for b in range(B):
                    nc.tensor.matmul(g.ps[b], g.G("xWq"), g.nT[:, b], start=True, stop=True).then_inc(s.q, 1)
                for b in range(B):
                    last = nc.tensor.matmul(g.ps[3][0:T, b * P:(b + 1) * P], g.G("ctxT")[:, b * T:(b + 1) * T],
                                            g.G("xWv"), start=True, stop=True)
                last.then_inc(s.v, 1)
                pe.wait_ge(s.kT, 1)
                for b in range(B):
                    pe.wait_ge(s.qT, b + 1)
                    for c in range(NC):
                        last = nc.tensor.matmul(g.ps[4 + b][:, c * P:c * P + T], qT[:, b, c * P:(c + 1) * P],
                                                kT[:, b * T:(b + 1) * T], start=True, stop=True)
                    last.then_inc(s.S, 1)
                for b in range(B):
                    pe.wait_ge(s.pn, b + 1)
                    for c in range(NC):
                        last = nc.tensor.transpose(g.ps[6 + b][0:T, c * P:(c + 1) * P], pn[:, b, c], g.C("ident"))
                    last.then_inc(s.T, 1)
                pe.wait_ge(s.V, 1)
                for b in range(B):
                    pe.wait_ge(s.pT, b + 1)
                    nc.tensor.matmul(g.ps[b], v[:, b], pT[:, b], start=True, stop=True).then_inc(s.o, 1)

            @block.scalar
            def _(act):
                for b in range(B):
                    act.wait_ge(s.q, b + 1)
                    nc.scalar.activation(qT[:, b], g.ps[b], ACT.Identity, bias=g.G("xbq")).then_inc(s.qT, 1)
                for b in range(B):
                    act.wait_ge(s.bias, b + 1)
                    for c in range(NC):
                        nc.scalar.activation(prob[:, b, c], g.ps[4 + b][:, c * P:c * P + T], ACT.Exp,
                                             bias=bias[:, b, c:c + 1], scale=float(SCALE),
                                             accum_out=sums[:, b, c:c + 1]).then_inc(s.exp, 1)
                for b in range(B):
                    act.wait_ge(s.T, b + 1)
                    nc.scalar.activation(pT[:, b], g.ps[6 + b][0:T, :], ACT.Identity).then_inc(s.pT, 1)

            @block.vector
            def _(dve):
                dve.wait_ge(s.k, 1)
                nc.vector.tensor_scalar(kT[:], g.ps[2][:, 0:B * T], g.G("xbk"), None, ALU.add).then_inc(s.kT, 1)
                dve.wait_ge(s.v, 1)
                nc.vector.tensor_tensor(v[:], g.ps[3][0:T, 0:B * P].rearrange("p (b d) -> p b d", d=P),
                                        g.G("xbv")[0:T].unsqueeze(1).broadcast_to([T, B, P]), ALU.add).then_inc(s.V, 1)
                for b in range(B):
                    dve.wait_ge(s.S, b + 1)
                    nc.vector.tensor_reduce(mx[:, b], g.ps[4 + b].rearrange("p (c k) -> p c k", k=P)[:, :, 0:T], AX.X,
                                            ALU.max).then_inc(s.mx, 1)
                    dve.wait_ge(s.mx, b + 1)
                    nc.vector.tensor_scalar(bias[:, b], mx[:, b], -float(SCALE), None, ALU.mult).then_inc(s.bias, 1)
                for b in range(B):
                    dve.wait_ge(s.exp, NC * (b + 1))
                    nc.vector.reciprocal(rsum[:, b], sums[:, b]).then_inc(s.rsum, 1)
                    dve.wait_ge(s.rsum, b + 1)
                    nc.vector.tensor_tensor(pn[:, b], prob[:, b], rsum[:, b].unsqueeze(2).broadcast_to([P, NC, T]),
                                            ALU.mult).then_inc(s.pn, 1)
                for b in range(B):
                    dve.wait_ge(s.o, b + 1)
                    nc.vector.tensor_tensor(g.xT[:, b], g.xT[:, b], g.ps[b], ALU.add)


def ffn_stage(nc, a, g):
    ln_block(nc, g)
    with ExitStack() as st:
        def sb(name, shape, dt=F32):
            return g.sb("ff_" + name, shape, dt, stack=st)

        MAGIC = 1.5 * 2.0 ** 23
        TURN1 = 6.28125
        TURN2 = round((2 * np.pi - TURN1) * 2 ** 21) / 2 ** 21
        TURN3 = 2 * np.pi - TURN1 - TURN2
        LIMIT = float(np.nextafter(np.float32(np.pi), np.float32(0)))
        arg, turns = sb("arg", [P, 2, NF]), sb("turns", [P, 2, NF])
        sc = sb("sincos", [P, 2, NF])
        coef = sb("coef", [P, NF])
        hid, ang = sb("hid", [P, B, NF, S]), sb("ang", [P, B, NF, S])
        n = sb("n", [P, B, NF, S])
        s = g.sem_set("ff", "h hid ang n red sin q relu f arg t args sc m1 m2 coef")

        def reduce_turns(dve, x, n_, sg, at, done):
            nc.vector.tensor_scalar(n_, x, 1.0 / (2 * np.pi), MAGIC, ALU.mult, ALU.add).then_inc(sg, 1)
            dve.wait_ge(sg, at + 1)
            nc.vector.tensor_scalar(n_, n_, MAGIC, None, ALU.subtract).then_inc(sg, 1)
            dve.wait_ge(sg, at + 2)
            for j, part in enumerate((TURN1, TURN2, TURN3)):
                nc.vector.scalar_tensor_tensor(out=x, in0=n_, scalar=-float(part), in1=x, op0=ALU.mult, op1=ALU.add
                                               ).then_inc(sg, 1)
                dve.wait_ge(sg, at + 3 + j)
            nc.vector.tensor_scalar(x, x, LIMIT, -LIMIT, ALU.min, ALU.max).then_inc(done, 1)

        with nc.Block() as block:
            @block.tensor
            def _(pe):
                for b in range(B):
                    for f in range(NF):
                        nc.tensor.matmul(g.ps[b * NF + f], g.G("fW1")[:, f * P:(f + 1) * P], g.nT[:, b],
                                         start=True, stop=True).then_inc(s.h, 1)
                for b in range(B):
                    for f in range(NF):
                        pe.wait_ge(s.relu, b * NF + f + 1)
                        last = nc.tensor.matmul(g.ps[b * NF], g.G("fW2")[:, f * P:(f + 1) * P], n[:, b, f],
                                                start=(f == 0), stop=(f == NF - 1))
                    last.then_inc(s.f, 1)

            @block.scalar
            def _(act):
                for b in range(B):
                    for f in range(NF):
                        act.wait_ge(s.h, b * NF + f + 1)
                        nc.scalar.activation(hid[:, b, f], g.ps[b * NF + f], ACT.Identity, bias=g.G("fb1")[:, f:f + 1]
                                             ).then_inc(s.hid, 1)
                nc.scalar.preload_act_table(ACT.Sin)
                act.wait_ge(s.args, 2)
                nc.scalar.activation(sc[:], arg[:], ACT.Sin).then_inc(s.sc, 1)
                for b in range(B):
                    for f in range(NF):
                        act.wait_ge(s.red, b * NF + f + 1)
                        nc.scalar.activation(ang[:, b, f], ang[:, b, f], ACT.Sin).then_inc(s.sin, 1)
                nc.scalar.preload_act_table(ACT.Relu)
                for b in range(B):
                    for f in range(NF):
                        act.wait_ge(s.q, b * NF + f + 1)
                        nc.scalar.activation(n[:, b, f], hid[:, b, f], ACT.Relu).then_inc(s.relu, 1)

            @block.vector
            def _(dve):
                theta = g.G("ph")
                nc.vector.tensor_copy(arg[:, 0], theta).then_inc(s.arg, 1)
                dve.wait_ge(s.arg, 1)
                reduce_turns(dve, arg[:, 0], turns[:, 0], s.t, 0, s.args)
                dve.wait_ge(s.args, 1)
                nc.vector.tensor_scalar(arg[:, 1], arg[:, 0], np.pi / 2, None, ALU.add).then_inc(s.arg, 1)
                dve.wait_ge(s.arg, 2)
                reduce_turns(dve, arg[:, 1], turns[:, 1], s.t, 5, s.args)
                dve.wait_ge(s.sc, 1)
                nc.vector.tensor_tensor(sc[:, 1], sc[:, 1], g.G("wr"), ALU.mult)
                nc.vector.tensor_tensor(sc[:, 0], sc[:, 0], g.G("wi"), ALU.mult).then_inc(s.m1, 1)
                dve.wait_ge(s.m1, 1)
                nc.vector.tensor_tensor(coef[:], sc[:, 0], sc[:, 1], ALU.add).then_inc(s.m2, 1)
                dve.wait_ge(s.m2, 1)
                nc.vector.scalar_tensor_tensor(out=coef[:], in0=coef[:], scalar=0.1, in1=g.G("wi"), op0=ALU.mult,
                                               op1=ALU.mult).then_inc(s.coef, 1)
                for b in range(B):
                    for f in range(NF):
                        k = b * NF + f
                        dve.wait_ge(s.hid, k + 1)
                        nc.vector.tensor_scalar(ang[:, b, f], hid[:, b, f], 0.1, theta[:, f:f + 1], ALU.mult, ALU.add
                                                ).then_inc(s.ang, 1)
                        dve.wait_ge(s.ang, k + 1)
                        reduce_turns(dve, ang[:, b, f], n[:, b, f], s.n, 5 * k, s.red)
                dve.wait_ge(s.coef, 1)
                for b in range(B):
                    for f in range(NF):
                        dve.wait_ge(s.sin, b * NF + f + 1)
                        nc.vector.scalar_tensor_tensor(out=hid[:, b, f], in0=ang[:, b, f], scalar=coef[:, f:f + 1],
                                                       in1=hid[:, b, f], op0=ALU.mult, op1=ALU.add).then_inc(s.q, 1)
                for b in range(B):
                    dve.wait_ge(s.f, b + 1)
                    nc.vector.scalar_tensor_tensor(out=g.xT[:, b], in0=g.ps[b * NF], scalar=g.G("fb2"), in1=g.xT[:, b],
                                                   op0=ALU.add, op1=ALU.add)


def store_stage(nc, a, g):
    with ExitStack() as st:
        rows = g.sb("out_rows", [P, B * NC, P], stack=st)
        s = g.sem_set("store", "turned rows out")
        with nc.Block() as block:
            @block.tensor
            def _(pe):
                for b in range(B):
                    for c in range(NC):
                        last = nc.tensor.transpose(g.ps[b][:, c * P:(c + 1) * P], g.xT[:, b, c * P:(c + 1) * P],
                                                   g.C("ident"))
                    last.then_inc(s.turned, 1)

            @block.vector
            def _(dve):
                for b in range(B):
                    dve.wait_ge(s.turned, b + 1)
                    nc.vector.tensor_copy(rows[:, b * NC:(b + 1) * NC, :].rearrange("p c d -> p (c d)"), g.ps[b][:]
                                          ).then_inc(s.rows, 1)

            @block.sync
            def _(sp):
                for b in range(B):
                    sp.wait_ge(s.rows, b + 1)
                    sp.dma_start(a["out"][b].rearrange("(c p) d -> p c d", p=P), rows[:, b * NC:(b + 1) * NC, :]
                                 ).then_inc(s.out, 16)
                sp.wait_ge(s.out, 16 * B)


def layout(i):
    f = {k: np.asarray(v) for k, v in i.items()}
    parts = []
    for n in L0_COLS:
        v = {"Wq": "Wq", "Wk": "Wk", "Wv": "Wv", "Wo": "Wo", "Wf1": "Wf1", "Wf2": "Wf2", "s1": "ln1_s", "b1": "ln1_b",
             "s2": "ln2_s", "b2": "ln2_b"}.get(n, n)
        w = f["L0_attn_" + v]
        if n == "Wf2":
            w = w.reshape(LAYERS, NF, P, P).transpose(0, 2, 1, 3).reshape(LAYERS, P, FF)
        elif n == "bf1":
            w = w.reshape(LAYERS, NF, P).transpose(0, 2, 1)
        elif w.ndim == 2:
            w = w[:, :, None]
        parts.append(w)
    l0 = np.ascontiguousarray(np.concatenate(parts, axis=2))
    row = lambda v: np.broadcast_to(v[None, :], (P, v.shape[0]))
    col = lambda v: v.reshape(-1, P).T
    b2 = np.zeros((P, P), f["L0_ffn_b2"].dtype)
    b2[0:64:8] = f["L0_ffn_b2"]
    b2[64:128:8] = f["L0_ffn_b2"]
    cols = {
        "ctxT": f["ctx_1024"].transpose(2, 0, 1).reshape(P, B * T),
        "wg": f["L0_ffn_w_gate_w"], "bg": row(f["L0_ffn_w_gate_b"]),
        "W1": f["L0_ffn_W1"].transpose(1, 0, 2).reshape(P, E * HID),
        "W2": f["L0_ffn_W2"].reshape(2, P, P).transpose(1, 0, 2).reshape(P, 2 * P),
        "b1": col(f["L0_ffn_b1"].reshape(-1)), "b2": b2,
        "aWq": f["L1_attn_Wq"].T, "aWk": f["L1_attn_Wk"].T, "aWv": f["L1_attn_Wv"].T, "aWo": f["L1_attn_Wo"].T,
        "abq": col(f["L1_attn_bq"]), "abk": col(f["L1_attn_bk"]), "abv": row(f["L1_attn_bv"]),
        "abo": col(f["L1_attn_bo"]),
        "conv_w": np.repeat(f["L1_attn_conv_w"].transpose(1, 0, 2).reshape(H, 3 * H), DH, axis=0),
        "conv_b": row(f["L1_attn_conv_b"]),
        "xWq": f["L1_xattn_Wq"].T, "xWk": f["L1_xattn_Wk"].T, "xWv": f["L1_xattn_Wv"].T,
        "xbq": col(f["L1_xattn_bq"]), "xbk": col(f["L1_xattn_bk"]), "xbv": row(f["L1_xattn_bv"]),
        "fW1": f["L1_ffn_W1"], "fW2": f["L1_ffn_W2"].reshape(NF, P, P).transpose(1, 0, 2).reshape(P, FF),
        "fb1": col(f["L1_ffn_b1"]), "ph": col(f["L1_ffn_quantum_phases"]), "wr": col(f["L1_ffn_quantum_weights_real"]),
        "wi": col(f["L1_ffn_quantum_weights_imag"]), "fb2": col(f["L1_ffn_b2"]),
    }
    params = np.ascontiguousarray(np.concatenate([cols[n] for n in G_AT], axis=1))
    assert params.shape == (P, G_N) and l0.shape == (LAYERS, P, L0_N)
    return {"x": f["x"], "ctx": f["ctx_1024"], "l0": l0, "params": params, "consts": constants()}


def kernel(**inputs):
    import concourse.bacc as bacc
    from concourse.bass_utils import run_bass_kernel_spmd

    nc = bacc.Bacc("TRN2", target_bir_lowering=False, num_devices=1)
    arrays = layout(inputs)
    a = {n: nc.dram_tensor("in_" + n, v.shape, mybir.dt.from_np(v.dtype), kind="ExternalInput").ap()
         for n, v in arrays.items()}
    a["out"] = nc.dram_tensor("out", (B, S, P), F32, kind="ExternalOutput").ap()
    build(nc, a)
    r = run_bass_kernel_spmd(nc, [{"in_" + n: v for n, v in arrays.items()}], core_ids=[0])
    return r.results[0]["out"]
```

```python
from collections import namedtuple
from contextlib import ExitStack

import numpy as np

import concourse.bass as bass
from concourse import mybir

P = 128
B = 2
S = 512
NC = S // P
T = 77
LAYERS = 8
FF = 512
NF = FF // P
E = 8
HID = 32
TOPK = 2
CAP = B
KEEP = S // 2
H = 16
DH = P // H
BLK = 16
W = S // BLK
LAG = 2
SLOTS = T + LAG * (BLK - 1)
PAD = LAG * (BLK - 1)
BIG = 1e30
SHIFTS = [28, 25, 22, 19, 16, 13, 10, 7, 4, 1, 0]

F32 = mybir.dt.float32
I32 = mybir.dt.int32
BF16 = mybir.dt.bfloat16
ALU = mybir.AluOpType
ACT = mybir.ActivationFunctionType
AX = mybir.AxisListType

LOWEST = [7.0 if s == 0 else 1.0 for s in SHIFTS]

L0_COLS = ["Wq", "Wk", "Wv", "Wo", "Wf1", "Wf2", "bq", "bk", "bv", "bo", "s1", "b1", "bf2", "s2", "b2", "bf1"]
L0_WIDTH = dict(Wq=P, Wk=P, Wv=P, Wo=P, Wf1=FF, Wf2=FF, bf1=NF)


def columns(names, width):
    at, out = 0, {}
    for n in names:
        w = width.get(n, 1)
        out[n] = (at, at + w)
        at += w
    return out, at


L0_AT, L0_N = columns(L0_COLS, L0_WIDTH)
C_WIDTH = dict(row_ok=SLOTS - T, ident=P, cent=P, mean=P, one=P, shift_r=32, shift_l=32, block8=P, kk=len(SHIFTS), pick=2 * P,
               lower=E * E)
C_AT, C_N = columns(["ident", "cent", "mean", "one", "shift_r", "shift_l", "big_first", "init0", "bnd_last", "row_ok", "block8",
                     "kk", "pick", "lower"], C_WIDTH)
G_WIDTH = dict(ctxT=B * T, wg=E, bg=E, W1=E * HID, W2=2 * P, b1=2, b2=P, aWq=P, aWk=P, aWv=P, aWo=P, abv=P,
               conv_w=3 * H, conv_b=H, xWq=P, xWk=P, xWv=P, xbv=P, fW1=FF, fW2=FF, fb1=NF, ph=NF, wr=NF, wi=NF)
G_AT, G_N = columns(["ctxT", "wg", "bg", "W1", "W2", "b1", "b2", "aWq", "aWk", "aWv", "aWo", "abq", "abk", "abv",
                     "abo", "conv_w", "conv_b", "xWq", "xWk", "xWv", "xbq", "xbk", "xbv", "fW1", "fW2", "fb1", "ph",
                     "wr", "wi", "fb2"], G_WIDTH)


def constants():
    c = np.zeros((P, C_N), np.float32)

    def put(name, a):
        lo, hi = C_AT[name]
        c[:a.shape[0], lo:hi] = a

    put("ident", np.eye(P))
    put("cent", np.eye(P) - 1.0 / P)
    put("mean", np.full((P, P), 1.0 / P))
    put("one", np.ones((P, P)))
    r, l = np.zeros((32, 32)), np.zeros((32, 32))
    big, init0, last = np.zeros((32, 1)), np.full((32, 1), BIG), np.ones((32, 1))
    for b in range(B):
        for k in range(BLK):
            p = b * BLK + BLK - 1 - k
            if k + 1 < BLK:
                r[p, p - 1] = 1
                l[p - 1, p] = 1
        big[b * BLK + BLK - 1] = BIG
        init0[b * BLK + BLK - 1] = 0
        last[b * BLK] = 0
    put("shift_r", r)
    put("shift_l", l)
    put("big_first", big)
    put("init0", init0)
    put("bnd_last", last)
    ok = np.zeros((32, SLOTS - T))
    for p in range(32):
        k = BLK - 1 - p % BLK
        ok[p] = np.arange(T, SLOTS) - LAG * k < T
    put("row_ok", ok)
    put("block8", np.kron(np.eye(P // 8), np.ones((8, 8))))
    kk = np.array([[(p % 8) << s if s or p % 8 < 2 else 0 for s in SHIFTS] for p in range(P)], np.int32)
    put("kk", kk.view(np.float32))
    pick = np.zeros((P, 2, P))
    for b in range(B):
        for e in range(E):
            pick[b * 64 + e * 8, e // 4, (e % 4) * HID:(e % 4 + 1) * HID] = 1
    put("pick", pick.reshape(P, 2 * P))
    put("lower", np.broadcast_to(np.tril(np.ones((E, E)), -1).reshape(1, E * E), (P, E * E)))
    return c


class Shared:
    pass


def build(nc, a):
    with ExitStack() as ctx:
        sems = {}

        def sem(name):
            assert name not in sems
            sems[name] = ctx.enter_context(nc.semaphore(name))
            return sems[name]

        def sem_set(prefix, names):
            return namedtuple("Semaphores", names)(*(sem(f"{prefix}_{n}") for n in names.split()))

        def sb(name, shape, dt=F32, stack=ctx):
            return stack.enter_context(nc.sbuf_tensor(name, shape, dt))

        g = Shared()
        g.c = sb("consts", [P, C_N])
        g.w = sb("params", [P, G_N])
        g.xT = sb("xT", [P, B, S])
        g.nT = sb("nT", [P, B, S])
        g.ctx = sb("ctx", [T, B, P])
        g.eps6 = sb("eps6", [P, 1])
        g.eps5 = sb("eps5", [P, 1])
        g.sq = sb("sq", [P, B, S])
        g.rs = sb("rs", [P, B, S])
        g.psum = ctx.enter_context(nc.psum_tensor("banks", [P, 8, 512], F32))
        g.ps = [g.psum[:, i] for i in range(8)]
        g.sem, g.sem_set, g.sb = sem, sem_set, sb
        g.C = lambda n: g.c[:, C_AT[n][0]:C_AT[n][1]]
        g.G = lambda n: g.w[:, G_AT[n][0]:G_AT[n][1]]
        g.loaded = sem("params_loaded")
        g.ln, g.norms = sem_set("ln", LN_SEMS), 0
        load_stage(nc, a, g)
        l0_stage(nc, a, g)
        if STAGES >= 2:
            dtw_stage(nc, a, g)
        if STAGES >= 3:
            moe_stage(nc, a, g)
        if STAGES >= 4:
            attn_stage(nc, a, g)
        if STAGES >= 5:
            xattn_stage(nc, a, g)
        if STAGES >= 6:
            ffn_stage(nc, a, g)
        store_stage(nc, a, g)


STAGES = 6


def ln_pe(nc, pe, g, s, n, src, bank_c, bank_v, sq):
    nc.tensor.matmul(bank_c[:], g.C("cent"), src, start=True, stop=True).then_inc(s.cen, 1)
    pe.wait_ge(s.sq, n)
    nc.tensor.matmul(bank_v[:], g.C("mean"), sq, start=True, stop=True).then_inc(s.var, 1)


def ln_act_square(nc, act, g, s, n, bank_c, sq):
    act.wait_ge(s.cen, n)
    nc.scalar.activation(sq, bank_c[:], ACT.Square).then_inc(s.sq, 1)


def ln_act_rstd(nc, act, g, s, n, bank_v, sq, rs, eps):
    act.wait_ge(s.var, n)
    nc.scalar.activation(sq, bank_v[:], ACT.Ln, bias=eps[:]).then_inc(s.ln, 1)
    act.wait_ge(s.ln, n)
    nc.scalar.activation(rs, sq, ACT.Exp, scale=-0.5).then_inc(s.rs, 1)


LN_SET = "natural_log_exp_and_others"
LN_SEMS = "cen sq var ln rs"


def ln_block(nc, g, dve_first=None):
    s, n0 = g.ln, g.norms * B
    g.norms += 1
    with nc.Block() as block:
        @block.tensor
        def _(pe):
            for b in range(B):
                nc.tensor.matmul(g.ps[b], g.C("cent"), g.xT[:, b], start=True, stop=True).then_inc(s.cen, 1)
            for b in range(B):
                pe.wait_ge(s.sq, n0 + b + 1)
                nc.tensor.matmul(g.ps[2 + b], g.C("mean"), g.sq[:, b], start=True, stop=True).then_inc(s.var, 1)

        @block.scalar
        def _(act):
            nc.scalar.preload_act_table_set(LN_SET)
            for b in range(B):
                ln_act_square(nc, act, g, s, n0 + b + 1, g.ps[b], g.sq[:, b])
            for b in range(B):
                ln_act_rstd(nc, act, g, s, n0 + b + 1, g.ps[2 + b], g.sq[:, b], g.rs[:, b], g.eps5)

        @block.vector
        def _(dve):
            if dve_first:
                dve_first(dve)
            for b in range(B):
                dve.wait_ge(s.rs, n0 + b + 1)
                nc.vector.tensor_tensor(g.nT[:, b], g.ps[b], g.rs[:, b], ALU.mult)


def load_stage(nc, a, g):
    with ExitStack() as st:
        xn = g.sb("x_rows", [P, B * NC, P], stack=st)
        s = g.sem_set("load", "x consts ctx turned")
        g.ctx_loaded = s.ctx
        with nc.Block() as block:
            @block.sync
            def _(sp):
                sp.dma_start(xn[:], a["x"].rearrange("b (c p) d -> p (b c) d", p=P)).then_inc(s.x, 16)
                sp.dma_start(g.w[:], a["params"]).then_inc(g.loaded, 16)
                sp.dma_start(g.ctx[:], a["ctx"].rearrange("b t d -> t b d")).then_inc(s.ctx, 16)

            @block.scalar
            def _(act):
                act.dma_start(g.c[:], a["consts"]).then_inc(s.consts, 16)

            @block.tensor
            def _(pe):
                pe.wait_ge(s.x, 16)
                pe.wait_ge(s.consts, 16)
                for b in range(B):
                    for c in range(NC):
                        last = nc.tensor.transpose(g.ps[b][:, c * P:(c + 1) * P], xn[:, b * NC + c, :], g.C("ident"))
                    last.then_inc(s.turned, 1)

            @block.vector
            def _(dve):
                nc.vector.memset(g.eps6[:], 1e-6)
                nc.vector.memset(g.eps5[:], 1e-5)
                for b in range(B):
                    dve.wait_ge(s.turned, b + 1)
                    nc.vector.tensor_copy(g.xT[:, b], g.ps[b][:])
    ln_block(nc, g)


def l0_stage(nc, a, g):
    with ExitStack() as st:
        def sb(name, shape, dt=F32):
            return g.sb("l0_" + name, shape, dt, stack=st)

        LOOP = 2 * 2
        wt = sb("wt", [P, 2, L0_N])
        x = sb("x", [P, B, S])
        x1 = sb("x1", [P, B, S])
        eq, rq, ek, rk = (sb(n, [P, S]) for n in ("eq", "rq", "ek", "rk"))
        Q, K, V, den, rec, junk = (sb(n, [P, S]) for n in ("Q", "K", "V", "den", "rec", "junk"))
        go, r1, gf, r2, u1, u2 = (sb(n, [P, S]) for n in ("go", "r1", "gf", "r2", "u1", "u2"))
        h = sb("h", [P, NF, S])
        ksum, kv = sb("ksum", [P, 1]), sb("kv", [P, 1])
        s = g.sem_set("l0", "w0 w1 q k v eq ek mq mk Q K kv den rec V o go r1 h1 hg f2 gf r2 x u1 x1 u2")
        nA, nF = g.sem_set("l0a", LN_SEMS), g.sem_set("l0f", LN_SEMS)
        bQ, bK, bV, bF = g.ps[0], g.ps[1], g.ps[2], g.ps[7]
        bH = g.ps[3:7]
        bO = bQ
        cA, vA, cF, vF = bH
        sqA, sqF, rsA, rsF = g.sq[:, 0], g.sq[:, 1], g.rs[:, 0], g.rs[:, 1]

        def slots(j):
            return j // 2 % 2, (j - 1) // 2 % 2

        def wcol(u, n):
            return wt[:, u, L0_AT[n][0]:L0_AT[n][1]]

        def halves(eng, half):
            half(0, 0, True, False)
            with eng.Fori(0, LAYERS // 2 - 1) as i:
                for j in range(1, LOOP + 1):
                    half(i * LOOP, j, True, True)
            for j in range(1, LOOP + 1):
                half((LAYERS // 2 - 1) * LOOP, j, j < LOOP, True)

        with nc.Block() as block:
            @block.sync
            def _(sp):
                for l in range(2):
                    sp.dma_start(wt[:, l], a["l0"][l]).then_inc((s.w0, s.w1)[l], 16)
                with sp.Fori(0, LAYERS // 2 - 1) as i:
                    for l in range(2):
                        sp.wait_ge(s.x, i * LOOP + (LOOP + 2 * l))
                        sp.dma_start(wt[:, l], a["l0"][bass.ds(i * 2 + (l + 2), 1)].rearrange("o p n -> p (o n)")
                                     ).then_inc((s.w0, s.w1)[l], 16)
                sp.wait_ge(g.ctx_loaded, 16)
                sp.wait_ge(g.loaded, 16)

            @block.tensor
            def _(pe):
                def half(i, j, A, F):
                    ua, uf = slots(j)
                    if A:
                        if j % 2 == 0:
                            pe.wait_ge((s.w0, s.w1)[ua], i * (16 // LOOP) + (16 * (j // 4 + 1)))
                        pe.wait_ge(s.x, i + (j + 1))
                        xa = x[:, j % 2]
                        nc.tensor.matmul(bK, wcol(ua, "Wk"), xa, start=True, stop=True).then_inc(s.k, 1)
                        nc.tensor.matmul(bQ, wcol(ua, "Wq"), xa, start=True, stop=True).then_inc(s.q, 1)
                        nc.tensor.matmul(bV, wcol(ua, "Wv"), xa, start=True, stop=True).then_inc(s.v, 1)
                    if F:
                        pe.wait_ge(s.x1, i + j)
                        pe.wait_ge(s.x, i + (j + 1))
                        for f in range(NF):
                            nc.tensor.matmul(bH[f], wcol(uf, "Wf1")[:, f * P:(f + 1) * P], x1[:, (j + 1) % 2],
                                             start=True, stop=True).then_inc(s.h1, 1)
                    for f in range(NF):
                        if F:
                            pe.wait_ge(s.hg, i * NF + (NF * (j - 1) + f + 1))
                            last = nc.tensor.matmul(bF, wcol(uf, "Wf2")[:, f * P:(f + 1) * P], h[:, f],
                                                    start=(f == 0), stop=(f == NF - 1))
                    if F:
                        last.then_inc(s.f2, 1)
                    if A:
                        pe.wait_ge(s.V, i + (j + 1))
                        nc.tensor.matmul(bO, wcol(ua, "Wo"), V[:], start=True, stop=True).then_inc(s.o, 1)
                    if F:
                        pe.wait_ge(s.r2, i + j)
                        nc.tensor.matmul(cF, g.C("cent"), r2[:], start=True, stop=True).then_inc(nF.cen, 1)
                    if F:
                        pe.wait_ge(nF.sq, i + j)
                        nc.tensor.matmul(vF, g.C("mean"), sqF, start=True, stop=True).then_inc(nF.var, 1)
                    if A:
                        pe.wait_ge(s.r1, i + (j + 1))
                        nc.tensor.matmul(cA, g.C("cent"), r1[:], start=True, stop=True).then_inc(nA.cen, 1)
                    if A:
                        pe.wait_ge(nA.sq, i + (j + 1))
                        nc.tensor.matmul(vA, g.C("mean"), sqA, start=True, stop=True).then_inc(nA.var, 1)

                halves(pe, half)

            @block.scalar
            def _(act):
                def half(i, j, A, F):
                    ua, uf = slots(j)
                    if A:
                        for src, sg, e_, r_, bias, out in ((bK, s.k, ek, rk, "bk", s.ek), (bQ, s.q, eq, rq, "bq", s.eq)):
                            act.wait_ge(sg, i + (j + 1))
                            nc.scalar.activation(e_[:], src, ACT.Exp, bias=wcol(ua, bias))
                            nc.scalar.activation(r_[:], src, ACT.Relu, bias=wcol(ua, bias)).then_inc(out, 1)
                    nc.scalar.preload_act_table(ACT.Gelu_apprx_tanh)
                    if F:
                        for f in range(NF):
                            act.wait_ge(s.h1, i * NF + (NF * (j - 1) + f + 1))
                            nc.scalar.activation(h[:, f], bH[f], ACT.Gelu_apprx_tanh, bias=wcol(uf, "bf1")[:, f:f + 1]
                                                 ).then_inc(s.hg, 1)
                        act.wait_ge(s.f2, i + j)
                        nc.scalar.activation(gf[:], bF, ACT.Gelu_apprx_tanh, bias=wcol(uf, "bf2")).then_inc(s.gf, 1)
                    if A:
                        act.wait_ge(s.o, i + (j + 1))
                        nc.scalar.activation(go[:], bO, ACT.Gelu_apprx_tanh, bias=wcol(ua, "bo")).then_inc(s.go, 1)
                    if F:
                        ln_act_square(nc, act, g, nF, i + j, cF, sqF)
                    nc.scalar.preload_act_table_set(LN_SET)
                    if F:
                        ln_act_rstd(nc, act, g, nF, i + j, vF, sqF, rsF, g.eps6)
                    if A:
                        ln_act_square(nc, act, g, nA, i + (j + 1), cA, sqA)
                        ln_act_rstd(nc, act, g, nA, i + (j + 1), vA, sqA, rsA, g.eps6)

                nc.scalar.preload_act_table_set(LN_SET)
                halves(act, half)

            @block.vector
            def _(dve):
                def half(i, j, A, F):
                    ua, uf = slots(j)
                    if A:
                        n = i + (j + 1)
                        dve.wait_ge(s.ek, n)
                        nc.vector.tensor_scalar(ek[:], ek[:], 1.0, -1.0, ALU.min, ALU.add).then_inc(s.mk, 1)
                        dve.wait_ge(s.mk, n)
                        nc.vector.scalar_tensor_tensor(out=K[:], in0=ek[:], scalar=1.0, in1=rk[:], op0=ALU.add,
                                                       op1=ALU.add, accum_out=ksum[:]).then_inc(s.K, 1)
                        dve.wait_ge(s.eq, n)
                        nc.vector.tensor_scalar(eq[:], eq[:], 1.0, -1.0, ALU.min, ALU.add).then_inc(s.mq, 1)
                        dve.wait_ge(s.mq, n)
                        nc.vector.scalar_tensor_tensor(out=Q[:], in0=eq[:], scalar=1.0, in1=rq[:], op0=ALU.add,
                                                       op1=ALU.add).then_inc(s.Q, 1)
                        dve.wait_ge(s.Q, n)
                        dve.wait_ge(s.K, n)
                        nc.vector.tensor_scalar(den[:], Q[:], ksum[:], 1e-6, ALU.mult, ALU.add).then_inc(s.den, 1)
                        dve.wait_ge(s.v, n)
                        dve.wait_ge(s.K, n)
                        nc.vector.scalar_tensor_tensor(out=junk[:], in0=bV, scalar=wcol(ua, "bv"), in1=K[:],
                                                       op0=ALU.add, op1=ALU.mult, accum_out=kv[:]).then_inc(s.kv, 1)
                        dve.wait_ge(s.den, n)
                        nc.vector.reciprocal(rec[:], den[:]).then_inc(s.rec, 1)
                        dve.wait_ge(s.rec, n)
                        dve.wait_ge(s.kv, n)
                        nc.vector.scalar_tensor_tensor(out=V[:], in0=Q[:], scalar=kv[:], in1=rec[:], op0=ALU.mult,
                                                       op1=ALU.mult).then_inc(s.V, 1)
                    if F:
                        dve.wait_ge(s.gf, i + j)
                        nc.vector.tensor_tensor(r2[:], gf[:], x1[:, (j + 1) % 2], ALU.add).then_inc(s.r2, 1)
                    if A:
                        dve.wait_ge(s.go, i + (j + 1))
                        nc.vector.tensor_tensor(r1[:], go[:], x[:, j % 2], ALU.add).then_inc(s.r1, 1)
                    if F:
                        dve.wait_ge(nF.rs, i + j)
                        nc.vector.tensor_tensor(u2[:], cF, rsF, ALU.mult).then_inc(s.u2, 1)
                        dve.wait_ge(s.u2, i + j)
                        nc.vector.tensor_scalar(x[:, (j + 1) % 2], u2[:], wcol(uf, "s2"), wcol(uf, "b2"), ALU.mult,
                                                ALU.add).then_inc(s.x, 1)
                    if A:
                        dve.wait_ge(nA.rs, i + (j + 1))
                        nc.vector.tensor_tensor(u1[:], cA, rsA, ALU.mult).then_inc(s.u1, 1)
                        dve.wait_ge(s.u1, i + (j + 1))
                        nc.vector.tensor_scalar(x1[:, j % 2], u1[:], wcol(ua, "s1"), wcol(ua, "b1"), ALU.mult,
                                                ALU.add).then_inc(s.x1, 1)

                for b in range(B):
                    nc.vector.tensor_copy(x[:, b], g.nT[:, b]).then_inc(s.x, 1)
                halves(dve, half)
                dve.wait_ge(s.x, 2 * LAYERS + B)
                for b in range(B):
                    nc.vector.tensor_tensor(g.xT[:, b], g.xT[:, b], x[:, b], ALU.add)


def dtw_stage(nc, a, g):
    ln_block(nc, g)
    with ExitStack() as st:
        def sb(name, shape, dt=F32):
            return g.sb("dtw_" + name, shape, dt, stack=st)

        rows = T + 2 * PAD
        scr_d = [nc.dram_tensor(f"scratch_dist{b}", (rows, S), F32, kind="Internal").ap() for b in range(B)]
        scr_p = [nc.dram_tensor(f"scratch_path{b}", (rows, S), F32, kind="Internal").ap() for b in range(B)]
        ctx2 = sb("ctx2", [P, B * T])
        nsq = sb("nsq", [P, B, S])
        junk, aa = sb("junk", [T, P]), sb("aa", [T, B])
        d2, dist = sb("d2", [T, B, S]), sb("dist", [T, B, S])
        zero = sb("zero", [PAD, S])
        D = sb("D", [32, SLOTS, W])
        R = sb("R", [32, SLOTS + 1, W + 1])
        q = sb("q", [32, SLOTS, W])
        isq, isn, nu = (sb(n, [32, SLOTS, W], BF16) for n in ("diag_le_up", "not_left", "up_less_1"))
        dg = sb("diag", [32, SLOTS, W + 1], BF16)
        theta = sb("theta", [32, SLOTS, W], BF16)
        I = sb("I", [32, SLOTS + 1, W + 1], BF16)
        X = sb("X", [32, SLOTS, W], BF16)
        t1, t2, t3 = isq, isn, nu
        path = sb("path", [32, SLOTS, W])
        shl = sb("shift_l", [32, 32], BF16)
        pn = sb("path_rows", [T, B, S])
        s = g.sem_set("dtw", "nsq ctx2 aa dd d2 dist zero stored D0 D1 q R edge Redge big isq isn dg nu dgs dge theta "
                             "X I Iedge t1 t2 t3 P pst pn ex")
        CH = 4
        NCH = -(-SLOTS // CH)
        PIECES = [(0, 20), (20, SLOTS)]
        STORES = [(13, NCH), (3, 13), (0, 3)]

        def span(c):
            return c * CH, min((c + 1) * CH, SLOTS)

        def skewed(scr, lo, hi):
            return bass.AP(tensor=scr.tensor, offset=scr.offset + W * (BLK - 1) + S * lo,
                           ap=[[LAG * S - W, BLK], [S, hi - lo], [1, W]])

        psR, psI, psD = g.ps[0:2], g.ps[5:7], g.ps[3:5]
        psG = psI

        with nc.Block() as block:
            @block.scalar
            def _(act):
                def diag_edge(c):
                    lo, hi = span(c)
                    lo = max(lo, LAG)
                    act.wait_ge(s.dgs, c + 1)
                    nc.scalar.activation(dg[:, lo - LAG:hi - LAG, W], psG[c % 2][0:32, lo:hi], ACT.Identity
                                         ).then_inc(s.dge, 1)

                for b in range(B):
                    nc.scalar.activation(nsq[:, b], g.nT[:, b], ACT.Square).then_inc(s.nsq, 1)
                nc.scalar.preload_act_table(ACT.Sqrt)
                for b in range(B):
                    act.wait_ge(s.d2, b + 1)
                    nc.scalar.activation(dist[:, b], d2[:, b], ACT.Sqrt).then_inc(s.dist, 1)
                for t in range(SLOTS - LAG):
                    if t >= CH and t % CH == 2:
                        diag_edge(t // CH - 1)
                    act.wait_ge(s.edge, t + 1)
                    nc.scalar.activation(R[:, t + LAG + 1, 0:1], psR[t % 2][0:32, t:t + 1], ACT.Identity,
                                         bias=g.C("big_first")[0:32]).then_inc(s.Redge, 1)
                for c in range(NCH - 2, NCH):
                    diag_edge(c)

            @block.tensor
            def _(pe):
                def diag_shift(c):
                    lo, hi = span(c)
                    pe.wait_ge(s.dg, c + 1)
                    if c >= 2:
                        pe.wait_ge(s.dge, c - 1)
                    nc.tensor.matmul(psG[c % 2][0:32, lo:hi], shl[:], dg[:, lo:hi, 0], start=True, stop=True
                                     ).then_inc(s.dgs, 1)

                pe.wait_ge(s.ctx2, 1)
                for b in range(B):
                    pe.wait_ge(s.nsq, b + 1)
                    nc.tensor.matmul(psD[b][0:T, :], g.C("one")[:, 0:T], nsq[:, b], start=True, stop=False)
                    nc.tensor.matmul(psD[b][0:T, :], ctx2[:, b * T:(b + 1) * T], g.nT[:, b], start=False, stop=True
                                     ).then_inc(s.dd, 1)
                for t in range(SLOTS - LAG):
                    if t >= CH and t % CH == 2:
                        diag_shift(t // CH - 1)
                    pe.wait_ge(s.R, t + 1)
                    nc.tensor.matmul(psR[t % 2][0:32, t:t + 1], g.C("shift_r")[0:32], R[:, t + 1, W:W + 1],
                                     start=True, stop=True).then_inc(s.edge, 1)
                for c in range(NCH - 2, NCH):
                    diag_shift(c)

            @block.vector
            def _(dve):
                def diag_le_up(c):
                    lo, hi = span(c)
                    nc.vector.tensor_tensor(isq[:, lo:hi], R[:, lo:hi, 0:W], R[:, lo:hi, 1:W + 1], ALU.is_le
                                            ).then_inc(s.isq, 1)

                def not_left(c):
                    lo, hi = span(c)
                    nc.vector.tensor_tensor(isn[:, lo:hi], q[:, lo:hi], R[:, lo + 1:hi + 1, 0:W], ALU.is_le
                                            ).then_inc(s.isn, 1)

                def diagonal(c):
                    lo, hi = span(c)
                    dve.wait_ge(s.isq, c + 1)
                    dve.wait_ge(s.isn, c + 1)
                    nc.vector.tensor_tensor(dg[:, lo:hi, 0:W], isq[:, lo:hi], isn[:, lo:hi], ALU.mult
                                            ).then_inc(s.dg, 1)

                def up_less_1(c):
                    lo, hi = span(c)
                    dve.wait_ge(s.dg, c + 1)
                    nc.vector.scalar_tensor_tensor(out=nu[:, lo:hi], in0=isn[:, lo:hi], scalar=1.0,
                                                   in1=dg[:, lo:hi, 0:W], op0=ALU.subtract, op1=ALU.subtract
                                                   ).then_inc(s.nu, 1)

                def thresholds(c):
                    lo, hi = span(c)
                    dve.wait_ge(s.nu, c + 1)
                    dve.wait_ge(s.dge, min(c + 2, NCH))
                    nc.vector.scalar_tensor_tensor(out=theta[:, lo:hi], in0=dg[:, lo:hi, 1:W + 1], scalar=2.0,
                                                   in1=nu[:, lo:hi], op0=ALU.subtract, op1=ALU.mult
                                                   ).then_inc(s.theta, 1)

                nc.vector.tensor_scalar(ctx2[:], g.G("ctxT"), -2.0, None, ALU.mult).then_inc(s.ctx2, 1)
                nc.vector.memset(zero[:], 0.0).then_inc(s.zero, 1)
                for b in range(B):
                    if b:
                        dve.wait_ge(s.aa, b)
                    nc.vector.scalar_tensor_tensor(out=junk[:], in0=g.ctx[:, b], scalar=1.0, in1=g.ctx[:, b],
                                                   op0=ALU.mult, op1=ALU.mult, accum_out=aa[:, b:b + 1]
                                                   ).then_inc(s.aa, 1)
                dve.wait_ge(s.aa, B)
                for b in range(B):
                    dve.wait_ge(s.dd, b + 1)
                    nc.vector.tensor_scalar(d2[:, b], psD[b][0:T, :], aa[:, b:b + 1], 0.0, ALU.add, ALU.max
                                            ).then_inc(s.d2, 1)
                nc.vector.tensor_copy(shl[:], g.C("shift_l")[0:32])
                nc.vector.memset(dg[:, :, W:W + 1], 0.0)
                nc.vector.memset(I[:, SLOTS, 0:W], 1.0)
                for t in range(SLOTS, SLOTS - LAG - 1, -1):
                    nc.vector.tensor_copy(I[:, t, W:W + 1], g.C("bnd_last")[0:32])
                nc.vector.memset(R[:, 0, :], BIG)
                nc.vector.memset(R[:, 1:LAG + 1, 0:1], BIG).then_inc(s.big, 1)
                dve.wait_ge(s.big, 1)
                for t in range(SLOTS):
                    if t == PIECES[0][0]:
                        dve.wait_ge(s.D0, 16 * B)
                    if t == PIECES[1][0]:
                        dve.wait_ge(s.D1, 16 * B)
                    if t >= 1:
                        dve.wait_ge(s.R, t)
                    nc.vector.tensor_tensor(q[:, t], R[:, t, 0:W], R[:, t, 1:W + 1], ALU.min).then_inc(s.q, 1)
                    if t >= CH:
                        (diag_le_up, not_left, diagonal, up_less_1)[t % CH](t // CH - 1)
                    dve.wait_ge(s.q, t + 1)
                    if t >= LAG:
                        dve.wait_ge(s.Redge, t - LAG + 1)
                    first = g.C("init0")[0:32] if t == 0 else R[:, t + 1, 0:1]
                    nc.vector.tensor_tensor_scan(R[:, t + 1, 1:W + 1], q[:, t], D[:, t], first, ALU.min, ALU.add
                                                 ).then_inc(s.R, 1)
                    if t >= 3 * CH and t % CH == 0:
                        thresholds(t // CH - 3)
                dve.wait_ge(s.R, SLOTS)
                up_less_1(NCH - 2)
                diag_le_up(NCH - 1)
                not_left(NCH - 1)
                diagonal(NCH - 1)
                up_less_1(NCH - 1)
                for c in range(NCH - 3, NCH):
                    thresholds(c)
                dve.wait_ge(s.theta, NCH)
                nc.vector.tensor_tensor(theta[:, T:SLOTS], theta[:, T:SLOTS],
                                        g.C("row_ok")[0:32].unsqueeze(2).broadcast_to([32, SLOTS - T, W]), ALU.mult)

            @block.sync
            def _(sp):
                sp.wait_ge(s.zero, 1)
                for b in range(B):
                    sp.dma_start(scr_d[b][0:PAD, :], zero[:]).then_inc(s.stored, 16)
                    sp.dma_start(scr_d[b][PAD + T:rows, :], zero[:]).then_inc(s.stored, 16)
                for b in range(B):
                    sp.wait_ge(s.dist, b + 1)
                    sp.dma_start(scr_d[b][PAD:PAD + T, :], dist[:, b]).then_inc(s.stored, 16)
                sp.wait_ge(s.stored, 16 * 3 * B)
                for (lo, hi), loaded in zip(PIECES, (s.D0, s.D1)):
                    for b in range(B):
                        sp.dma_start(D[b * BLK:(b + 1) * BLK, lo:hi], skewed(scr_d[b], lo, hi)).then_inc(loaded, 16)

        with nc.Block() as block:
            @block.vector
            def _(dve):
                def step_here(c):
                    lo, hi = span(c)
                    nc.vector.tensor_tensor(t1[:, lo:hi], I[:, lo:hi, 0:W], I[:, lo:hi, 1:W + 1], ALU.subtract
                                            ).then_inc(s.t1, 1)

                def right_diagonal(c):
                    lo, hi = span(c)
                    nc.vector.tensor_tensor(t2[:, lo:hi], dg[:, lo:hi, 1:W + 1], I[:, lo + 1:hi + 1, 1:W + 1], ALU.mult
                                            ).then_inc(s.t2, 1)

                def diagonal_leaves(c):
                    lo, hi = span(c)
                    dve.wait_ge(s.t1, NCH - c)
                    dve.wait_ge(s.t2, 2 * (NCH - c) - 1)
                    nc.vector.tensor_tensor(t2[:, lo:hi], t1[:, lo:hi], t2[:, lo:hi], ALU.mult).then_inc(s.t2, 1)

                def entered_between(c):
                    lo, hi = span(c)
                    nc.vector.tensor_tensor(t3[:, lo:hi], I[:, lo + 1:hi + 1, 0:W], I[:, lo:hi, 1:W + 1], ALU.subtract
                                            ).then_inc(s.t3, 1)

                def on_path(c):
                    lo, hi = span(c)
                    dve.wait_ge(s.t2, 2 * (NCH - c))
                    dve.wait_ge(s.t3, NCH - c)
                    nc.vector.tensor_tensor(path[:, lo:hi], t3[:, lo:hi], t2[:, lo:hi], ALU.subtract).then_inc(s.P, 1)

                for k, t in enumerate(range(SLOTS - 1, -1, -1)):
                    c = t // CH + 1
                    if k >= 1:
                        dve.wait_ge(s.I, k)
                    nc.vector.tensor_tensor(X[:, t], I[:, t + 1, 0:W], I[:, t + 1, 1:W + 1], ALU.add).then_inc(s.X, 1)
                    if c < NCH and t % CH:
                        (on_path, diagonal_leaves, step_here)[t % CH - 1](c)
                    dve.wait_ge(s.X, k + 1)
                    if k >= LAG:
                        dve.wait_ge(s.Iedge, k - LAG + 1)
                    nc.vector.tensor_tensor_scan(I[:, t, W - 1::-1], X[:, t, ::-1], theta[:, t, ::-1],
                                                 I[:, t, W:W + 1], ALU.add, ALU.is_gt).then_inc(s.I, 1)
                    if c < NCH and t % CH >= 2:
                        (entered_between, right_diagonal)[t % CH - 2](c)
                dve.wait_ge(s.I, SLOTS)
                for part in (step_here, right_diagonal, diagonal_leaves, entered_between, on_path):
                    part(0)
                for b in range(B):
                    dve.wait_ge(s.ex, b + 1)
                    nc.vector.tensor_tensor(g.xT[:, b], g.xT[:, b], psD[b], ALU.add)

            @block.tensor
            def _(pe):
                for k, t in enumerate(range(SLOTS - 1, LAG - 1, -1)):
                    pe.wait_ge(s.I, k + 1)
                    nc.tensor.matmul(psI[t % 2][0:32, t:t + 1], shl[:], I[:, t, 0:1], start=True, stop=True
                                     ).then_inc(s.edge, 1)
                for b in range(B):
                    pe.wait_ge(s.pn, 16 * B)
                    nc.tensor.matmul(psD[b], g.ctx[:, b], pn[:, b], start=True, stop=True).then_inc(s.ex, 1)

            @block.scalar
            def _(act):
                for k, t in enumerate(range(SLOTS - 1, LAG - 1, -1)):
                    act.wait_ge(s.edge, SLOTS - LAG + k + 1)
                    nc.scalar.activation(I[:, t - LAG, W:W + 1], psI[t % 2][0:32, t:t + 1], ACT.Identity
                                         ).then_inc(s.Iedge, 1)

            @block.sync
            def _(sp):
                for c0, c1 in STORES:
                    sp.wait_ge(s.P, NCH - c0)
                    lo, hi = span(c0)[0], span(c1 - 1)[1]
                    for b in range(B):
                        sp.dma_start(skewed(scr_p[b], lo, hi), path[b * BLK:(b + 1) * BLK, lo:hi]).then_inc(s.pst, 16)
                sp.wait_ge(s.pst, 16 * B * len(STORES))
                for b in range(B):
                    sp.dma_start(pn[:, b], scr_p[b][PAD:PAD + T, :]).then_inc(s.pn, 16)


def moe_stage(nc, a, g):
    ln_block(nc, g)
    with ExitStack() as st:
        def sb(name, shape, dt=F32):
            return g.sb("moe_" + name, shape, dt, stack=st)

        N = B * NC
        lg, ex, mx = sb("lg", [P, N, E]), sb("ex", [P, N, E]), sb("mx", [P, N])
        sm, rsm, sc = sb("sm", [P, N]), sb("rsm", [P, N]), sb("sc", [P, N, E])
        gt, ge, rank, top = sb("gt", [P, N * E, E]), sb("ge", [P, N * E, E]), sb("rank", [P, N * E]), sb("top", [P, N, E])
        den, rden, route = sb("den", [P, NC, E]), sb("rden", [P, NC, E]), sb("route", [P, NC, B, E])
        route8 = sb("route8", [P, NC, B * E * 8])
        v = sb("v", [P, S])
        hit = sb("hit", [P, S])
        cnt, enough, pick_i = sb("cnt", [P, 1]), sb("enough", [P, 1], BF16), sb("pick_i", [P, 1], I32)
        low, thr, base = (sb(n, [P, 1], I32) for n in ("low", "thr", "base"))
        above, eqm, run, chosen = sb("above", [P, S]), sb("eqm", [P, S]), sb("run", [P, S]), sb("chosen", [P, S])
        room = sb("room", [P, 2])
        block8, pick16 = sb("block8", [P, P], BF16), sb("pick16", [P, 2 * P], BF16)
        chosen16 = sb("chosen16", [P, S], BF16)
        hT = sb("hT", [P, B, 2, S])
        s = g.sem_set("moe", "gate gates ex0 ex vps v low thr base cnt enough sum pick route8 "
                             "b8 above eqm run room chosen h1 h mask hm out")
        psA, psV, psS = g.ps[0], g.ps[1], g.ps[2]
        kk = g.C("kk").bitcast(I32)
        NF_ = len(SHIFTS)
        with nc.Block() as block:
            @block.tensor
            def _(pe):
                for b in range(B):
                    for c in range(NC):
                        n = b * NC + c
                        last = nc.tensor.matmul(psA[:, n * E:(n + 1) * E], g.nT[:, b, c * P:(c + 1) * P], g.G("wg"),
                                                start=True, stop=True)
                last.then_inc(s.gate, 1)
                for b in range(B):
                    for k in range(2):
                        nc.tensor.matmul(g.ps[4 + 2 * b + k][:], g.G("W1")[:, k * P:(k + 1) * P], g.nT[:, b],
                                         start=True, stop=True).then_inc(s.h1, 1)
                pe.wait_ge(s.route8, 1)
                for c in range(NC):
                    last = nc.tensor.matmul(psV[:, c * P:(c + 1) * P], route8[:, c], g.C("ident"), start=True,
                                            stop=True)
                last.then_inc(s.vps, 1)
                pe.wait_ge(s.b8, 1)
                for n in range(NF_):
                    pe.wait_ge(s.enough, n + 1)
                    nc.tensor.matmul(psS[:, n:n + 1], block8[:], enough[:], start=True, stop=True).then_inc(s.sum, 1)
                pe.wait_ge(s.chosen, 1)
                pe.wait_ge(s.h, 4)
                for b in range(B):
                    rows = slice(b * 64, b * 64 + 64)
                    for k in range(2):
                        nc.tensor.matmul(g.ps[4 + 2 * b + k][:], pick16[rows, k * P:(k + 1) * P], chosen16[rows],
                                         start=True, stop=True).then_inc(s.mask, 1)
                pe.wait_ge(s.chosen, 2)
                for b in range(B):
                    rows = slice(b * 64, b * 64 + 64)
                    nc.tensor.matmul(g.ps[b][:], g.G("b2")[rows], chosen[rows], start=True, stop=False)
                    for k in range(2):
                        pe.wait_ge(s.hm, 2 * b + k + 1)
                        last = nc.tensor.matmul(g.ps[b][:], g.G("W2")[:, k * P:(k + 1) * P], hT[:, b, k],
                                                start=False, stop=(k == 1))
                    last.then_inc(s.out, 1)

            @block.scalar
            def _(act):
                act.wait_ge(s.ex0, 1)
                nc.scalar.activation(ex[:], lg[:], ACT.Exp).then_inc(s.ex, 1)
                for b in range(B):
                    for k in range(2):
                        act.wait_ge(s.h1, 2 * b + k + 1)
                        nc.scalar.activation(hT[:, b, k], g.ps[4 + 2 * b + k][:], ACT.Gelu,
                                             bias=g.G("b1")[:, k:k + 1]).then_inc(s.h, 1)

            @block.vector
            def _(dve):
                def bc(t, axis, shape):
                    return t.unsqueeze(axis).broadcast_to(shape)

                nc.vector.tensor_copy(pick16[:], g.C("pick"))
                nc.vector.tensor_copy(block8[:], g.C("block8")).then_inc(s.b8, 1)
                nc.vector.memset(low[:], 0).then_inc(s.low, 1)
                dve.wait_ge(s.gate, 1)
                nc.vector.tensor_tensor(lg[:], psA[:, 0:N * E].rearrange("p (n e) -> p n e", e=E),
                                        bc(g.G("bg"), 1, [P, N, E]), ALU.add).then_inc(s.gates, 1)
                dve.wait_ge(s.gates, 1)
                nc.vector.tensor_reduce(mx[:], lg[:], AX.X, ALU.max).then_inc(s.gates, 1)
                dve.wait_ge(s.gates, 2)
                nc.vector.tensor_tensor(lg[:], lg[:], bc(mx[:], 2, [P, N, E]), ALU.subtract).then_inc(s.ex0, 1)
                dve.wait_ge(s.ex, 1)
                nc.vector.tensor_reduce(sm[:], ex[:], AX.X, ALU.add).then_inc(s.gates, 1)
                dve.wait_ge(s.gates, 3)
                nc.vector.reciprocal(rsm[:], sm[:]).then_inc(s.gates, 1)
                dve.wait_ge(s.gates, 4)
                nc.vector.tensor_tensor(sc[:], ex[:], bc(rsm[:], 2, [P, N, E]), ALU.mult).then_inc(s.gates, 1)
                dve.wait_ge(s.gates, 5)
                mine = bc(sc[:].rearrange("p n e -> p (n e)"), 2, [P, N * E, E]).rearrange("p (n e) f -> p n e f", e=E)
                other = bc(sc[:], 2, [P, N, E, E])
                gt4, ge4 = (t[:].rearrange("p (n e) f -> p n e f", e=E) for t in (gt, ge))
                nc.vector.tensor_tensor(gt4, other, mine, ALU.is_gt)
                nc.vector.tensor_tensor(ge4, other, mine, ALU.is_ge).then_inc(s.gates, 1)
                dve.wait_ge(s.gates, 6)
                lower = bc(g.C("lower"), 1, [P, N, E * E])
                flat = lambda t: t[:].rearrange("p (n e) f -> p n (e f)", e=E)
                nc.vector.tensor_tensor(flat(ge), flat(ge), lower, ALU.mult).then_inc(s.gates, 1)
                dve.wait_ge(s.gates, 7)
                nc.vector.tensor_tensor(gt[:], gt[:], ge[:], ALU.max).then_inc(s.gates, 1)
                dve.wait_ge(s.gates, 8)
                nc.vector.tensor_reduce(rank[:], gt[:], AX.X, ALU.add).then_inc(s.gates, 1)
                dve.wait_ge(s.gates, 9)
                nc.vector.scalar_tensor_tensor(out=top[:].rearrange("p n e -> p (n e)"), in0=rank[:],
                                               scalar=float(TOPK), in1=sc[:].rearrange("p n e -> p (n e)"),
                                               op0=ALU.is_lt, op1=ALU.mult).then_inc(s.gates, 1)
                dve.wait_ge(s.gates, 10)
                nc.vector.scalar_tensor_tensor(out=den[:], in0=top[:, 0:NC], scalar=1.0, in1=top[:, NC:N],
                                               op0=ALU.mult, op1=ALU.add).then_inc(s.gates, 1)
                dve.wait_ge(s.gates, 11)
                nc.vector.tensor_scalar(den[:], den[:], 1e-6, None, ALU.add).then_inc(s.gates, 1)
                dve.wait_ge(s.gates, 12)
                nc.vector.reciprocal(rden[:], den[:]).then_inc(s.gates, 1)
                dve.wait_ge(s.gates, 13)
                for b in range(B):
                    last = nc.vector.scalar_tensor_tensor(out=route[:, :, b, :], in0=top[:, b * NC:(b + 1) * NC],
                                                          scalar=float(CAP), in1=rden[:], op0=ALU.mult, op1=ALU.mult)
                last.then_inc(s.gates, 1)
                dve.wait_ge(s.gates, 14)
                nc.vector.tensor_copy(route8[:].rearrange("p c (r k) -> p (c r) k", k=8),
                                      bc(route[:].rearrange("p c b e -> p (c b e)"), 2, [P, NC * B * E, 8])
                                      ).then_inc(s.route8, 1)
                dve.wait_ge(s.vps, 1)
                nc.vector.tensor_copy(v[:], psV[:]).then_inc(s.v, 1)
                dve.wait_ge(s.low, 1)
                nc.vector.tensor_tensor(thr[:], low[:], kk[:, 0:1], ALU.bitwise_or).then_inc(s.thr, 1)
                dve.wait_ge(s.v, 1)
                for n, shift in enumerate(SHIFTS):
                    dve.wait_ge(s.thr, n + 1)
                    nc.vector.tensor_scalar(hit[:], v[:], thr[:].bitcast(F32), None, ALU.is_ge, ALU.add,
                                            accum_out=cnt[:]).then_inc(s.cnt, 1)
                    dve.wait_ge(s.cnt, n + 1)
                    nc.vector.tensor_scalar(enough[:], cnt[:], float(KEEP), None, ALU.is_ge).then_inc(s.enough, 1)
                    dve.wait_ge(s.low, n + 1)
                    if n + 1 < NF_:
                        nc.vector.tensor_tensor(base[:], low[:], kk[:, n + 1:n + 2], ALU.bitwise_or
                                                ).then_inc(s.base, 1)
                    dve.wait_ge(s.sum, n + 1)
                    nc.vector.tensor_scalar(pick_i[:], psS[:, n:n + 1], -LOWEST[n], float(1 << shift), ALU.add, ALU.mult
                                            ).then_inc(s.pick, 1)
                    dve.wait_ge(s.pick, n + 1)
                    if n + 1 < NF_:
                        dve.wait_ge(s.base, n + 1)
                        nc.vector.tensor_tensor(thr[:], base[:], pick_i[:], ALU.bitwise_or).then_inc(s.thr, 1)
                    nc.vector.tensor_tensor(low[:], low[:], pick_i[:], ALU.bitwise_or).then_inc(s.low, 1)
                dve.wait_ge(s.low, NF_ + 1)
                least = low[:].bitcast(F32)
                nc.vector.tensor_scalar(above[:], v[:], least, None, ALU.is_gt, ALU.add, accum_out=room[:, 0:1]
                                        ).then_inc(s.above, 1)
                nc.vector.tensor_scalar(eqm[:], v[:], least, None, ALU.is_equal).then_inc(s.eqm, 1)
                dve.wait_ge(s.above, 1)
                nc.vector.tensor_scalar(room[:, 1:2], room[:, 0:1], -1.0, float(KEEP), ALU.mult, ALU.add
                                        ).then_inc(s.room, 1)
                dve.wait_ge(s.eqm, 1)
                nc.vector.tensor_tensor_scan(run[:], g.C("one")[:, 0:1].broadcast_to([P, S]), eqm[:], 0.0,
                                             ALU.mult, ALU.add).then_inc(s.run, 1)
                dve.wait_ge(s.run, 1)
                dve.wait_ge(s.room, 1)
                nc.vector.scalar_tensor_tensor(out=run[:], in0=run[:], scalar=room[:, 1:2], in1=eqm[:], op0=ALU.is_le,
                                               op1=ALU.mult).then_inc(s.run, 1)
                dve.wait_ge(s.run, 2)
                nc.vector.tensor_tensor(chosen16[:], run[:], above[:], ALU.add).then_inc(s.chosen, 1)
                nc.vector.tensor_tensor(chosen[:], run[:], above[:], ALU.add).then_inc(s.chosen, 1)
                for b in range(B):
                    for k in range(2):
                        dve.wait_ge(s.mask, 2 * b + k + 1)
                        nc.vector.tensor_tensor(hT[:, b, k], hT[:, b, k], g.ps[4 + 2 * b + k][:], ALU.mult
                                                ).then_inc(s.hm, 1)
                for b in range(B):
                    dve.wait_ge(s.out, b + 1)
                    nc.vector.tensor_tensor(g.xT[:, b], g.xT[:, b], g.ps[b][:], ALU.add)


def attn_stage(nc, a, g):
    ln_block(nc, g)
    with ExitStack() as st:
        def sb(name, shape, dt=F32):
            return g.sb("at_" + name, shape, dt, stack=st)

        SCALE = 1.0 / np.sqrt(np.float32(DH))
        PAIRS = NC // 2
        STEPS = B * PAIRS
        UNROLL = 2
        BODY = UNROLL * STEPS
        QT = sb("QT", [P, B, S])
        KT = sb("KT", [P, B, S + 2])
        V = sb("V", [P, B, NC, P])
        kc = sb("kc", [P, 2, B, S])
        prob = sb("prob", [P, 2, S])
        pT = sb("pT", [P, 2, NC, P])
        mx, mb, bias = sb("mx", [P, 2, 2]), sb("mb", [P, 2, 2]), sb("bias", [P, 2, 2])
        sums, rsum = sb("sums", [P, B, NC, H]), sb("rsum", [P, B * NC * H])
        on, oT = sb("on", [P, B, S]), sb("oT", [P, B, S])
        s = g.sem_set("at", "q k v k1 kc0 kc S mx mb bias exp T copy rsum on turned oT o")
        psS = [g.psum[:, 0:2], g.psum[:, 2:4]]
        psT, psO = g.ps[4:6], g.ps[6:8]

        with nc.Block() as block:
            @block.tensor
            def _(pe):
                for b in range(B):
                    nc.tensor.matmul(g.ps[b], g.G("aWq"), g.nT[:, b], start=True, stop=True).then_inc(s.q, 1)
                    nc.tensor.matmul(g.ps[2 + b], g.G("aWk"), g.nT[:, b], start=True, stop=True).then_inc(s.k, 1)
                for b in range(B):
                    for c in range(NC):
                        last = nc.tensor.matmul(g.ps[4 + b][:, c * P:(c + 1) * P], g.nT[:, b, c * P:(c + 1) * P],
                                                g.G("aWv"), start=True, stop=True)
                    last.then_inc(s.v, 1)

            @block.scalar
            def _(act):
                for b in range(B):
                    act.wait_ge(s.q, b + 1)
                    nc.scalar.activation(QT[:, b], g.ps[b], ACT.Identity, bias=g.G("abq"))

            @block.vector
            def _(dve):
                nc.vector.memset(KT[:, :, 0:1], 0.0)
                nc.vector.memset(KT[:, :, S + 1:S + 2], 0.0)
                for b in range(B):
                    dve.wait_ge(s.k, b + 1)
                    nc.vector.tensor_scalar(KT[:, b, 1:S + 1], g.ps[2 + b], g.G("abk"), None, ALU.add
                                            )
                for b in range(B):
                    dve.wait_ge(s.v, b + 1)
                    nc.vector.tensor_tensor(V[:, b], g.ps[4 + b].rearrange("p (c d) -> p c d", d=P),
                                            g.G("abv").unsqueeze(1).broadcast_to([P, NC, P]), ALU.add
                                            )

        def tap(o, t):
            return g.G("conv_w")[:, bass.ds(o * 3 + t, 1)]

        def at_step(k):
            return k % STEPS // PAIRS, k % PAIRS * 2, k % 2

        with nc.Block() as block:
            @block.tensor
            def _(pe):
                def scores(k, c):
                    b, c0, u = at_step(k)
                    nc.tensor.matmul(psS[u][:, c], QT[:, b, (c0 + c) * P:(c0 + c + 1) * P],
                                     kc[:, k % BODY // STEPS, b], start=True, stop=True).then_inc(s.S, 1)

                def body(i, last):
                    for k in range(BODY):
                        b, c0, u = at_step(k)
                        more = not (last and k == BODY - 1)
                        if more and (k + 1) % STEPS == 0:
                            pe.wait_ge(s.kc, i * UNROLL + (k + 1) // STEPS + 1)
                        for c in range(2):
                            if more:
                                scores(k + 1, c)
                            pe.wait_ge(s.exp, i * (2 * BODY) + (2 * k + c + 1))
                            for kt in range(NC):
                                t = nc.tensor.transpose(psT[c][:, kt * P:(kt + 1) * P],
                                                        prob[:, c, kt * P:(kt + 1) * P], g.C("ident"))
                            t.then_inc(s.T, 1)
                        for c in range(2):
                            pe.wait_ge(s.copy, i * (2 * BODY) + (2 * k + c + 1))
                            head = i * (UNROLL * DH) + (k // STEPS * DH)
                            for kt in range(NC):
                                o = nc.tensor.matmul(psO[b][:, bass.ds(head + ((c0 + c) * P), DH)], pT[:, c, kt],
                                                     V[:, b, kt, bass.ds(head, DH)], start=(kt == 0),
                                                     stop=(kt == NC - 1))

                pe.wait_ge(s.kc, 1)
                for c in range(2):
                    scores(0, c)
                with pe.Fori(0, H // UNROLL - 1) as i:
                    body(i, False)
                body(H // UNROLL - 1, True)

            @block.scalar
            def _(act):
                def middle(o, u):
                    nc.scalar.activation(kc[:, u], KT[:, :, 1:S + 1], ACT.Identity, scale=tap(o, 1)
                                         ).then_inc(s.k1, 1)

                def exps(i, k):
                    b, c0, u = at_step(k)
                    act.wait_ge(s.bias, i * BODY + (k + 1))
                    for c in range(2):
                        col = i * UNROLL + ((b * NC + c0 + c) * H + k // STEPS)
                        nc.scalar.activation(prob[:, c], psS[u][:, c], ACT.Exp, bias=bias[:, u, c:c + 1],
                                             scale=float(SCALE),
                                             accum_out=sums[:].rearrange("p b c h -> p (b c h)")[:, bass.ds(col, 1)]
                                             ).then_inc(s.exp, 1)

                def body(i, last):
                    for k in range(BODY):
                        for c in range(2):
                            act.wait_ge(s.T, i * (2 * BODY) + (2 * k + c + 1))
                            nc.scalar.activation(pT[:, c].rearrange("p c q -> p (c q)"), psT[c], ACT.Identity
                                                 ).then_inc(s.copy, 1)
                        if k < BODY - 1:
                            exps(i, k + 1)
                        elif not last:
                            exps_next(i)
                        if k % STEPS == 0 and not (last and k // STEPS == UNROLL - 1):
                            middle(i * UNROLL + (k // STEPS + 1), (k // STEPS + 1) % 2)

                def exps_next(i):
                    act.wait_ge(s.bias, i * BODY + (BODY + 1))
                    for c in range(2):
                        col = i * UNROLL + (c * H + UNROLL)
                        nc.scalar.activation(prob[:, c], psS[0][:, c], ACT.Exp, bias=bias[:, 0, c:c + 1],
                                             scale=float(SCALE),
                                             accum_out=sums[:].rearrange("p b c h -> p (b c h)")[:, bass.ds(col, 1)]
                                             ).then_inc(s.exp, 1)

                middle(0, 0)
                exps(0, 0)
                with act.Fori(0, H // UNROLL - 1) as i:
                    body(i, False)
                body(H // UNROLL - 1, True)

            @block.vector
            def _(dve):
                def outer(o, u, t):
                    if t == 0:
                        dve.wait_ge(s.k1, o + 1)
                    else:
                        dve.wait_ge(s.kc0, o + 1)
                    nc.vector.scalar_tensor_tensor(out=kc[:, u], in0=KT[:, :, t:t + S], scalar=tap(o, t),
                                                   in1=kc[:, u], op0=ALU.mult, op1=ALU.add
                                                   ).then_inc(s.kc if t else s.kc0, 1)

                def maxima(n, u, head):
                    cb = g.G("conv_b")[:, bass.ds(head, 1)]
                    dve.wait_ge(s.S, n * 2 + 2)
                    nc.vector.tensor_reduce(mx[:, u], psS[u], AX.X, ALU.max).then_inc(s.mx, 1)
                    dve.wait_ge(s.mx, n + 1)
                    nc.vector.tensor_scalar(mb[:, u], mx[:, u], float(SCALE), cb, ALU.mult, ALU.add).then_inc(s.mb, 1)
                    dve.wait_ge(s.mb, n + 1)
                    nc.vector.tensor_scalar(bias[:, u], mb[:, u], -1.0, cb, ALU.mult, ALU.add).then_inc(s.bias, 1)

                def body(i, last):
                    for k in range(BODY):
                        if not (last and k == BODY - 1):
                            maxima(i * BODY + (k + 1), (k + 1) % 2, i * UNROLL + ((k + 1) // STEPS))
                        if k % STEPS in (1, 2) and not (last and k // STEPS == UNROLL - 1):
                            outer(i * UNROLL + (k // STEPS + 1), (k // STEPS + 1) % 2, 0 if k % STEPS == 1 else 2)

                outer(0, 0, 0)
                outer(0, 0, 2)
                maxima(0, 0, 0)
                with dve.Fori(0, H // UNROLL - 1) as i:
                    body(i, False)
                body(H // UNROLL - 1, True)

        with nc.Block() as block:
            @block.vector
            def _(dve):
                nc.vector.reciprocal(rsum[:], sums[:].rearrange("p b c h -> p (b c h)")).then_inc(s.rsum, 1)
                dve.wait_ge(s.rsum, 1)
                for b in range(B):
                    nc.vector.tensor_tensor(on[:, b].rearrange("p (n d) -> p n d", d=DH),
                                            psO[b].rearrange("p (n d) -> p n d", d=DH),
                                            rsum[:, b * NC * H:(b + 1) * NC * H].unsqueeze(2
                                                ).broadcast_to([P, NC * H, DH]), ALU.mult).then_inc(s.on, 1)
                for b in range(B):
                    dve.wait_ge(s.o, b + 1)
                    nc.vector.scalar_tensor_tensor(out=g.xT[:, b], in0=g.ps[2 + b], scalar=g.G("abo"), in1=g.xT[:, b],
                                                   op0=ALU.add, op1=ALU.add)

            @block.tensor
            def _(pe):
                for b in range(B):
                    pe.wait_ge(s.on, b + 1)
                    for c in range(NC):
                        last = nc.tensor.transpose(g.ps[b][:, c * P:(c + 1) * P], on[:, b, c * P:(c + 1) * P],
                                                   g.C("ident"))
                    last.then_inc(s.turned, 1)
                for b in range(B):
                    pe.wait_ge(s.oT, b + 1)
                    nc.tensor.matmul(g.ps[2 + b], g.G("aWo"), oT[:, b], start=True, stop=True).then_inc(s.o, 1)

            @block.scalar
            def _(act):
                for b in range(B):
                    act.wait_ge(s.turned, b + 1)
                    nc.scalar.activation(oT[:, b], g.ps[b], ACT.Identity).then_inc(s.oT, 1)


def xattn_stage(nc, a, g):
    ln_block(nc, g)
    with ExitStack() as st:
        def sb(name, shape, dt=F32):
            return g.sb("xa_" + name, shape, dt, stack=st)

        SCALE = 1.0 / np.sqrt(np.float32(P))
        qT, kT, v = sb("qT", [P, B, S]), sb("kT", [P, B * T]), sb("v", [T, B, P])
        mx, bias = sb("mx", [P, B, NC]), sb("bias", [P, B, NC])
        sums, rsum = sb("sums", [P, B, NC]), sb("rsum", [P, B, NC])
        prob, pn, pT = sb("prob", [P, B, NC, T]), sb("pn", [P, B, NC, T]), sb("pT", [T, B, S])
        s = g.sem_set("xa", "k kT v V q qT S mx bias exp rsum pn T pT o")
        with nc.Block() as block:
            @block.tensor
            def _(pe):
                nc.tensor.matmul(g.ps[2][:, 0:B * T], g.G("xWk"), g.G("ctxT"), start=True, stop=True).then_inc(s.k, 1)
                for b in range(B):
                    nc.tensor.matmul(g.ps[b], g.G("xWq"), g.nT[:, b], start=True, stop=True).then_inc(s.q, 1)
                for b in range(B):
                    last = nc.tensor.matmul(g.ps[3][0:T, b * P:(b + 1) * P], g.G("ctxT")[:, b * T:(b + 1) * T],
                                            g.G("xWv"), start=True, stop=True)
                last.then_inc(s.v, 1)
                pe.wait_ge(s.kT, 1)
                for b in range(B):
                    pe.wait_ge(s.qT, b + 1)
                    for c in range(NC):
                        last = nc.tensor.matmul(g.ps[4 + b][:, c * P:c * P + T], qT[:, b, c * P:(c + 1) * P],
                                                kT[:, b * T:(b + 1) * T], start=True, stop=True)
                    last.then_inc(s.S, 1)
                for b in range(B):
                    pe.wait_ge(s.pn, b + 1)
                    for c in range(NC):
                        last = nc.tensor.transpose(g.ps[6 + b][0:T, c * P:(c + 1) * P], pn[:, b, c], g.C("ident"))
                    last.then_inc(s.T, 1)
                pe.wait_ge(s.V, 1)
                for b in range(B):
                    pe.wait_ge(s.pT, b + 1)
                    nc.tensor.matmul(g.ps[b], v[:, b], pT[:, b], start=True, stop=True).then_inc(s.o, 1)

            @block.scalar
            def _(act):
                for b in range(B):
                    act.wait_ge(s.q, b + 1)
                    nc.scalar.activation(qT[:, b], g.ps[b], ACT.Identity, bias=g.G("xbq")).then_inc(s.qT, 1)
                for b in range(B):
                    act.wait_ge(s.bias, b + 1)
                    for c in range(NC):
                        nc.scalar.activation(prob[:, b, c], g.ps[4 + b][:, c * P:c * P + T], ACT.Exp,
                                             bias=bias[:, b, c:c + 1], scale=float(SCALE),
                                             accum_out=sums[:, b, c:c + 1]).then_inc(s.exp, 1)
                for b in range(B):
                    act.wait_ge(s.T, b + 1)
                    nc.scalar.activation(pT[:, b], g.ps[6 + b][0:T, :], ACT.Identity).then_inc(s.pT, 1)

            @block.vector
            def _(dve):
                dve.wait_ge(s.k, 1)
                nc.vector.tensor_scalar(kT[:], g.ps[2][:, 0:B * T], g.G("xbk"), None, ALU.add).then_inc(s.kT, 1)
                dve.wait_ge(s.v, 1)
                nc.vector.tensor_tensor(v[:], g.ps[3][0:T, 0:B * P].rearrange("p (b d) -> p b d", d=P),
                                        g.G("xbv")[0:T].unsqueeze(1).broadcast_to([T, B, P]), ALU.add).then_inc(s.V, 1)
                for b in range(B):
                    dve.wait_ge(s.S, b + 1)
                    nc.vector.tensor_reduce(mx[:, b], g.ps[4 + b].rearrange("p (c k) -> p c k", k=P)[:, :, 0:T], AX.X,
                                            ALU.max).then_inc(s.mx, 1)
                    dve.wait_ge(s.mx, b + 1)
                    nc.vector.tensor_scalar(bias[:, b], mx[:, b], -float(SCALE), None, ALU.mult).then_inc(s.bias, 1)
                for b in range(B):
                    dve.wait_ge(s.exp, NC * (b + 1))
                    nc.vector.reciprocal(rsum[:, b], sums[:, b]).then_inc(s.rsum, 1)
                    dve.wait_ge(s.rsum, b + 1)
                    nc.vector.tensor_tensor(pn[:, b], prob[:, b], rsum[:, b].unsqueeze(2).broadcast_to([P, NC, T]),
                                            ALU.mult).then_inc(s.pn, 1)
                for b in range(B):
                    dve.wait_ge(s.o, b + 1)
                    nc.vector.tensor_tensor(g.xT[:, b], g.xT[:, b], g.ps[b], ALU.add)


def ffn_stage(nc, a, g):
    with ExitStack() as st:
        def sb(name, shape, dt=F32):
            return g.sb("ff_" + name, shape, dt, stack=st)

        MAGIC = 1.5 * 2.0 ** 23
        TURN1 = 6.28125
        TURN2 = round((2 * np.pi - TURN1) * 2 ** 21) / 2 ** 21
        TURN3 = 2 * np.pi - TURN1 - TURN2
        LIMIT = float(np.nextafter(np.float32(np.pi), np.float32(0)))
        arg, turns, sincos = sb("arg", [P, 2, NF]), sb("turns", [P, 2, NF]), sb("sincos", [P, 2, NF])
        start, coef = sb("start", [P, NF]), sb("coef", [P, NF])
        ang, whole, q, hid = (sb(n, [P, B * NF, S]) for n in ("ang", "whole", "q", "hid"))
        s = g.sem_set("ff", "h ang whole red sin q relu f arg t args start sc m coef")

        def reduce_turns(dve, k):
            x, n_ = arg[:, k], turns[:, k]
            nc.vector.tensor_scalar(n_, x, 1.0 / (2 * np.pi), MAGIC, ALU.mult, ALU.add).then_inc(s.t, 1)
            dve.wait_ge(s.t, 5 * k + 1)
            nc.vector.tensor_scalar(n_, n_, MAGIC, None, ALU.subtract).then_inc(s.t, 1)
            dve.wait_ge(s.t, 5 * k + 2)
            for j, part in enumerate((TURN1, TURN2, TURN3)):
                nc.vector.scalar_tensor_tensor(out=x, in0=n_, scalar=-float(part), in1=x, op0=ALU.mult, op1=ALU.add
                                               ).then_inc(s.t, 1)
                dve.wait_ge(s.t, 5 * k + 3 + j)
            nc.vector.tensor_scalar(x, x, LIMIT, -LIMIT, ALU.min, ALU.max).then_inc(s.args, 1)

        def angles(dve):
            nc.vector.tensor_copy(arg[:, 0], g.G("ph")).then_inc(s.arg, 1)
            dve.wait_ge(s.arg, 1)
            reduce_turns(dve, 0)
            dve.wait_ge(s.args, 1)
            nc.vector.tensor_scalar(arg[:, 1], arg[:, 0], np.pi / 2, None, ALU.add).then_inc(s.arg, 1)
            nc.vector.scalar_tensor_tensor(out=start[:], in0=g.G("fb1"), scalar=0.1, in1=arg[:, 0], op0=ALU.mult,
                                           op1=ALU.add).then_inc(s.start, 1)
            dve.wait_ge(s.arg, 2)
            reduce_turns(dve, 1)
            dve.wait_ge(s.start, 1)
            nc.vector.tensor_scalar(start[:], start[:], 1 / (2 * np.pi), None, ALU.mult)

        ln_block(nc, g, angles)
        with nc.Block() as block:
            @block.tensor
            def _(pe):
                for b in range(B):
                    for f in range(NF):
                        nc.tensor.matmul(g.ps[b * NF + f], g.G("fW1")[:, f * P:(f + 1) * P], g.nT[:, b],
                                         start=True, stop=True).then_inc(s.h, 1)
                for b in range(B):
                    for f in range(NF):
                        pe.wait_ge(s.relu, b * NF + f + 1)
                        last = nc.tensor.matmul(g.ps[b * NF], g.G("fW2")[:, f * P:(f + 1) * P], hid[:, b * NF + f],
                                                start=(f == 0), stop=(f == NF - 1))
                    last.then_inc(s.f, 1)

            @block.scalar
            def _(act):
                LEAD = 2

                def angle(k):
                    act.wait_ge(s.h, k + 1)
                    nc.scalar.activation(ang[:, k], g.ps[k], ACT.Identity, bias=start[:, k % NF:k % NF + 1],
                                         scale=0.1 / (2 * np.pi)).then_inc(s.ang, 1)

                def sine(k):
                    act.wait_ge(s.red, k + 1)
                    nc.scalar.activation(ang[:, k], ang[:, k], ACT.Sin, scale=2 * LIMIT).then_inc(s.sin, 1)

                def relu(k):
                    act.wait_ge(s.q, k + 1)
                    nc.scalar.activation(hid[:, k], q[:, k], ACT.Relu, bias=g.G("fb1")[:, k % NF:k % NF + 1]
                                         ).then_inc(s.relu, 1)

                nc.scalar.preload_act_table(ACT.Sin)
                nc.scalar.activation(sincos[:], arg[:], ACT.Sin).then_inc(s.sc, 1)
                for k in range(B * NF + 2 * LEAD):
                    if k < B * NF:
                        angle(k)
                    if LEAD <= k < B * NF + LEAD:
                        sine(k - LEAD)
                    if k >= 2 * LEAD:
                        relu(k - 2 * LEAD)

            @block.vector
            def _(dve):
                dve.wait_ge(s.sc, 1)
                nc.vector.tensor_tensor(sincos[:, 1], sincos[:, 1], g.G("wr"), ALU.mult)
                nc.vector.tensor_tensor(sincos[:, 0], sincos[:, 0], g.G("wi"), ALU.mult).then_inc(s.m, 1)
                dve.wait_ge(s.m, 1)
                nc.vector.tensor_tensor(coef[:], sincos[:, 0], sincos[:, 1], ALU.add).then_inc(s.m, 1)
                dve.wait_ge(s.m, 2)
                nc.vector.scalar_tensor_tensor(out=coef[:], in0=coef[:], scalar=0.1, in1=g.G("wi"), op0=ALU.mult,
                                               op1=ALU.mult).then_inc(s.coef, 1)
                dve.wait_ge(s.coef, 1)
                LAG_ = 2
                for k in range(B * NF + LAG_):
                    if k < B * NF:
                        dve.wait_ge(s.ang, k + 1)
                        nc.vector.tensor_scalar(whole[:, k], ang[:, k], MAGIC, MAGIC, ALU.add, ALU.subtract
                                                ).then_inc(s.whole, 1)
                    if k >= LAG_:
                        dve.wait_ge(s.sin, k - LAG_ + 1)
                        nc.vector.scalar_tensor_tensor(out=q[:, k - LAG_], in0=ang[:, k - LAG_],
                                                       scalar=coef[:, (k - LAG_) % NF:(k - LAG_) % NF + 1],
                                                       in1=g.ps[k - LAG_], op0=ALU.mult, op1=ALU.add).then_inc(s.q, 1)
                    if k < B * NF:
                        dve.wait_ge(s.whole, k + 1)
                        nc.vector.tensor_tensor(ang[:, k], ang[:, k], whole[:, k], ALU.subtract).then_inc(s.red, 1)
                for b in range(B):
                    dve.wait_ge(s.f, b + 1)
                    nc.vector.scalar_tensor_tensor(out=g.xT[:, b], in0=g.ps[b * NF], scalar=g.G("fb2"), in1=g.xT[:, b],
                                                   op0=ALU.add, op1=ALU.add)


def store_stage(nc, a, g):
    with ExitStack() as st:
        rows = g.sb("out_rows", [P, B * NC, P], stack=st)
        s = g.sem_set("store", "turned rows out")
        with nc.Block() as block:
            @block.tensor
            def _(pe):
                for b in range(B):
                    for c in range(NC):
                        last = nc.tensor.transpose(g.ps[b][:, c * P:(c + 1) * P], g.xT[:, b, c * P:(c + 1) * P],
                                                   g.C("ident"))
                    last.then_inc(s.turned, 1)

            @block.vector
            def _(dve):
                for b in range(B):
                    dve.wait_ge(s.turned, b + 1)
                    nc.vector.tensor_copy(rows[:, b * NC:(b + 1) * NC, :].rearrange("p c d -> p (c d)"), g.ps[b][:]
                                          ).then_inc(s.rows, 1)

            @block.sync
            def _(sp):
                for b in range(B):
                    sp.wait_ge(s.rows, b + 1)
                    sp.dma_start(a["out"][b].rearrange("(c p) d -> p c d", p=P), rows[:, b * NC:(b + 1) * NC, :]
                                 ).then_inc(s.out, 16)
                sp.wait_ge(s.out, 16 * B)


def layout(i):
    f = {k: np.asarray(v) for k, v in i.items()}
    parts = []
    for n in L0_COLS:
        v = {"Wq": "Wq", "Wk": "Wk", "Wv": "Wv", "Wo": "Wo", "Wf1": "Wf1", "Wf2": "Wf2", "s1": "ln1_s", "b1": "ln1_b",
             "s2": "ln2_s", "b2": "ln2_b"}.get(n, n)
        w = f["L0_attn_" + v]
        if n == "Wf2":
            w = w.reshape(LAYERS, NF, P, P).transpose(0, 2, 1, 3).reshape(LAYERS, P, FF)
        elif n == "bf1":
            w = w.reshape(LAYERS, NF, P).transpose(0, 2, 1)
        elif w.ndim == 2:
            w = w[:, :, None]
        parts.append(w)
    l0 = np.ascontiguousarray(np.concatenate(parts, axis=2))
    row = lambda v: np.broadcast_to(v[None, :], (P, v.shape[0]))
    col = lambda v: v.reshape(-1, P).T
    b2 = np.zeros((P, P), f["L0_ffn_b2"].dtype)
    b2[0:64:8] = f["L0_ffn_b2"]
    b2[64:128:8] = f["L0_ffn_b2"]
    cols = {
        "ctxT": f["ctx_1024"].transpose(2, 0, 1).reshape(P, B * T),
        "wg": f["L0_ffn_w_gate_w"], "bg": row(f["L0_ffn_w_gate_b"]),
        "W1": f["L0_ffn_W1"].transpose(1, 0, 2).reshape(P, E * HID),
        "W2": f["L0_ffn_W2"].reshape(2, P, P).transpose(1, 0, 2).reshape(P, 2 * P),
        "b1": col(f["L0_ffn_b1"].reshape(-1)), "b2": b2,
        "aWq": f["L1_attn_Wq"].T, "aWk": f["L1_attn_Wk"].T, "aWv": f["L1_attn_Wv"].T, "aWo": f["L1_attn_Wo"].T,
        "abq": col(f["L1_attn_bq"]), "abk": col(f["L1_attn_bk"]), "abv": row(f["L1_attn_bv"]),
        "abo": col(f["L1_attn_bo"]),
        "conv_w": np.repeat(f["L1_attn_conv_w"].transpose(1, 0, 2).reshape(H, 3 * H), DH, axis=0),
        "conv_b": row(f["L1_attn_conv_b"]),
        "xWq": f["L1_xattn_Wq"].T, "xWk": f["L1_xattn_Wk"].T, "xWv": f["L1_xattn_Wv"].T,
        "xbq": col(f["L1_xattn_bq"]), "xbk": col(f["L1_xattn_bk"]), "xbv": row(f["L1_xattn_bv"]),
        "fW1": f["L1_ffn_W1"], "fW2": f["L1_ffn_W2"].reshape(NF, P, P).transpose(1, 0, 2).reshape(P, FF),
        "fb1": col(f["L1_ffn_b1"]), "ph": col(f["L1_ffn_quantum_phases"]), "wr": col(f["L1_ffn_quantum_weights_real"]),
        "wi": col(f["L1_ffn_quantum_weights_imag"]), "fb2": col(f["L1_ffn_b2"]),
    }
    params = np.ascontiguousarray(np.concatenate([cols[n] for n in G_AT], axis=1))
    assert params.shape == (P, G_N) and l0.shape == (LAYERS, P, L0_N)
    return {"x": f["x"], "ctx": f["ctx_1024"], "l0": l0, "params": params, "consts": constants()}


def kernel(**inputs):
    import concourse.bacc as bacc
    from concourse.bass_utils import run_bass_kernel_spmd

    nc = bacc.Bacc("TRN2", target_bir_lowering=False, num_devices=1)
    arrays = layout(inputs)
    a = {n: nc.dram_tensor("in_" + n, v.shape, mybir.dt.from_np(v.dtype), kind="ExternalInput").ap()
         for n, v in arrays.items()}
    a["out"] = nc.dram_tensor("out", (B, S, P), F32, kind="ExternalOutput").ap()
    build(nc, a)
    r = run_bass_kernel_spmd(nc, [{"in_" + n: v for n, v in arrays.items()}], core_ids=[0])
    return r.results[0]["out"]
```

```python
from collections import namedtuple
from contextlib import ExitStack

import numpy as np

import concourse.bass as bass
from concourse import mybir

P = 128
B = 2
S = 512
NC = S // P
T = 77
LAYERS = 8
FF = 512
NF = FF // P
E = 8
HID = 32
TOPK = 2
CAP = B
KEEP = S // 2
H = 16
DH = P // H
BLK = 16
W = S // BLK
LAG = 2
SLOTS = T + LAG * (BLK - 1)
PAD = LAG * (BLK - 1)
BIG = 1e30
SHIFTS = [28, 25, 22, 19, 16, 13, 10, 7, 4, 1, 0]

F32 = mybir.dt.float32
I32 = mybir.dt.int32
BF16 = mybir.dt.bfloat16
ALU = mybir.AluOpType
ACT = mybir.ActivationFunctionType
AX = mybir.AxisListType

LOWEST = [7.0 if s == 0 else 1.0 for s in SHIFTS]

L0_COLS = ["Wq", "Wk", "Wv", "Wo", "Wf1", "Wf2", "bq", "bk", "bv", "bo", "s1", "b1", "bf2", "s2", "b2", "bf1"]
L0_WIDTH = dict(Wq=P, Wk=P, Wv=P, Wo=P, Wf1=FF, Wf2=FF, bf1=NF)


def columns(names, width):
    at, out = 0, {}
    for n in names:
        w = width.get(n, 1)
        out[n] = (at, at + w)
        at += w
    return out, at


L0_AT, L0_N = columns(L0_COLS, L0_WIDTH)
C_WIDTH = dict(row_ok=SLOTS - T, ident=P, cent=P, mean=P, one=P, shift_r=32, shift_l=32, block8=P, kk=len(SHIFTS),
               pick=2 * P, diag4=4 * DH, lower=E * E)
C_AT, C_N = columns(["ident", "cent", "mean", "one", "shift_r", "shift_l", "big_first", "init0", "bnd_last", "row_ok",
                     "block8", "kk", "pick", "lower", "diag4"], C_WIDTH)
G_WIDTH = dict(ctxT=B * T, wg=E, bg=E, W1=E * HID, W2=2 * P, b1=2, b2=P, aWq=P, aWk=P, aWv=P, aWo=P,
               conv_w=3 * H, conv_b=H, xWq=P, xWk=P, xWv=P, xbv=P, fW1=FF, fW2=FF, fb1=NF, ph=NF, wr=NF, wi=NF)
G_AT, G_N = columns(["ctxT", "wg", "bg", "W1", "W2", "b1", "b2", "aWq", "aWk", "aWv", "aWo", "abq", "abk", "abv",
                     "abo", "conv_w", "conv_b", "xWq", "xWk", "xWv", "xbq", "xbk", "xbv", "fW1", "fW2", "fb1", "ph",
                     "wr", "wi", "fb2"], G_WIDTH)


def constants():
    c = np.zeros((P, C_N), np.float32)

    def put(name, a):
        lo, hi = C_AT[name]
        c[:a.shape[0], lo:hi] = a

    put("ident", np.eye(P))
    put("cent", np.eye(P) - 1.0 / P)
    put("mean", np.full((P, P), 1.0 / P))
    put("one", np.ones((P, P)))
    r, l = np.zeros((32, 32)), np.zeros((32, 32))
    big, init0, last = np.zeros((32, 1)), np.full((32, 1), BIG), np.ones((32, 1))
    for b in range(B):
        for k in range(BLK):
            p = b * BLK + BLK - 1 - k
            if k + 1 < BLK:
                r[p, p - 1] = 1
                l[p - 1, p] = 1
        big[b * BLK + BLK - 1] = BIG
        init0[b * BLK + BLK - 1] = 0
        last[b * BLK] = 0
    put("shift_r", r)
    put("shift_l", l)
    put("big_first", big)
    put("init0", init0)
    put("bnd_last", last)
    ok = np.zeros((32, SLOTS - T))
    for p in range(32):
        k = BLK - 1 - p % BLK
        ok[p] = np.arange(T, SLOTS) - LAG * k < T
    put("row_ok", ok)
    put("block8", np.kron(np.eye(P // 8), np.ones((8, 8))))
    kk = np.array([[(p % 8) << s if s or p % 8 < 2 else 0 for s in SHIFTS] for p in range(P)], np.int32)
    put("kk", kk.view(np.float32))
    pick = np.zeros((P, 2, P))
    for b in range(B):
        for e in range(E):
            pick[b * 64 + e * 8, e // 4, (e % 4) * HID:(e % 4 + 1) * HID] = 1
    put("pick", pick.reshape(P, 2 * P))
    put("lower", np.broadcast_to(np.tril(np.ones((E, E)), -1).reshape(1, E * E), (P, E * E)))
    put("diag4", np.kron(np.eye(4), np.ones((P // 4, DH))))
    return c


class Shared:
    pass


def build(nc, a):
    with ExitStack() as ctx:
        sems = {}

        def sem(name):
            assert name not in sems, len(sems)
            sems[name] = ctx.enter_context(nc.semaphore(name))
            return sems[name]

        def sem_set(prefix, names):
            return namedtuple("Semaphores", names)(*(sem(f"{prefix}_{n}") for n in names.split()))

        def sb(name, shape, dt=F32, stack=ctx):
            return stack.enter_context(nc.sbuf_tensor(name, shape, dt))

        g = Shared()
        g.c = sb("consts", [P, C_N])
        g.w = sb("params", [P, G_N])
        g.xT = sb("xT", [P, B, S])
        g.nT = sb("nT", [P, B, S])
        g.ctx = sb("ctx", [T, B, P])
        g.eps6 = sb("eps6", [P, 1])
        g.eps5 = sb("eps5", [P, 1])
        g.sq = sb("sq", [P, B, S])
        g.rs = sb("rs", [P, B, S])
        g.psum = ctx.enter_context(nc.psum_tensor("banks", [P, 8, 512], F32))
        g.ps = [g.psum[:, i] for i in range(8)]
        g.sem, g.sem_set, g.sb = sem, sem_set, sb
        g.C = lambda n: g.c[:, C_AT[n][0]:C_AT[n][1]]
        g.G = lambda n: g.w[:, G_AT[n][0]:G_AT[n][1]]
        g.loaded = sem("params_loaded")
        g.ln, g.norms = sem_set("ln", LN_SEMS), 0
        with ExitStack() as early:
            g.wt = sb("l0_params", [P, 2, L0_N], stack=early)
            g.wt_loaded = sem_set("l0_params", "w0 w1")
            load_stage(nc, a, g)
            l0_stage(nc, a, g)
        dtw_stage(nc, a, g)
        moe_stage(nc, a, g)
        attn_stage(nc, a, g)
        xattn_stage(nc, a, g)
        ffn_stage(nc, a, g)
        store_stage(nc, a, g)


def ln_act_square(nc, act, g, s, n, bank_c, sq):
    act.wait_ge(s.cen, n)
    nc.scalar.activation(sq, bank_c, ACT.Square).then_inc(s.sq, 1)


def ln_act_rstd(nc, act, g, s, n, bank_v, sq, rs, eps):
    act.wait_ge(s.var, n)
    nc.scalar.activation(sq, bank_v, ACT.Ln, bias=eps[:]).then_inc(s.ln, 1)
    act.wait_ge(s.ln, n)
    nc.scalar.activation(rs, sq, ACT.Exp, scale=-0.5).then_inc(s.rs, 1)


LN_SET = "natural_log_exp_and_others"
LN_SEMS = "cen sq var ln rs"


def ln_block(nc, g, dve_first=None):
    s, n0 = g.ln, g.norms * B
    g.norms += 1
    with nc.Block() as block:
        @block.tensor
        def _(pe):
            for b in range(B):
                nc.tensor.matmul(g.ps[b], g.C("cent"), g.xT[:, b], start=True, stop=True).then_inc(s.cen, 1)
            for b in range(B):
                pe.wait_ge(s.sq, n0 + b + 1)
                nc.tensor.matmul(g.ps[2 + b], g.C("mean"), g.sq[:, b], start=True, stop=True).then_inc(s.var, 1)

        @block.scalar
        def _(act):
            nc.scalar.preload_act_table_set(LN_SET)
            for b in range(B):
                ln_act_square(nc, act, g, s, n0 + b + 1, g.ps[b], g.sq[:, b])
            for b in range(B):
                ln_act_rstd(nc, act, g, s, n0 + b + 1, g.ps[2 + b], g.sq[:, b], g.rs[:, b], g.eps5)

        @block.vector
        def _(dve):
            if dve_first:
                dve_first(dve)
            for b in range(B):
                dve.wait_ge(s.rs, n0 + b + 1)
                nc.vector.tensor_tensor(g.nT[:, b], g.ps[b], g.rs[:, b], ALU.mult)


def load_stage(nc, a, g):
    with ExitStack() as st:
        xn = g.sb("x_rows", [P, B * NC, P], stack=st)
        s = g.sem_set("load", "x consts ctx turned")
        g.ctx_loaded = s.ctx
        with nc.Block() as block:
            @block.sync
            def _(sp):
                sp.dma_start(xn[:], a["x"].rearrange("b (c p) d -> p (b c) d", p=P)).then_inc(s.x, 16)
                sp.dma_start(g.wt[:, 0], a["l0"][0]).then_inc(g.wt_loaded.w0, 16)
                sp.dma_start(g.wt[:, 1], a["l0"][1]).then_inc(g.wt_loaded.w1, 16)
                sp.dma_start(g.w[:], a["params"]).then_inc(g.loaded, 16)
                sp.dma_start(g.ctx[:], a["ctx"].rearrange("b t d -> t b d")).then_inc(s.ctx, 16)

            @block.scalar
            def _(act):
                act.dma_start(g.c[:], a["consts"]).then_inc(s.consts, 16)

            @block.tensor
            def _(pe):
                pe.wait_ge(s.x, 16)
                pe.wait_ge(s.consts, 16)
                for b in range(B):
                    for c in range(NC):
                        last = nc.tensor.transpose(g.ps[b][:, c * P:(c + 1) * P], xn[:, b * NC + c, :], g.C("ident"))
                    last.then_inc(s.turned, 1)

            @block.vector
            def _(dve):
                nc.vector.memset(g.eps6[:], 1e-6)
                nc.vector.memset(g.eps5[:], 1e-5)
                for b in range(B):
                    dve.wait_ge(s.turned, b + 1)
                    nc.vector.tensor_copy(g.xT[:, b], g.ps[b][:])
    ln_block(nc, g)


def l0_stage(nc, a, g):
    with ExitStack() as st:
        def sb(name, shape, dt=F32):
            return g.sb("l0_" + name, shape, dt, stack=st)

        LOOP = 2 * 2
        wt, (w0, w1) = g.wt, g.wt_loaded
        x = sb("x", [P, B, S])
        x1 = sb("x1", [P, B, S])
        eq, rq, ek, rk = (sb(n, [P, S]) for n in ("eq", "rq", "ek", "rk"))
        Q, K, V, den, rec, junk = (sb(n, [P, S]) for n in ("Q", "K", "V", "den", "rec", "junk"))
        go, r1, gf, r2, u1, u2, ccF = (sb(n, [P, S]) for n in ("go", "r1", "gf", "r2", "u1", "u2", "cc"))
        h = sb("h", [P, NF, S])
        ksum, kv = sb("ksum", [P, 1]), sb("kv", [P, 1])
        s = g.sem_set("l0", "q k v eq ek mkq Q K den rec V o go r1 h1 hg f2 gf r2 x u1 x1 u2 cc")
        nA, nF = g.sem_set("l0a", LN_SEMS), g.sem_set("l0f", LN_SEMS)
        bQ, bK, bV = g.ps[0:3]
        bH = g.ps[3:7]
        HALF = S // 2
        cols = [slice(u * HALF, (u + 1) * HALF) for u in range(2)]
        bF = (g.ps[7], bH[0])
        bO, cA, vA = (bQ, bK), (bH[1], bV), (bK, bQ)
        cF, vF = (bH[2], bH[3]), bF
        sqA, sqF, rsA, rsF = g.sq[:, 0], g.sq[:, 1], g.rs[:, 0], g.rs[:, 1]

        def slots(j):
            return j // 2 % 2, (j - 1) // 2 % 2

        def wcol(u, n):
            return wt[:, u, L0_AT[n][0]:L0_AT[n][1]]

        def halves(eng, half):
            half(0, 0, True, False)
            with eng.Fori(0, LAYERS // 2 - 1) as i:
                for j in range(1, LOOP + 1):
                    half(i * LOOP, j, True, True)
            for j in range(1, LOOP + 1):
                half((LAYERS // 2 - 1) * LOOP, j, j < LOOP, True)

        with nc.Block() as block:
            @block.sync
            def _(sp):
                with sp.Fori(0, LAYERS // 2 - 1) as i:
                    for l in range(2):
                        sp.wait_ge(s.x, i * (2 * LOOP) + (6 + 4 * l))
                        sp.dma_start(wt[:, l], a["l0"][bass.ds(i * 2 + (l + 2), 1)].rearrange("o p n -> p (o n)")
                                     ).then_inc((w0, w1)[l], 16)
                sp.wait_ge(g.ctx_loaded, 16)
                sp.wait_ge(g.loaded, 16)

            @block.tensor
            def _(pe):
                def half(i, j, A, F):
                    ua, uf = slots(j)
                    if A:
                        if j % 2 == 0:
                            pe.wait_ge((w0, w1)[ua], i * (16 // LOOP) + (16 * (j // 4 + 1)))
                        pe.wait_ge(s.x, i * 2 + (2 * j) if j else 1)
                        xa = x[:, j % 2]
                        if j:
                            pe.wait_ge(nA.ln, i * 2 + (2 * j - 1))
                        nc.tensor.matmul(bK, wcol(ua, "Wk"), xa, start=True, stop=True).then_inc(s.k, 1)
                        if j:
                            pe.wait_ge(nA.ln, i * 2 + (2 * j))
                        nc.tensor.matmul(bQ, wcol(ua, "Wq"), xa, start=True, stop=True).then_inc(s.q, 1)
                    if F:
                        pe.wait_ge(s.x1, i * 2 + 2 * j)
                        pe.wait_ge(s.x, i * 2 + (2 * j))
                    if A:
                        nc.tensor.matmul(bV, wcol(ua, "Wv"), xa, start=True, stop=True).then_inc(s.v, 1)
                    if F:
                        for f in range(NF):
                            nc.tensor.matmul(bH[f], wcol(uf, "Wf1")[:, f * P:(f + 1) * P], x1[:, (j + 1) % 2],
                                             start=True, stop=True).then_inc(s.h1, 1)
                    if F:
                        for u in range(2):
                            for f in range(NF):
                                if u == 0:
                                    pe.wait_ge(s.hg, i * NF + (NF * (j - 1) + f + 1))
                                last = nc.tensor.matmul(bF[u][:, cols[u]], wcol(uf, "Wf2")[:, f * P:(f + 1) * P],
                                                        h[:, f, cols[u]], start=(f == 0), stop=(f == NF - 1))
                            last.then_inc(s.f2, 1)
                    if A:
                        for u in range(2):
                            pe.wait_ge(s.V, i * 2 + (2 * j + u + 1))
                            nc.tensor.matmul(bO[u][:, cols[u]], wcol(ua, "Wo"), V[:, cols[u]], start=True, stop=True
                                             ).then_inc(s.o, 1)
                    if F:
                        for u in range(2):
                            pe.wait_ge(s.r2, i * 2 + (2 * j + u - 1))
                            nc.tensor.matmul(cF[u][:, cols[u]], g.C("cent"), r2[:, cols[u]], start=True, stop=True
                                             ).then_inc(nF.cen, 1)
                    if A:
                        for u in range(2):
                            pe.wait_ge(s.r1, i * 2 + (2 * j + u + 1))
                            nc.tensor.matmul(cA[u][:, cols[u]], g.C("cent"), r1[:, cols[u]], start=True, stop=True
                                             ).then_inc(nA.cen, 1)
                    if F:
                        for u in range(2):
                            pe.wait_ge(nF.sq, i * 2 + (2 * j + u - 1))
                            nc.tensor.matmul(vF[u][:, cols[u]], g.C("mean"), sqF[:, cols[u]], start=True, stop=True
                                             ).then_inc(nF.var, 1)
                    if A:
                        for u in range(2):
                            pe.wait_ge(nA.sq, i * 2 + (2 * j + u + 1))
                            nc.tensor.matmul(vA[u][:, cols[u]], g.C("mean"), sqA[:, cols[u]], start=True, stop=True
                                             ).then_inc(nA.var, 1)

                halves(pe, half)

            @block.scalar
            def _(act):
                def rstd(n, at, bank, t, rs):
                    for u in range(2):
                        act.wait_ge(n.var, at + u)
                        nc.scalar.activation(t[:, cols[u]], bank[u][:, cols[u]], ACT.Ln, bias=g.eps6[:]
                                             ).then_inc(n.ln, 1)
                    for u in range(2):
                        act.wait_ge(n.ln, at + u)
                        nc.scalar.activation(rs[:, cols[u]], t[:, cols[u]], ACT.Exp, scale=-0.5).then_inc(n.rs, 1)

                def half(i, j, A, F):
                    ua, uf = slots(j)
                    if A:
                        for src, sg, e_, r_, bias, out in ((bK, s.k, ek, rk, "bk", s.ek), (bQ, s.q, eq, rq, "bq", s.eq)):
                            act.wait_ge(sg, i + (j + 1))
                            nc.scalar.activation(e_[:], src, ACT.Exp, bias=wcol(ua, bias))
                            nc.scalar.activation(r_[:], src, ACT.Relu, bias=wcol(ua, bias)).then_inc(out, 1)
                    nc.scalar.preload_act_table(ACT.Gelu_apprx_tanh)
                    if F:
                        for f in range(NF):
                            act.wait_ge(s.h1, i * NF + (NF * (j - 1) + f + 1))
                            nc.scalar.activation(h[:, f], bH[f], ACT.Gelu_apprx_tanh, bias=wcol(uf, "bf1")[:, f:f + 1]
                                                 ).then_inc(s.hg, 1)
                        for u in range(2):
                            act.wait_ge(s.f2, i * 2 + (2 * j + u - 1))
                            nc.scalar.activation(gf[:, cols[u]], bF[u][:, cols[u]], ACT.Gelu_apprx_tanh,
                                                 bias=wcol(uf, "bf2")).then_inc(s.gf, 1)
                    if A:
                        for u in range(2):
                            act.wait_ge(s.o, i * 2 + (2 * j + u + 1))
                            nc.scalar.activation(go[:, cols[u]], bO[u][:, cols[u]], ACT.Gelu_apprx_tanh,
                                                 bias=wcol(ua, "bo")).then_inc(s.go, 1)
                    nc.scalar.preload_act_table_set(LN_SET)
                    if A:
                        for u in range(2):
                            ln_act_square(nc, act, g, nA, i * 2 + (2 * j + u + 1), cA[u][:, cols[u]], sqA[:, cols[u]])
                    if F:
                        rstd(nF, i * 2 + (2 * j - 1), vF, sqF, rsF)
                    if A:
                        rstd(nA, i * 2 + (2 * j + 1), vA, sqA, rsA)

                nc.scalar.preload_act_table_set(LN_SET)
                halves(act, half)

            @block.vector
            def _(dve):
                def half(i, j, A, F):
                    ua, uf = slots(j)
                    if A:
                        n = i + (j + 1)
                        dve.wait_ge(s.ek, n)
                        nc.vector.tensor_scalar(ek[:], ek[:], 1.0, -1.0, ALU.min, ALU.add).then_inc(s.mkq, 1)
                        dve.wait_ge(s.mkq, n * 2 - 1)
                        nc.vector.scalar_tensor_tensor(out=K[:], in0=ek[:], scalar=1.0, in1=rk[:], op0=ALU.add,
                                                       op1=ALU.add, accum_out=ksum[:]).then_inc(s.K, 1)
                        dve.wait_ge(s.eq, n)
                        nc.vector.tensor_scalar(eq[:], eq[:], 1.0, -1.0, ALU.min, ALU.add).then_inc(s.mkq, 1)
                        dve.wait_ge(s.mkq, n * 2)
                        nc.vector.scalar_tensor_tensor(out=Q[:], in0=eq[:], scalar=1.0, in1=rq[:], op0=ALU.add,
                                                       op1=ALU.add).then_inc(s.Q, 1)
                        dve.wait_ge(s.Q, n)
                        dve.wait_ge(s.K, n)
                        nc.vector.tensor_scalar(den[:], Q[:], ksum[:], 1e-6, ALU.mult, ALU.add).then_inc(s.den, 1)
                        dve.wait_ge(s.v, n)
                        nc.vector.scalar_tensor_tensor(out=junk[:], in0=bV, scalar=wcol(ua, "bv"), in1=K[:],
                                                       op0=ALU.add, op1=ALU.mult, accum_out=kv[:]).then_inc(s.den, 1)
                        dve.wait_ge(s.den, n * 2 - 1)
                        for u in range(2):
                            nc.vector.reciprocal(rec[:, cols[u]], den[:, cols[u]]).then_inc(s.rec, 1)
                        dve.wait_ge(s.den, n * 2)
                        for u in range(2):
                            dve.wait_ge(s.rec, i * 2 + (2 * j + u + 1))
                            nc.vector.scalar_tensor_tensor(out=V[:, cols[u]], in0=Q[:, cols[u]], scalar=kv[:],
                                                           in1=rec[:, cols[u]], op0=ALU.mult, op1=ALU.mult
                                                           ).then_inc(s.V, 1)
                    if F:
                        for u in range(2):
                            dve.wait_ge(s.gf, i * 2 + (2 * j + u - 1))
                            nc.vector.tensor_tensor(r2[:, cols[u]], gf[:, cols[u]], x1[:, (j + 1) % 2, cols[u]],
                                                    ALU.add).then_inc(s.r2, 1)
                    if A:
                        for u in range(2):
                            dve.wait_ge(s.go, i * 2 + (2 * j + u + 1))
                            nc.vector.tensor_tensor(r1[:, cols[u]], go[:, cols[u]], x[:, j % 2, cols[u]], ALU.add
                                                    ).then_inc(s.r1, 1)
                    if F:
                        for u in range(2):
                            dve.wait_ge(nF.cen, i * 2 + (2 * j + u - 1))
                            nc.vector.tensor_copy(ccF[:, cols[u]], cF[u][:, cols[u]]).then_inc(s.cc, 1)
                        for u in range(2):
                            dve.wait_ge(s.cc, i * 2 + (2 * j + u - 1))
                            nc.vector.tensor_tensor(sqF[:, cols[u]], ccF[:, cols[u]], ccF[:, cols[u]], ALU.mult
                                                    ).then_inc(nF.sq, 1)
                        for u in range(2):
                            dve.wait_ge(nF.rs, i * 2 + (2 * j + u - 1))
                            nc.vector.tensor_tensor(u2[:, cols[u]], ccF[:, cols[u]], rsF[:, cols[u]], ALU.mult
                                                    ).then_inc(s.u2, 1)
                        for u in range(2):
                            dve.wait_ge(s.u2, i * 2 + (2 * j + u - 1))
                            nc.vector.tensor_scalar(x[:, (j + 1) % 2, cols[u]], u2[:, cols[u]], wcol(uf, "s2"),
                                                    wcol(uf, "b2"), ALU.mult, ALU.add).then_inc(s.x, 1)
                    if A:
                        for u in range(2):
                            dve.wait_ge(nA.rs, i * 2 + (2 * j + u + 1))
                            nc.vector.tensor_tensor(u1[:, cols[u]], cA[u][:, cols[u]], rsA[:, cols[u]], ALU.mult
                                                    ).then_inc(s.u1, 1)
                        for u in range(2):
                            dve.wait_ge(s.u1, i * 2 + (2 * j + u + 1))
                            nc.vector.tensor_scalar(x1[:, j % 2, cols[u]], u1[:, cols[u]], wcol(ua, "s1"),
                                                    wcol(ua, "b1"), ALU.mult, ALU.add).then_inc(s.x1, 1)

                for b in range(B):
                    nc.vector.tensor_copy(x[:, b], g.nT[:, b]).then_inc(s.x, 1)
                halves(dve, half)
                dve.wait_ge(s.x, 4 * LAYERS + B)
                for b in range(B):
                    nc.vector.tensor_tensor(g.xT[:, b], g.xT[:, b], x[:, b], ALU.add)


def dtw_stage(nc, a, g):
    ln_block(nc, g)
    with ExitStack() as st:
        def sb(name, shape, dt=F32):
            return g.sb("dtw_" + name, shape, dt, stack=st)

        rows = T + 2 * PAD
        scr_d = [nc.dram_tensor(f"scratch_dist{b}", (rows, S), F32, kind="Internal").ap() for b in range(B)]
        scr_p = [nc.dram_tensor(f"scratch_path{b}", (rows, S), F32, kind="Internal").ap() for b in range(B)]
        ctx2 = sb("ctx2", [P, B * T])
        nsq = sb("nsq", [P, B, S])
        junk, aa = sb("junk", [T, P]), sb("aa", [T, B])
        d2, dist = sb("d2", [T, B, S]), sb("dist", [T, B, S])
        zero = sb("zero", [PAD, S])
        D = sb("D", [32, SLOTS, W])
        R = sb("R", [32, SLOTS + 1, W + 1])
        q = sb("q", [32, SLOTS, W])
        isq, isn, nu = (sb(n, [32, SLOTS, W], BF16) for n in ("diag_le_up", "not_left", "up_less_1"))
        dg = sb("diag", [32, SLOTS, W + 1], BF16)
        theta = sb("theta", [32, SLOTS, W], BF16)
        I = sb("I", [32, SLOTS + 1, W + 1], BF16)
        X = sb("X", [32, SLOTS, W], BF16)
        t1, t2, t3 = isq, isn, nu
        path = sb("path", [32, SLOTS, W])
        shl = sb("shift_l", [32, 32], BF16)
        pn = sb("path_rows", [T, B, S])
        s = g.sem_set("dtw", "nsq ctx2 aa dd d2 dist zero stored D0 D1 q R edge Redge big isq isn dg nu dgs dge theta "
                             "X I Iedge t1 t2 t3 P pst pn ex")
        CH = 4
        NCH = -(-SLOTS // CH)
        PIECES = [(0, 20), (20, SLOTS)]
        STORES = [(13, NCH), (3, 13), (0, 3)]

        def span(c):
            return c * CH, min((c + 1) * CH, SLOTS)

        def skewed(scr, lo, hi):
            return bass.AP(tensor=scr.tensor, offset=scr.offset + W * (BLK - 1) + S * lo,
                           ap=[[LAG * S - W, BLK], [S, hi - lo], [1, W]])

        psR, psI, psD = g.ps[0:2], g.ps[5:7], g.ps[3:5]
        psG = psI

        with nc.Block() as block:
            @block.scalar
            def _(act):
                def diag_edge(c):
                    lo, hi = span(c)
                    lo = max(lo, LAG)
                    act.wait_ge(s.dgs, c + 1)
                    nc.scalar.activation(dg[:, lo - LAG:hi - LAG, W], psG[c % 2][0:32, lo:hi], ACT.Identity
                                         ).then_inc(s.dge, 1)

                for b in range(B):
                    nc.scalar.activation(nsq[:, b], g.nT[:, b], ACT.Square).then_inc(s.nsq, 1)
                nc.scalar.preload_act_table(ACT.Sqrt)
                for b in range(B):
                    act.wait_ge(s.d2, b + 1)
                    nc.scalar.activation(dist[:, b], d2[:, b], ACT.Sqrt).then_inc(s.dist, 1)
                for t in range(SLOTS - LAG):
                    if t >= CH and t % CH == 2:
                        diag_edge(t // CH - 1)
                    act.wait_ge(s.edge, t + 1)
                    nc.scalar.activation(R[:, t + LAG + 1, 0:1], psR[t % 2][0:32, t:t + 1], ACT.Identity,
                                         bias=g.C("big_first")[0:32]).then_inc(s.Redge, 1)
                for c in range(NCH - 2, NCH):
                    diag_edge(c)

            @block.tensor
            def _(pe):
                def diag_shift(c):
                    lo, hi = span(c)
                    pe.wait_ge(s.dg, c + 1)
                    if c >= 2:
                        pe.wait_ge(s.dge, c - 1)
                    nc.tensor.matmul(psG[c % 2][0:32, lo:hi], shl[:], dg[:, lo:hi, 0], start=True, stop=True
                                     ).then_inc(s.dgs, 1)

                pe.wait_ge(s.ctx2, 1)
                for b in range(B):
                    pe.wait_ge(s.nsq, b + 1)
                    nc.tensor.matmul(psD[b][0:T, :], g.C("one")[:, 0:T], nsq[:, b], start=True, stop=False)
                    nc.tensor.matmul(psD[b][0:T, :], ctx2[:, b * T:(b + 1) * T], g.nT[:, b], start=False, stop=True
                                     ).then_inc(s.dd, 1)
                for t in range(SLOTS - LAG):
                    if t >= CH and t % CH == 2:
                        diag_shift(t // CH - 1)
                    pe.wait_ge(s.R, t + 1)
                    nc.tensor.matmul(psR[t % 2][0:32, t:t + 1], g.C("shift_r")[0:32], R[:, t + 1, W:W + 1],
                                     start=True, stop=True).then_inc(s.edge, 1)
                for c in range(NCH - 2, NCH):
                    diag_shift(c)

            @block.vector
            def _(dve):
                def diag_le_up(c):
                    lo, hi = span(c)
                    nc.vector.tensor_tensor(isq[:, lo:hi], R[:, lo:hi, 0:W], R[:, lo:hi, 1:W + 1], ALU.is_le
                                            ).then_inc(s.isq, 1)

                def not_left(c):
                    lo, hi = span(c)
                    nc.vector.tensor_tensor(isn[:, lo:hi], q[:, lo:hi], R[:, lo + 1:hi + 1, 0:W], ALU.is_le
                                            ).then_inc(s.isn, 1)

                def diagonal(c):
                    lo, hi = span(c)
                    dve.wait_ge(s.isq, c + 1)
                    dve.wait_ge(s.isn, c + 1)
                    nc.vector.tensor_tensor(dg[:, lo:hi, 0:W], isq[:, lo:hi], isn[:, lo:hi], ALU.mult
                                            ).then_inc(s.dg, 1)

                def up_less_1(c):
                    lo, hi = span(c)
                    dve.wait_ge(s.dg, c + 1)
                    nc.vector.scalar_tensor_tensor(out=nu[:, lo:hi], in0=isn[:, lo:hi], scalar=1.0,
                                                   in1=dg[:, lo:hi, 0:W], op0=ALU.subtract, op1=ALU.subtract
                                                   ).then_inc(s.nu, 1)

                def thresholds(c):
                    lo, hi = span(c)
                    dve.wait_ge(s.nu, c + 1)
                    dve.wait_ge(s.dge, min(c + 2, NCH))
                    nc.vector.scalar_tensor_tensor(out=theta[:, lo:hi], in0=dg[:, lo:hi, 1:W + 1], scalar=2.0,
                                                   in1=nu[:, lo:hi], op0=ALU.subtract, op1=ALU.mult
                                                   ).then_inc(s.theta, 1)

                nc.vector.tensor_scalar(ctx2[:], g.G("ctxT"), -2.0, None, ALU.mult).then_inc(s.ctx2, 1)
                nc.vector.memset(zero[:], 0.0).then_inc(s.zero, 1)
                for b in range(B):
                    if b:
                        dve.wait_ge(s.aa, b)
                    nc.vector.scalar_tensor_tensor(out=junk[:], in0=g.ctx[:, b], scalar=1.0, in1=g.ctx[:, b],
                                                   op0=ALU.mult, op1=ALU.mult, accum_out=aa[:, b:b + 1]
                                                   ).then_inc(s.aa, 1)
                dve.wait_ge(s.aa, B)
                for b in range(B):
                    dve.wait_ge(s.dd, b + 1)
                    nc.vector.tensor_scalar(d2[:, b], psD[b][0:T, :], aa[:, b:b + 1], 0.0, ALU.add, ALU.max
                                            ).then_inc(s.d2, 1)
                nc.vector.tensor_copy(shl[:], g.C("shift_l")[0:32])
                nc.vector.memset(dg[:, :, W:W + 1], 0.0)
                nc.vector.memset(I[:, SLOTS, 0:W], 1.0)
                for t in range(SLOTS, SLOTS - LAG - 1, -1):
                    nc.vector.tensor_copy(I[:, t, W:W + 1], g.C("bnd_last")[0:32])
                nc.vector.memset(R[:, 0, :], BIG)
                nc.vector.memset(R[:, 1:LAG + 1, 0:1], BIG).then_inc(s.big, 1)
                dve.wait_ge(s.big, 1)
                for t in range(SLOTS):
                    if t == PIECES[0][0]:
                        dve.wait_ge(s.D0, 16 * B)
                    if t == PIECES[1][0]:
                        dve.wait_ge(s.D1, 16 * B)
                    if t >= 1:
                        dve.wait_ge(s.R, t)
                    nc.vector.tensor_tensor(q[:, t], R[:, t, 0:W], R[:, t, 1:W + 1], ALU.min).then_inc(s.q, 1)
                    if t >= CH:
                        (diag_le_up, not_left, diagonal, up_less_1)[t % CH](t // CH - 1)
                    dve.wait_ge(s.q, t + 1)
                    if t >= LAG:
                        dve.wait_ge(s.Redge, t - LAG + 1)
                    first = g.C("init0")[0:32] if t == 0 else R[:, t + 1, 0:1]
                    nc.vector.tensor_tensor_scan(R[:, t + 1, 1:W + 1], q[:, t], D[:, t], first, ALU.min, ALU.add
                                                 ).then_inc(s.R, 1)
                    if t >= 3 * CH and t % CH == 0:
                        thresholds(t // CH - 3)
                dve.wait_ge(s.R, SLOTS)
                up_less_1(NCH - 2)
                diag_le_up(NCH - 1)
                not_left(NCH - 1)
                diagonal(NCH - 1)
                up_less_1(NCH - 1)
                for c in range(NCH - 3, NCH):
                    thresholds(c)
                dve.wait_ge(s.theta, NCH)
                nc.vector.tensor_tensor(theta[:, T:SLOTS], theta[:, T:SLOTS],
                                        g.C("row_ok")[0:32].unsqueeze(2).broadcast_to([32, SLOTS - T, W]), ALU.mult)

            @block.sync
            def _(sp):
                sp.wait_ge(s.zero, 1)
                for b in range(B):
                    sp.dma_start(scr_d[b][0:PAD, :], zero[:]).then_inc(s.stored, 16)
                    sp.dma_start(scr_d[b][PAD + T:rows, :], zero[:]).then_inc(s.stored, 16)
                for b in range(B):
                    sp.wait_ge(s.dist, b + 1)
                    sp.dma_start(scr_d[b][PAD:PAD + T, :], dist[:, b]).then_inc(s.stored, 16)
                sp.wait_ge(s.stored, 16 * 3 * B)
                for (lo, hi), loaded in zip(PIECES, (s.D0, s.D1)):
                    for b in range(B):
                        sp.dma_start(D[b * BLK:(b + 1) * BLK, lo:hi], skewed(scr_d[b], lo, hi)).then_inc(loaded, 16)

        with nc.Block() as block:
            @block.vector
            def _(dve):
                def step_here(c):
                    lo, hi = span(c)
                    nc.vector.tensor_tensor(t1[:, lo:hi], I[:, lo:hi, 0:W], I[:, lo:hi, 1:W + 1], ALU.subtract
                                            ).then_inc(s.t1, 1)

                def right_diagonal(c):
                    lo, hi = span(c)
                    nc.vector.tensor_tensor(t2[:, lo:hi], dg[:, lo:hi, 1:W + 1], I[:, lo + 1:hi + 1, 1:W + 1], ALU.mult
                                            ).then_inc(s.t2, 1)

                def diagonal_leaves(c):
                    lo, hi = span(c)
                    dve.wait_ge(s.t1, NCH - c)
                    dve.wait_ge(s.t2, 2 * (NCH - c) - 1)
                    nc.vector.tensor_tensor(t2[:, lo:hi], t1[:, lo:hi], t2[:, lo:hi], ALU.mult).then_inc(s.t2, 1)

                def entered_between(c):
                    lo, hi = span(c)
                    nc.vector.tensor_tensor(t3[:, lo:hi], I[:, lo + 1:hi + 1, 0:W], I[:, lo:hi, 1:W + 1], ALU.subtract
                                            ).then_inc(s.t3, 1)

                def on_path(c):
                    lo, hi = span(c)
                    dve.wait_ge(s.t2, 2 * (NCH - c))
                    dve.wait_ge(s.t3, NCH - c)
                    nc.vector.tensor_tensor(path[:, lo:hi], t3[:, lo:hi], t2[:, lo:hi], ALU.subtract).then_inc(s.P, 1)

                for k, t in enumerate(range(SLOTS - 1, -1, -1)):
                    c = t // CH + 1
                    if k >= 1:
                        dve.wait_ge(s.I, k)
                    nc.vector.tensor_tensor(X[:, t], I[:, t + 1, 0:W], I[:, t + 1, 1:W + 1], ALU.add).then_inc(s.X, 1)
                    if c < NCH and t % CH:
                        (on_path, diagonal_leaves, step_here)[t % CH - 1](c)
                    dve.wait_ge(s.X, k + 1)
                    if k >= LAG:
                        dve.wait_ge(s.Iedge, k - LAG + 1)
                    nc.vector.tensor_tensor_scan(I[:, t, W - 1::-1], X[:, t, ::-1], theta[:, t, ::-1],
                                                 I[:, t, W:W + 1], ALU.add, ALU.is_gt).then_inc(s.I, 1)
                    if c < NCH and t % CH >= 2:
                        (entered_between, right_diagonal)[t % CH - 2](c)
                dve.wait_ge(s.I, SLOTS)
                for part in (step_here, right_diagonal, diagonal_leaves, entered_between, on_path):
                    part(0)
                for b in range(B):
                    dve.wait_ge(s.ex, b + 1)
                    nc.vector.tensor_tensor(g.xT[:, b], g.xT[:, b], psD[b], ALU.add)

            @block.tensor
            def _(pe):
                for k, t in enumerate(range(SLOTS - 1, LAG - 1, -1)):
                    pe.wait_ge(s.I, k + 1)
                    nc.tensor.matmul(psI[t % 2][0:32, t:t + 1], shl[:], I[:, t, 0:1], start=True, stop=True
                                     ).then_inc(s.edge, 1)
                for b in range(B):
                    pe.wait_ge(s.pn, 16 * B)
                    nc.tensor.matmul(psD[b], g.ctx[:, b], pn[:, b], start=True, stop=True).then_inc(s.ex, 1)

            @block.scalar
            def _(act):
                for k, t in enumerate(range(SLOTS - 1, LAG - 1, -1)):
                    act.wait_ge(s.edge, SLOTS - LAG + k + 1)
                    nc.scalar.activation(I[:, t - LAG, W:W + 1], psI[t % 2][0:32, t:t + 1], ACT.Identity
                                         ).then_inc(s.Iedge, 1)

            @block.sync
            def _(sp):
                for c0, c1 in STORES:
                    sp.wait_ge(s.P, NCH - c0)
                    lo, hi = span(c0)[0], span(c1 - 1)[1]
                    for b in range(B):
                        sp.dma_start(skewed(scr_p[b], lo, hi), path[b * BLK:(b + 1) * BLK, lo:hi]).then_inc(s.pst, 16)
                sp.wait_ge(s.pst, 16 * B * len(STORES))
                for b in range(B):
                    sp.dma_start(pn[:, b], scr_p[b][PAD:PAD + T, :]).then_inc(s.pn, 16)


def moe_stage(nc, a, g):
    ln_block(nc, g)
    with ExitStack() as st:
        def sb(name, shape, dt=F32):
            return g.sb("moe_" + name, shape, dt, stack=st)

        N = B * NC
        lg, ex, mx = sb("lg", [P, N, E]), sb("ex", [P, N, E]), sb("mx", [P, N])
        sm, rsm, sc = sb("sm", [P, N]), sb("rsm", [P, N]), sb("sc", [P, N, E])
        gt, ge = sb("gt", [P, N * E, E]), sb("ge", [P, N * E, E])
        rank, top = sb("rank", [P, N * E]), sb("top", [P, N, E])
        den, rden, route = sb("den", [P, NC, E]), sb("rden", [P, NC, E]), sb("route", [P, NC, B, E])
        route8 = sb("route8", [P, NC, B * E * 8])
        v = sb("v", [P, S])
        hit = sb("hit", [P, S])
        cnt, enough, pick_i = sb("cnt", [P, 1]), sb("enough", [P, 1], BF16), sb("pick_i", [P, 1], I32)
        low, thr, base = (sb(n, [P, 1], I32) for n in ("low", "thr", "base"))
        above, eqm, run, chosen = sb("above", [P, S]), sb("eqm", [P, S]), sb("run", [P, S]), sb("chosen", [P, S])
        room = sb("room", [P, 2])
        block8, pick16 = sb("block8", [P, P], BF16), sb("pick16", [P, 2 * P], BF16)
        chosen16 = sb("chosen16", [P, S], BF16)
        hT = sb("hT", [P, B, 2, S])
        s = g.sem_set("moe", "gate gates ex0 ex vps v low thr base cnt enough sum pick route8 "
                             "b8 above eqm run chosen h1 h mask hm out")
        psA, psV, psS = g.ps[0], g.ps[1], g.ps[2]
        kk = g.C("kk").bitcast(I32)
        NF_ = len(SHIFTS)
        with nc.Block() as block:
            @block.tensor
            def _(pe):
                for b in range(B):
                    for c in range(NC):
                        n = b * NC + c
                        last = nc.tensor.matmul(psA[:, n * E:(n + 1) * E], g.nT[:, b, c * P:(c + 1) * P], g.G("wg"),
                                                start=True, stop=True)
                last.then_inc(s.gate, 1)
                for b in range(B):
                    for k in range(2):
                        nc.tensor.matmul(g.ps[4 + 2 * b + k][:], g.G("W1")[:, k * P:(k + 1) * P], g.nT[:, b],
                                         start=True, stop=True).then_inc(s.h1, 1)
                pe.wait_ge(s.route8, 1)
                for c in range(NC):
                    last = nc.tensor.matmul(psV[:, c * P:(c + 1) * P], route8[:, c], g.C("ident"), start=True,
                                            stop=True)
                last.then_inc(s.vps, 1)
                pe.wait_ge(s.b8, 1)
                for n in range(NF_):
                    pe.wait_ge(s.enough, n + 1)
                    nc.tensor.matmul(psS[:, n:n + 1], block8[:], enough[:], start=True, stop=True).then_inc(s.sum, 1)
                pe.wait_ge(s.chosen, 1)
                pe.wait_ge(s.h, 4)
                for b in range(B):
                    rows = slice(b * 64, b * 64 + 64)
                    for k in range(2):
                        nc.tensor.matmul(g.ps[4 + 2 * b + k][:], pick16[rows, k * P:(k + 1) * P], chosen16[rows],
                                         start=True, stop=True).then_inc(s.mask, 1)
                pe.wait_ge(s.chosen, 2)
                for b in range(B):
                    rows = slice(b * 64, b * 64 + 64)
                    nc.tensor.matmul(g.ps[b][:], g.G("b2")[rows], chosen[rows], start=True, stop=False)
                    for k in range(2):
                        pe.wait_ge(s.hm, 2 * b + k + 1)
                        last = nc.tensor.matmul(g.ps[b][:], g.G("W2")[:, k * P:(k + 1) * P], hT[:, b, k],
                                                start=False, stop=(k == 1))
                    last.then_inc(s.out, 1)

            @block.scalar
            def _(act):
                act.wait_ge(s.ex0, 1)
                nc.scalar.activation(ex[:], lg[:], ACT.Exp).then_inc(s.ex, 1)
                for b in range(B):
                    for k in range(2):
                        act.wait_ge(s.h1, 2 * b + k + 1)
                        nc.scalar.activation(hT[:, b, k], g.ps[4 + 2 * b + k][:], ACT.Gelu,
                                             bias=g.G("b1")[:, k:k + 1]).then_inc(s.h, 1)

            @block.vector
            def _(dve):
                def bc(t, axis, shape):
                    return t.unsqueeze(axis).broadcast_to(shape)

                nc.vector.tensor_copy(pick16[:], g.C("pick"))
                nc.vector.tensor_copy(block8[:], g.C("block8")).then_inc(s.b8, 1)
                nc.vector.memset(low[:], 0).then_inc(s.low, 1)
                dve.wait_ge(s.gate, 1)
                nc.vector.tensor_tensor(lg[:], psA[:, 0:N * E].rearrange("p (n e) -> p n e", e=E),
                                        bc(g.G("bg"), 1, [P, N, E]), ALU.add).then_inc(s.gates, 1)
                dve.wait_ge(s.gates, 1)
                nc.vector.tensor_reduce(mx[:], lg[:], AX.X, ALU.max).then_inc(s.gates, 1)
                dve.wait_ge(s.gates, 2)
                nc.vector.tensor_tensor(lg[:], lg[:], bc(mx[:], 2, [P, N, E]), ALU.subtract).then_inc(s.ex0, 1)
                dve.wait_ge(s.ex, 1)
                nc.vector.tensor_reduce(sm[:], ex[:], AX.X, ALU.add).then_inc(s.gates, 1)
                dve.wait_ge(s.gates, 3)
                nc.vector.reciprocal(rsm[:], sm[:]).then_inc(s.gates, 1)
                dve.wait_ge(s.gates, 4)
                nc.vector.tensor_tensor(sc[:], ex[:], bc(rsm[:], 2, [P, N, E]), ALU.mult).then_inc(s.gates, 1)
                dve.wait_ge(s.gates, 5)
                mine = bc(sc[:].rearrange("p n e -> p (n e)"), 2, [P, N * E, E]).rearrange("p (n e) f -> p n e f", e=E)
                other = bc(sc[:], 2, [P, N, E, E])
                gt4, ge4 = (t[:].rearrange("p (n e) f -> p n e f", e=E) for t in (gt, ge))
                nc.vector.tensor_tensor(gt4, other, mine, ALU.is_gt)
                nc.vector.tensor_tensor(ge4, other, mine, ALU.is_ge).then_inc(s.gates, 1)
                dve.wait_ge(s.gates, 6)
                lower = bc(g.C("lower"), 1, [P, N, E * E])
                flat = lambda t: t[:].rearrange("p (n e) f -> p n (e f)", e=E)
                nc.vector.tensor_tensor(flat(ge), flat(ge), lower, ALU.mult).then_inc(s.gates, 1)
                dve.wait_ge(s.gates, 7)
                nc.vector.tensor_tensor(gt[:], gt[:], ge[:], ALU.max).then_inc(s.gates, 1)
                dve.wait_ge(s.gates, 8)
                nc.vector.tensor_reduce(rank[:], gt[:], AX.X, ALU.add).then_inc(s.gates, 1)
                dve.wait_ge(s.gates, 9)
                nc.vector.scalar_tensor_tensor(out=top[:].rearrange("p n e -> p (n e)"), in0=rank[:],
                                               scalar=float(TOPK), in1=sc[:].rearrange("p n e -> p (n e)"),
                                               op0=ALU.is_lt, op1=ALU.mult).then_inc(s.gates, 1)
                dve.wait_ge(s.gates, 10)
                nc.vector.scalar_tensor_tensor(out=den[:], in0=top[:, 0:NC], scalar=1.0, in1=top[:, NC:N],
                                               op0=ALU.mult, op1=ALU.add).then_inc(s.gates, 1)
                dve.wait_ge(s.gates, 11)
                nc.vector.tensor_scalar(den[:], den[:], 1e-6, None, ALU.add).then_inc(s.gates, 1)
                dve.wait_ge(s.gates, 12)
                nc.vector.reciprocal(rden[:], den[:]).then_inc(s.gates, 1)
                dve.wait_ge(s.gates, 13)
                for b in range(B):
                    last = nc.vector.scalar_tensor_tensor(out=route[:, :, b, :], in0=top[:, b * NC:(b + 1) * NC],
                                                          scalar=float(CAP), in1=rden[:], op0=ALU.mult, op1=ALU.mult)
                last.then_inc(s.gates, 1)
                dve.wait_ge(s.gates, 14)
                nc.vector.tensor_copy(route8[:].rearrange("p c (r k) -> p (c r) k", k=8),
                                      bc(route[:].rearrange("p c b e -> p (c b e)"), 2, [P, NC * B * E, 8])
                                      ).then_inc(s.route8, 1)
                dve.wait_ge(s.vps, 1)
                nc.vector.tensor_copy(v[:], psV[:]).then_inc(s.v, 1)
                dve.wait_ge(s.low, 1)
                nc.vector.tensor_tensor(thr[:], low[:], kk[:, 0:1], ALU.bitwise_or).then_inc(s.thr, 1)
                dve.wait_ge(s.v, 1)
                for n, shift in enumerate(SHIFTS):
                    dve.wait_ge(s.thr, n + 1)
                    nc.vector.tensor_scalar(hit[:], v[:], thr[:].bitcast(F32), None, ALU.is_ge, ALU.add,
                                            accum_out=cnt[:]).then_inc(s.cnt, 1)
                    dve.wait_ge(s.cnt, n + 1)
                    nc.vector.tensor_scalar(enough[:], cnt[:], float(KEEP), None, ALU.is_ge).then_inc(s.enough, 1)
                    dve.wait_ge(s.low, n + 1)
                    if n + 1 < NF_:
                        nc.vector.tensor_tensor(base[:], low[:], kk[:, n + 1:n + 2], ALU.bitwise_or
                                                ).then_inc(s.base, 1)
                    dve.wait_ge(s.sum, n + 1)
                    nc.vector.tensor_scalar(pick_i[:], psS[:, n:n + 1], -LOWEST[n], float(1 << shift), ALU.add, ALU.mult
                                            ).then_inc(s.pick, 1)
                    dve.wait_ge(s.pick, n + 1)
                    if n + 1 < NF_:
                        dve.wait_ge(s.base, n + 1)
                        nc.vector.tensor_tensor(thr[:], base[:], pick_i[:], ALU.bitwise_or).then_inc(s.thr, 1)
                    nc.vector.tensor_tensor(low[:], low[:], pick_i[:], ALU.bitwise_or).then_inc(s.low, 1)
                dve.wait_ge(s.low, NF_ + 1)
                least = low[:].bitcast(F32)
                nc.vector.tensor_scalar(above[:], v[:], least, None, ALU.is_gt, ALU.add, accum_out=room[:, 0:1]
                                        ).then_inc(s.above, 1)
                nc.vector.tensor_scalar(eqm[:], v[:], least, None, ALU.is_equal).then_inc(s.eqm, 1)
                dve.wait_ge(s.above, 1)
                nc.vector.tensor_scalar(room[:, 1:2], room[:, 0:1], -1.0, float(KEEP), ALU.mult, ALU.add
                                        ).then_inc(s.above, 1)
                dve.wait_ge(s.eqm, 1)
                nc.vector.tensor_tensor_scan(run[:], g.C("one")[:, 0:1].broadcast_to([P, S]), eqm[:], 0.0,
                                             ALU.mult, ALU.add).then_inc(s.run, 1)
                dve.wait_ge(s.run, 1)
                dve.wait_ge(s.above, 2)
                nc.vector.scalar_tensor_tensor(out=run[:], in0=run[:], scalar=room[:, 1:2], in1=eqm[:], op0=ALU.is_le,
                                               op1=ALU.mult).then_inc(s.run, 1)
                dve.wait_ge(s.run, 2)
                nc.vector.tensor_tensor(chosen16[:], run[:], above[:], ALU.add).then_inc(s.chosen, 1)
                nc.vector.tensor_tensor(chosen[:], run[:], above[:], ALU.add).then_inc(s.chosen, 1)
                for b in range(B):
                    for k in range(2):
                        dve.wait_ge(s.mask, 2 * b + k + 1)
                        nc.vector.tensor_tensor(hT[:, b, k], hT[:, b, k], g.ps[4 + 2 * b + k][:], ALU.mult
                                                ).then_inc(s.hm, 1)
                for b in range(B):
                    dve.wait_ge(s.out, b + 1)
                    nc.vector.tensor_tensor(g.xT[:, b], g.xT[:, b], g.ps[b][:], ALU.add)


def attn_stage(nc, a, g):
    ln_block(nc, g)
    with ExitStack() as st:
        def sb(name, shape, dt=F32):
            return g.sb("at_" + name, shape, dt, stack=st)

        SCALE = 1.0 / np.sqrt(np.float32(DH))
        UNITS = H * B
        BODY = 4
        Q32 = 32
        G4, NR = P // Q32, S // Q32
        QT = sb("QT", [P, B, S])
        KT = sb("KT", [P, B, S + 2])
        nrep = sb("nrep", [P, 2, NR, P])
        V = sb("V", [P, B, NR, P])
        vd = sb("vd", [P, 2, NR, G4 * DH])
        kc = sb("kc", [P, BODY, S])
        kl = sb("kl", [P, 2, S])
        prob = sb("prob", [P, 2, 2, S])
        pT = sb("pT", [P, 2, NC, S])
        mx, mb, bias = (sb(n, [P, 2, 2]) for n in ("mx", "mb", "bias"))
        sums, rsum = sb("sums", [P, B * NC * H]), sb("rsum", [P, B * NC * H])
        rexp = sb("rexp", [P, B * NC, H * DH])
        oh = sb("oh", [G4 * DH, B, H, P])
        oT = sb("oT", [P, B, S])
        on, ob = sb("on", [P, B, S]), sb("ob", [P, B, S])
        scr = nc.dram_tensor("scratch_heads", (P, B * S), F32, kind="Internal").ap()
        s = g.sem_set("at", "q k KT nrep v V k1 k2 kc S mx bias exp T vd O oh rsum turned on ob o st ld")
        psS = [g.psum[:, 0:2], g.psum[:, 2:4]]
        psO = g.ps[4:6]
        CUT = H - 2

        def tap(o, t):
            return g.G("conv_w")[:, bass.ds(o * 3 + t, 1)]

        def head(i, k):
            return i * (BODY // B) + (k // B)

        def move_head(eng, o, groups):
            for q in groups:
                eng.dma_start(oT[o * DH:(o + 1) * DH, :, q * P:(q + 1) * P], oh[q * DH:(q + 1) * DH, :, o]
                              ).then_inc(s.ld, 16)

        LAST = UNITS // BODY - 1

        with nc.Block() as block:
            @block.tensor
            def _(pe):
                def scores(n, k, p):
                    for c in range(2):
                        q0 = (2 * p + c) * P
                        nc.tensor.matmul(psS[p][:, c], QT[:, k % B, q0:q0 + P], kc[:, k % BODY], start=True, stop=True
                                         ).then_inc(s.S, 1)

                def body(i, last):
                    for k in range(BODY):
                        n = i * BODY + k
                        if not (last and k == BODY - 1):
                            pe.wait_ge(s.kc, n + 2)
                            for p in range(2):
                                pe.wait_ge(s.exp, n * 4 + (2 * p + 2))
                                scores(n + 1, k + 1, p)
                        pe.wait_ge(s.T, n * 2 + 2)
                        pe.wait_ge(s.vd, n + 1)
                        for r in range(NR):
                            m = nc.tensor.matmul(psO[k % 2][0:G4 * DH, 0:P], vd[:, k % 2, r],
                                                 pT[:, k % 2, :, r * Q32:(r + 1) * Q32], start=(r == 0),
                                                 stop=(r == NR - 1))
                        m.then_inc(s.O, 1)

                def values(b):
                    pe.wait_ge(s.nrep, b + 1)
                    for r in range(NR):
                        n = b * NR + r
                        if n % 4 == 0 and n >= 16:
                            pe.wait_ge(s.V, n // 4 - 3)
                        m = nc.tensor.matmul(g.ps[4 + n // 4 % 4][:, n % 4 * P:(n % 4 + 1) * P], nrep[:, b, r],
                                             g.G("aWv"), start=True, stop=True)
                        if n % 4 == 3:
                            m.then_inc(s.v, 1)

                for b in range(B):
                    nc.tensor.matmul(g.ps[b], g.G("aWk"), g.nT[:, b], start=True, stop=True).then_inc(s.k, 1)
                for b in range(B):
                    nc.tensor.matmul(g.ps[2 + b], g.G("aWq"), g.nT[:, b], start=True, stop=True).then_inc(s.q, 1)
                values(0)
                pe.wait_ge(s.kc, 1)
                for p in range(2):
                    scores(0, 0, p)
                values(1)
                pe.wait_ge(s.V, B * NR // 4)
                with pe.Fori(0, LAST) as i:
                    body(i, False)
                body(LAST, True)

            @block.scalar
            def _(act):
                def taps(i, k):
                    nc.scalar.activation(kc[:, k % BODY], KT[:, k % B, 1:S + 1], ACT.Identity, scale=tap(head(i, k), 1)
                                         ).then_inc(s.k1, 1)
                    nc.scalar.activation(kl[:, k % 2], KT[:, k % B, 2:S + 2], ACT.Identity, scale=tap(head(i, k), 2)
                                         ).then_inc(s.k1, 1)

                def exps(i, k):
                    for p in range(2):
                        act.wait_ge(s.bias, i * (2 * BODY) + (2 * k + p + 1))
                        for c in range(2):
                            col = i * (BODY // B) + ((k % B * NC + 2 * p + c) * H + k // B)
                            nc.scalar.activation(prob[:, p, c], psS[p][:, c], ACT.Exp, bias=bias[:, p, c:c + 1],
                                                 scale=float(SCALE), accum_out=sums[:, bass.ds(col, 1)]
                                                 ).then_inc(s.exp, 1)

                def body(i, last):
                    for k in range(BODY):
                        if not (last and k >= BODY - 2):
                            taps(i, k + 2)
                        if not (last and k == BODY - 1):
                            exps(i, k + 1)
                        act.wait_ge(s.O, i * BODY + (k + 1))
                        nc.scalar.activation(oh[:, k % B, bass.ds(head(i, k), 1)].rearrange("p o q -> p (o q)"),
                                             psO[k % 2][0:G4 * DH, 0:P], ACT.Identity).then_inc(s.oh, 1)

                def values(n):
                    act.wait_ge(s.v, n + 1)
                    if n:
                        act.wait_ge(s.V, n)
                    nc.scalar.activation(V[:, n // 4, n % 4 * 4:n % 4 * 4 + 4].rearrange("p r d -> p (r d)"),
                                         g.ps[4 + n % 4], ACT.Identity).then_inc(s.V, 1)

                nc.scalar.activation(nrep[:, 0].rearrange("p r (g j) -> p r g j", g=G4),
                                     g.nT[:, 0].rearrange("p (r j) -> p r j", j=Q32).unsqueeze(2
                                         ).broadcast_to([P, NR, G4, Q32]), ACT.Identity).then_inc(s.nrep, 1)
                for b in range(B):
                    act.wait_ge(s.q, b + 1)
                    nc.scalar.activation(QT[:, b], g.ps[2 + b], ACT.Identity, bias=g.G("abq"))
                act.wait_ge(s.KT, 2)
                taps(0, 0)
                values(0)
                values(2)
                taps(0, 1)
                values(4)
                values(5)
                exps(0, 0)
                with act.Fori(0, LAST) as i:
                    body(i, False)
                body(LAST, True)

            @block.gpsimd
            def _(pool):
                def sum_taps(i, k):
                    pool.wait_ge(s.k2, i * BODY + (k + 1))
                    pool.wait_ge(s.k1, i * (2 * BODY) + (2 * k + 2))
                    nc.gpsimd.tensor_tensor(kc[:, k % BODY], kc[:, k % BODY], kl[:, k % 2], ALU.add).then_inc(s.kc, 1)

                def diagonal(i, k):
                    nc.gpsimd.tensor_tensor(vd[:, k % 2].rearrange("p r (g d) -> p r g d", g=G4),
                                            V[:, k % B, :, bass.ds(head(i, k) * DH, DH)].unsqueeze(2
                                                ).broadcast_to([P, NR, G4, DH]),
                                            g.C("diag4").rearrange("p (g d) -> p g d", g=G4).unsqueeze(1
                                                ).broadcast_to([P, NR, G4, DH]), ALU.mult).then_inc(s.vd, 1)

                def body(i, last):
                    for k in range(BODY):
                        if not (last and k >= BODY - 2):
                            sum_taps(i, k + 2)
                            pool.wait_ge(s.O, i * BODY + (k + 1))
                            diagonal(i, k + 2)

                for k in range(2):
                    sum_taps(0, k)
                for k in range(2):
                    pool.wait_ge(s.V, (k + 1) * NR // 4)
                    diagonal(0, k)
                with pool.Fori(0, LAST) as i:
                    body(i, False)
                body(LAST, True)

            @block.vector
            def _(dve):
                def first_tap(i, k):
                    dve.wait_ge(s.k1, i * (2 * BODY) + (2 * k + 1))
                    nc.vector.scalar_tensor_tensor(out=kc[:, k % BODY], in0=KT[:, k % B, 0:S], scalar=tap(head(i, k), 0),
                                                   in1=kc[:, k % BODY], op0=ALU.mult, op1=ALU.add).then_inc(s.k2, 1)

                def maxima(i, k, p):
                    cb = g.G("conv_b")[:, bass.ds(head(i, k), 1)]
                    m = i * (2 * BODY) + (2 * k + p + 1)
                    dve.wait_ge(s.S, m * 2)
                    nc.vector.tensor_reduce(mx[:, p], psS[p], AX.X, ALU.max).then_inc(s.mx, 1)
                    dve.wait_ge(s.mx, m * 2 - 1)
                    nc.vector.tensor_scalar(mb[:, p], mx[:, p], float(SCALE), cb, ALU.mult, ALU.add).then_inc(s.mx, 1)
                    dve.wait_ge(s.mx, m * 2)
                    nc.vector.tensor_scalar(bias[:, p], mb[:, p], -1.0, cb, ALU.mult, ALU.add).then_inc(s.bias, 1)

                def turn(i, k, p):
                    dve.wait_ge(s.exp, i * (4 * BODY) + (4 * k + 2 * p + 2))
                    nc.vector.transpose(pT[:, k % 2, 2 * p:2 * p + 2].rearrange("p c k -> p (c k)"),
                                        prob[:, p].rearrange("p c k -> p (c k)")).then_inc(s.T, 1)

                def unit(i, k, taps):
                    maxima(i, k, 0)
                    if taps:
                        first_tap(i, k + 1)
                    maxima(i, k, 1)
                    for p in range(2):
                        turn(i, k, p)

                def body(i, last):
                    for k in range(BODY):
                        if not (last and k == BODY - 1):
                            unit(i, k + 1, not (last and k == BODY - 2))

                def values(n):
                    dve.wait_ge(s.v, n + 1)
                    dve.wait_ge(s.V, n)
                    nc.vector.tensor_copy(V[:, n // 4, n % 4 * 4:n % 4 * 4 + 4].rearrange("p r d -> p (r d)"),
                                          g.ps[4 + n % 4]).then_inc(s.V, 1)

                nc.vector.memset(KT[:, :, 0:1], 0.0)
                nc.vector.memset(KT[:, :, S + 1:S + 2], 0.0)
                for b in range(B):
                    dve.wait_ge(s.k, b + 1)
                    nc.vector.tensor_scalar(KT[:, b, 1:S + 1], g.ps[b], g.G("abk"), None, ALU.add).then_inc(s.KT, 1)
                dve.wait_ge(s.KT, 2)
                dve.wait_ge(s.nrep, 1)
                nc.vector.tensor_copy(nrep[:, 1].rearrange("p r (g j) -> p r g j", g=G4),
                                      g.nT[:, 1].rearrange("p (r j) -> p r j", j=Q32).unsqueeze(2
                                          ).broadcast_to([P, NR, G4, Q32])).then_inc(s.nrep, 1)
                first_tap(0, 0)
                values(1)
                values(3)
                maxima(0, 0, 0)
                first_tap(0, 1)
                maxima(0, 0, 1)
                values(6)
                values(7)
                for p in range(2):
                    turn(0, 0, p)
                with dve.Fori(0, LAST) as i:
                    body(i, False)
                body(LAST, True)

            @block.sync
            def _(sp):
                sp.wait_ge(s.oh, CUT * B)
                for b in range(B):
                    for q in range(G4):
                        to = bass.AP(tensor=scr.tensor, offset=scr.offset + b * S + q * P,
                                     ap=[[B * S, DH], [DH * B * S, CUT], [1, P]])
                        sp.dma_start(to, oh[q * DH:(q + 1) * DH, b, 0:CUT]).then_inc(s.st, 16)
                sp.wait_ge(s.st, 16 * G4 * B)
                sp.dma_start(oT[0:CUT * DH].rearrange("p b q -> p (b q)"), scr[0:CUT * DH]).then_inc(s.ld, 16)
                sp.wait_ge(s.oh, (CUT + 1) * B)
                move_head(sp, CUT, range(G4))

        with nc.Block() as block:
            @block.sync
            def _(sp):
                move_head(sp, H - 1, (0, 1))

            @block.vector
            def _(dve):
                nc.vector.reciprocal(rsum[:], sums[:]).then_inc(s.rsum, 1)
                dve.wait_ge(s.rsum, 1)
                nc.vector.tensor_copy(rexp[:].rearrange("p n (h d) -> p (n h) d", d=DH),
                                      rsum[:].unsqueeze(2).broadcast_to([P, B * NC * H, DH])).then_inc(s.rsum, 1)
                dve.wait_ge(s.ld, 16 * (1 + 2 * G4))
                for b in range(B):
                    dve.wait_ge(s.turned, b + 1)
                    nc.vector.tensor_tensor(on[:, b].rearrange("p (c g j) -> p c g j", g=G4, j=Q32),
                                            oT[:, b].rearrange("p (g c j) -> p c g j", c=NC, j=Q32),
                                            g.ps[b].rearrange("p (c g j) -> p c g j", g=G4, j=Q32), ALU.mult
                                            ).then_inc(s.on, 1)
                for b in range(B):
                    dve.wait_ge(s.o, b + 1)
                    nc.vector.scalar_tensor_tensor(out=g.xT[:, b], in0=g.ps[2 + b], scalar=g.G("abo"), in1=g.xT[:, b],
                                                   op0=ALU.add, op1=ALU.add)

            @block.tensor
            def _(pe):
                pe.wait_ge(s.rsum, 2)
                for b in range(B):
                    for c in range(NC):
                        last = nc.tensor.transpose(g.ps[b][:, c * P:(c + 1) * P], rexp[:, b * NC + c], g.C("ident"))
                    last.then_inc(s.turned, 1)
                for b in range(B):
                    pe.wait_ge(s.ob, b + 1)
                    nc.tensor.matmul(g.ps[2 + b], g.G("aWo"), ob[:, b], start=True, stop=True).then_inc(s.o, 1)

            @block.scalar
            def _(act):
                move_head(act, H - 1, (2, 3))
                for b in range(B):
                    act.wait_ge(s.on, b + 1)
                    nc.scalar.activation(ob[:, b], on[:, b], ACT.Identity, bias=g.G("abv")).then_inc(s.ob, 1)


def xattn_stage(nc, a, g):
    ln_block(nc, g)
    with ExitStack() as st:
        def sb(name, shape, dt=F32):
            return g.sb("xa_" + name, shape, dt, stack=st)

        SCALE = 1.0 / np.sqrt(np.float32(P))
        qT, kT, v = sb("qT", [P, B, S]), sb("kT", [P, B * T]), sb("v", [T, B, P])
        mx, bias = sb("mx", [P, B, NC]), sb("bias", [P, B, NC])
        sums, rsum = sb("sums", [P, B, NC]), sb("rsum", [P, B, NC])
        prob, pn, pT = sb("prob", [P, B, NC, T]), sb("pn", [P, B, NC, T]), sb("pT", [T, B, S])
        s = g.sem_set("xa", "k kT v V q qT S lim bias exp pn T pT o")
        with nc.Block() as block:
            @block.tensor
            def _(pe):
                nc.tensor.matmul(g.ps[2][:, 0:B * T], g.G("xWk"), g.G("ctxT"), start=True, stop=True).then_inc(s.k, 1)
                for b in range(B):
                    nc.tensor.matmul(g.ps[b], g.G("xWq"), g.nT[:, b], start=True, stop=True).then_inc(s.q, 1)
                for b in range(B):
                    last = nc.tensor.matmul(g.ps[3][0:T, b * P:(b + 1) * P], g.G("ctxT")[:, b * T:(b + 1) * T],
                                            g.G("xWv"), start=True, stop=True)
                last.then_inc(s.v, 1)
                pe.wait_ge(s.kT, 1)
                for b in range(B):
                    pe.wait_ge(s.qT, b + 1)
                    for c in range(NC):
                        last = nc.tensor.matmul(g.ps[4 + b][:, c * P:c * P + T], qT[:, b, c * P:(c + 1) * P],
                                                kT[:, b * T:(b + 1) * T], start=True, stop=True)
                    last.then_inc(s.S, 1)
                for b in range(B):
                    pe.wait_ge(s.pn, b + 1)
                    for c in range(NC):
                        last = nc.tensor.transpose(g.ps[6 + b][0:T, c * P:(c + 1) * P], pn[:, b, c], g.C("ident"))
                    last.then_inc(s.T, 1)
                pe.wait_ge(s.V, 1)
                for b in range(B):
                    pe.wait_ge(s.pT, b + 1)
                    nc.tensor.matmul(g.ps[b], v[:, b], pT[:, b], start=True, stop=True).then_inc(s.o, 1)

            @block.scalar
            def _(act):
                for b in range(B):
                    act.wait_ge(s.q, b + 1)
                    nc.scalar.activation(qT[:, b], g.ps[b], ACT.Identity, bias=g.G("xbq")).then_inc(s.qT, 1)
                for b in range(B):
                    act.wait_ge(s.bias, b + 1)
                    for c in range(NC):
                        nc.scalar.activation(prob[:, b, c], g.ps[4 + b][:, c * P:c * P + T], ACT.Exp,
                                             bias=bias[:, b, c:c + 1], scale=float(SCALE),
                                             accum_out=sums[:, b, c:c + 1]).then_inc(s.exp, 1)
                for b in range(B):
                    act.wait_ge(s.T, b + 1)
                    nc.scalar.activation(pT[:, b], g.ps[6 + b][0:T, :], ACT.Identity).then_inc(s.pT, 1)

            @block.vector
            def _(dve):
                dve.wait_ge(s.k, 1)
                nc.vector.tensor_scalar(kT[:], g.ps[2][:, 0:B * T], g.G("xbk"), None, ALU.add).then_inc(s.kT, 1)
                dve.wait_ge(s.v, 1)
                nc.vector.tensor_tensor(v[:], g.ps[3][0:T, 0:B * P].rearrange("p (b d) -> p b d", d=P),
                                        g.G("xbv")[0:T].unsqueeze(1).broadcast_to([T, B, P]), ALU.add).then_inc(s.V, 1)
                for b in range(B):
                    dve.wait_ge(s.S, b + 1)
                    nc.vector.tensor_reduce(mx[:, b], g.ps[4 + b].rearrange("p (c k) -> p c k", k=P)[:, :, 0:T], AX.X,
                                            ALU.max).then_inc(s.lim, 1)
                    dve.wait_ge(s.lim, b + 1)
                    nc.vector.tensor_scalar(bias[:, b], mx[:, b], -float(SCALE), None, ALU.mult).then_inc(s.bias, 1)
                for b in range(B):
                    dve.wait_ge(s.exp, NC * (b + 1))
                    nc.vector.reciprocal(rsum[:, b], sums[:, b]).then_inc(s.lim, 1)
                    dve.wait_ge(s.lim, B + b + 1)
                    nc.vector.tensor_tensor(pn[:, b], prob[:, b], rsum[:, b].unsqueeze(2).broadcast_to([P, NC, T]),
                                            ALU.mult).then_inc(s.pn, 1)
                for b in range(B):
                    dve.wait_ge(s.o, b + 1)
                    nc.vector.tensor_tensor(g.xT[:, b], g.xT[:, b], g.ps[b], ALU.add)


def ffn_stage(nc, a, g):
    with ExitStack() as st:
        def sb(name, shape, dt=F32):
            return g.sb("ff_" + name, shape, dt, stack=st)

        MAGIC = 1.5 * 2.0 ** 23
        TURN1 = 6.28125
        TURN2 = round((2 * np.pi - TURN1) * 2 ** 21) / 2 ** 21
        TURN3 = 2 * np.pi - TURN1 - TURN2
        LIMIT = float(np.nextafter(np.float32(np.pi), np.float32(0)))
        arg, turns, sincos = sb("arg", [P, 2, NF]), sb("turns", [P, 2, NF]), sb("sincos", [P, 2, NF])
        start, coef = sb("start", [P, NF]), sb("coef", [P, NF])
        ang, whole, q, hid = (sb(n, [P, B * NF, S]) for n in ("ang", "whole", "q", "hid"))
        s = g.sem_set("ff", "h ang whole red sin q relu f arg t args start sc coef")

        def reduce_turns(dve, k):
            x, n_ = arg[:, k], turns[:, k]
            nc.vector.tensor_scalar(n_, x, 1.0 / (2 * np.pi), MAGIC, ALU.mult, ALU.add).then_inc(s.t, 1)
            dve.wait_ge(s.t, 5 * k + 1)
            nc.vector.tensor_scalar(n_, n_, MAGIC, None, ALU.subtract).then_inc(s.t, 1)
            dve.wait_ge(s.t, 5 * k + 2)
            for j, part in enumerate((TURN1, TURN2, TURN3)):
                nc.vector.scalar_tensor_tensor(out=x, in0=n_, scalar=-float(part), in1=x, op0=ALU.mult, op1=ALU.add
                                               ).then_inc(s.t, 1)
                dve.wait_ge(s.t, 5 * k + 3 + j)
            nc.vector.tensor_scalar(x, x, LIMIT, -LIMIT, ALU.min, ALU.max).then_inc(s.args, 1)

        def angles(dve):
            nc.vector.tensor_copy(arg[:, 0], g.G("ph")).then_inc(s.arg, 1)
            dve.wait_ge(s.arg, 1)
            reduce_turns(dve, 0)
            dve.wait_ge(s.args, 1)
            nc.vector.tensor_scalar(arg[:, 1], arg[:, 0], np.pi / 2, None, ALU.add).then_inc(s.arg, 1)
            nc.vector.scalar_tensor_tensor(out=start[:], in0=g.G("fb1"), scalar=0.1, in1=arg[:, 0], op0=ALU.mult,
                                           op1=ALU.add).then_inc(s.start, 1)
            dve.wait_ge(s.arg, 2)
            reduce_turns(dve, 1)
            dve.wait_ge(s.start, 1)
            nc.vector.tensor_scalar(start[:], start[:], 1 / (2 * np.pi), None, ALU.mult)

        ln_block(nc, g, angles)
        with nc.Block() as block:
            @block.tensor
            def _(pe):
                for b in range(B):
                    for f in range(NF):
                        nc.tensor.matmul(g.ps[b * NF + f], g.G("fW1")[:, f * P:(f + 1) * P], g.nT[:, b],
                                         start=True, stop=True).then_inc(s.h, 1)
                for b in range(B):
                    for f in range(NF):
                        pe.wait_ge(s.relu, b * NF + f + 1)
                        last = nc.tensor.matmul(g.ps[b * NF], g.G("fW2")[:, f * P:(f + 1) * P], hid[:, b * NF + f],
                                                start=(f == 0), stop=(f == NF - 1))
                    last.then_inc(s.f, 1)

            @block.scalar
            def _(act):
                LEAD = 2

                def angle(k):
                    act.wait_ge(s.h, k + 1)
                    nc.scalar.activation(ang[:, k], g.ps[k], ACT.Identity, bias=start[:, k % NF:k % NF + 1],
                                         scale=0.1 / (2 * np.pi)).then_inc(s.ang, 1)

                def sine(k):
                    act.wait_ge(s.red, k + 1)
                    nc.scalar.activation(ang[:, k], ang[:, k], ACT.Sin, scale=2 * LIMIT).then_inc(s.sin, 1)

                def relu(k):
                    act.wait_ge(s.q, k + 1)
                    nc.scalar.activation(hid[:, k], q[:, k], ACT.Relu, bias=g.G("fb1")[:, k % NF:k % NF + 1]
                                         ).then_inc(s.relu, 1)

                nc.scalar.preload_act_table(ACT.Sin)
                nc.scalar.activation(sincos[:], arg[:], ACT.Sin).then_inc(s.sc, 1)
                for k in range(B * NF + 2 * LEAD):
                    if k < B * NF:
                        angle(k)
                    if LEAD <= k < B * NF + LEAD:
                        sine(k - LEAD)
                    if k >= 2 * LEAD:
                        relu(k - 2 * LEAD)

            @block.vector
            def _(dve):
                dve.wait_ge(s.sc, 1)
                nc.vector.tensor_tensor(sincos[:, 1], sincos[:, 1], g.G("wr"), ALU.mult)
                nc.vector.tensor_tensor(sincos[:, 0], sincos[:, 0], g.G("wi"), ALU.mult).then_inc(s.coef, 1)
                dve.wait_ge(s.coef, 1)
                nc.vector.tensor_tensor(coef[:], sincos[:, 0], sincos[:, 1], ALU.add).then_inc(s.coef, 1)
                dve.wait_ge(s.coef, 2)
                nc.vector.scalar_tensor_tensor(out=coef[:], in0=coef[:], scalar=0.1, in1=g.G("wi"), op0=ALU.mult,
                                               op1=ALU.mult).then_inc(s.coef, 1)
                dve.wait_ge(s.coef, 3)
                LAG_ = 2
                for k in range(B * NF + LAG_):
                    if k < B * NF:
                        dve.wait_ge(s.ang, k + 1)
                        nc.vector.tensor_scalar(whole[:, k], ang[:, k], MAGIC, MAGIC, ALU.add, ALU.subtract
                                                ).then_inc(s.whole, 1)
                    if k >= LAG_:
                        dve.wait_ge(s.sin, k - LAG_ + 1)
                        nc.vector.scalar_tensor_tensor(out=q[:, k - LAG_], in0=ang[:, k - LAG_],
                                                       scalar=coef[:, (k - LAG_) % NF:(k - LAG_) % NF + 1],
                                                       in1=g.ps[k - LAG_], op0=ALU.mult, op1=ALU.add).then_inc(s.q, 1)
                    if k < B * NF:
                        dve.wait_ge(s.whole, k + 1)
                        nc.vector.tensor_tensor(ang[:, k], ang[:, k], whole[:, k], ALU.subtract).then_inc(s.red, 1)
                for b in range(B):
                    dve.wait_ge(s.f, b + 1)
                    nc.vector.scalar_tensor_tensor(out=g.xT[:, b], in0=g.ps[b * NF], scalar=g.G("fb2"), in1=g.xT[:, b],
                                                   op0=ALU.add, op1=ALU.add)


def store_stage(nc, a, g):
    with ExitStack() as st:
        rows = g.sb("out_rows", [P, B * NC, P], stack=st)
        s = g.sem_set("store", "turned rows out")
        with nc.Block() as block:
            @block.tensor
            def _(pe):
                for b in range(B):
                    for c in range(NC):
                        last = nc.tensor.transpose(g.ps[b][:, c * P:(c + 1) * P], g.xT[:, b, c * P:(c + 1) * P],
                                                   g.C("ident"))
                    last.then_inc(s.turned, 1)

            @block.vector
            def _(dve):
                for b in range(B):
                    dve.wait_ge(s.turned, b + 1)
                    nc.vector.tensor_copy(rows[:, b * NC:(b + 1) * NC, :].rearrange("p c d -> p (c d)"), g.ps[b][:]
                                          ).then_inc(s.rows, 1)

            @block.sync
            def _(sp):
                for b in range(B):
                    sp.wait_ge(s.rows, b + 1)
                    sp.dma_start(a["out"][b].rearrange("(c p) d -> p c d", p=P), rows[:, b * NC:(b + 1) * NC, :]
                                 ).then_inc(s.out, 16)
                sp.wait_ge(s.out, 16 * B)


def layout(i):
    f = {k: np.asarray(v) for k, v in i.items()}
    parts = []
    for n in L0_COLS:
        v = {"Wq": "Wq", "Wk": "Wk", "Wv": "Wv", "Wo": "Wo", "Wf1": "Wf1", "Wf2": "Wf2", "s1": "ln1_s", "b1": "ln1_b",
             "s2": "ln2_s", "b2": "ln2_b"}.get(n, n)
        w = f["L0_attn_" + v]
        if n == "Wf2":
            w = w.reshape(LAYERS, NF, P, P).transpose(0, 2, 1, 3).reshape(LAYERS, P, FF)
        elif n == "bf1":
            w = w.reshape(LAYERS, NF, P).transpose(0, 2, 1)
        elif w.ndim == 2:
            w = w[:, :, None]
        parts.append(w)
    l0 = np.ascontiguousarray(np.concatenate(parts, axis=2))
    row = lambda v: np.broadcast_to(v[None, :], (P, v.shape[0]))
    col = lambda v: v.reshape(-1, P).T
    b2 = np.zeros((P, P), f["L0_ffn_b2"].dtype)
    b2[0:64:8] = f["L0_ffn_b2"]
    b2[64:128:8] = f["L0_ffn_b2"]
    cols = {
        "ctxT": f["ctx_1024"].transpose(2, 0, 1).reshape(P, B * T),
        "wg": f["L0_ffn_w_gate_w"], "bg": row(f["L0_ffn_w_gate_b"]),
        "W1": f["L0_ffn_W1"].transpose(1, 0, 2).reshape(P, E * HID),
        "W2": f["L0_ffn_W2"].reshape(2, P, P).transpose(1, 0, 2).reshape(P, 2 * P),
        "b1": col(f["L0_ffn_b1"].reshape(-1)), "b2": b2,
        "aWq": f["L1_attn_Wq"].T, "aWk": f["L1_attn_Wk"].T, "aWv": f["L1_attn_Wv"].T, "aWo": f["L1_attn_Wo"].T,
        "abq": col(f["L1_attn_bq"]), "abk": col(f["L1_attn_bk"]), "abv": col(f["L1_attn_bv"]),
        "abo": col(f["L1_attn_bo"]),
        "conv_w": np.repeat(f["L1_attn_conv_w"].transpose(1, 0, 2).reshape(H, 3 * H), DH, axis=0),
        "conv_b": row(f["L1_attn_conv_b"]),
        "xWq": f["L1_xattn_Wq"].T, "xWk": f["L1_xattn_Wk"].T, "xWv": f["L1_xattn_Wv"].T,
        "xbq": col(f["L1_xattn_bq"]), "xbk": col(f["L1_xattn_bk"]), "xbv": row(f["L1_xattn_bv"]),
        "fW1": f["L1_ffn_W1"], "fW2": f["L1_ffn_W2"].reshape(NF, P, P).transpose(1, 0, 2).reshape(P, FF),
        "fb1": col(f["L1_ffn_b1"]), "ph": col(f["L1_ffn_quantum_phases"]), "wr": col(f["L1_ffn_quantum_weights_real"]),
        "wi": col(f["L1_ffn_quantum_weights_imag"]), "fb2": col(f["L1_ffn_b2"]),
    }
    params = np.ascontiguousarray(np.concatenate([cols[n] for n in G_AT], axis=1))
    assert params.shape == (P, G_N) and l0.shape == (LAYERS, P, L0_N)
    return {"x": f["x"], "ctx": f["ctx_1024"], "l0": l0, "params": params, "consts": constants()}


def kernel(**inputs):
    import concourse.bacc as bacc
    from concourse.bass_utils import run_bass_kernel_spmd

    nc = bacc.Bacc("TRN2", target_bir_lowering=False, num_devices=1)
    arrays = layout(inputs)
    a = {n: nc.dram_tensor("in_" + n, v.shape, mybir.dt.from_np(v.dtype), kind="ExternalInput").ap()
         for n, v in arrays.items()}
    a["out"] = nc.dram_tensor("out", (B, S, P), F32, kind="ExternalOutput").ap()
    build(nc, a)
    r = run_bass_kernel_spmd(nc, [{"in_" + n: v for n, v in arrays.items()}], core_ids=[0])
    return r.results[0]["out"]
```
